# Optimizing a Trainium2 kernel written in Bass

```python
import numpy as np
import jax
import jax.numpy as jnp

def _softmax(x, axis=-1):
    return jax.nn.softmax(x, axis=axis)

def _gelu(x):
    return jax.nn.gelu(x, approximate=True)

def _silu(x):
    return jax.nn.silu(x)

def _sigmoid(x):
    return jax.nn.sigmoid(x)

def _layernorm(x, axis=-1, eps=1e-05):
    m = jnp.mean(x, axis=axis, keepdims=True)
    v = jnp.var(x, axis=axis, keepdims=True)
    return (x - m) / jnp.sqrt(v + eps)

def _scatter_add(tgt, idx, src, axis=0):
    return tgt.at[idx].add(src)

def _segment_sum(src, seg, n):
    return jax.ops.segment_sum(src, seg, n)
kernel_name = 'mk_sandwich_d2_jaxref_r8_1c7667'

def setup_inputs(seed: int=0):
    np.random.seed(seed)
    _w = jnp.asarray

    def _L0_attn_setup():
        import jax, jax.numpy as jnp
        import numpy as np
        B, S, D = (2, 256, 512)
        H = 32
        HD = D // H
        THETA = 10000.0

        def _rope_cos_sin(seq_len, head_dim, theta=THETA):
            inv = 1.0 / theta ** (np.arange(0, head_dim, 2)[:head_dim // 2].astype(np.float32) / head_dim)
            t = np.arange(seq_len)
            f = np.outer(t, inv).astype(np.float32)
            return (jnp.asarray(np.cos(f)), jnp.asarray(np.sin(f)))

        def _apply_rotary(x, cos, sin):
            xr = x.astype(jnp.float32).reshape(*x.shape[:-1], HD // 2, 2)
            x0, x1 = (xr[..., 0], xr[..., 1])
            c = cos[None, :, None, :]
            s = sin[None, :, None, :]
            o0 = x0 * c - x1 * s
            o1 = x0 * s + x1 * c
            return jnp.stack((o0, o1), axis=-1).reshape(*x.shape[:-1], HD)
        key = jax.random.key(seed)
        ks = jax.random.split(key, 5)
        std = 0.02
        return {'x': jax.random.normal(ks[0], (B, S, D), dtype=jnp.float32), 'wq': jax.random.normal(ks[1], (D, D), dtype=jnp.float32) * std, 'wk': jax.random.normal(ks[2], (D, D), dtype=jnp.float32) * std, 'wv': jax.random.normal(ks[3], (D, D), dtype=jnp.float32) * std, 'wo': jax.random.normal(ks[4], (D, D), dtype=jnp.float32) * std}
    _L0_attn_in = _L0_attn_setup()

    def _L0_ffn_setup():
        import jax, jax.numpy as jnp
        import numpy as np
        IN_F = 512
        OUT_F = 512
        N_CLUSTERS = 64
        THRESHOLD = 0.01
        TEMPERATURE = 0.1
        BATCH, SEQ = (4, 256)
        key = jax.random.key(seed)
        k1, k2, k3, k4, k5 = jax.random.split(key, 5)
        s = 1.0 / np.sqrt(IN_F)
        return {'input': jax.random.normal(k1, (BATCH, SEQ, IN_F), dtype=jnp.float32), 'weight': jax.random.normal(k2, (OUT_F, IN_F), dtype=jnp.float32) * s, 'bias': jax.random.uniform(k3, (OUT_F,), dtype=jnp.float32, minval=-s, maxval=s), 'centroids': jax.random.normal(k4, (N_CLUSTERS, IN_F), dtype=jnp.float32) * s, 'assignments': jax.random.randint(k5, (OUT_F,), 0, N_CLUSTERS, dtype=jnp.int32)}
    _L0_ffn_in = _L0_ffn_setup()

    def _L1_attn_setup():
        import jax, jax.numpy as jnp
        import numpy as np
        from jax import lax
        H = 512
        DIN = 1024
        N = 16
        K = 4
        R = 32
        B_SZ = 2
        L = 256
        EPS = 1e-06

        def rmsnorm(x, w):
            return x * lax.rsqrt(jnp.mean(x * x, axis=-1, keepdims=True) + EPS) * w

        def _selective_scan(x, dt, A, Bm, Cm):
            xT = jnp.transpose(x, (2, 0, 1))
            dtT = jnp.transpose(dt, (2, 0, 1))
            BT = jnp.transpose(Bm, (2, 0, 1))
            CT = jnp.transpose(Cm, (2, 0, 1))

            def step(h, inp):
                x_t, dt_t, B_t, C_t = inp
                dA = jnp.exp(dt_t[..., None] * A)
                dBx = dt_t[..., None] * B_t[:, None, :] * x_t[..., None]
                h = dA * h + dBx
                y = jnp.einsum('bdn,bn->bd', h, C_t)
                return (h, y)
            h0 = jnp.zeros((x.shape[0], x.shape[1], A.shape[1]), dtype=x.dtype)
            _, ys = lax.scan(step, h0, (xT, dtT, BT, CT))
            return jnp.transpose(ys, (1, 2, 0))
        key = jax.random.key(seed)
        ks = jax.random.split(key, 8)
        hidden_states = jax.random.normal(ks[0], (B_SZ, L, H), dtype=jnp.float32)
        s = 0.02
        in_proj_w = jax.random.normal(ks[1], (H, 2 * DIN), dtype=jnp.float32) * s
        conv_w = jax.random.normal(ks[2], (DIN, K), dtype=jnp.float32) * 0.2
        conv_b = jax.random.normal(ks[3], (DIN,), dtype=jnp.float32) * 0.02
        x_proj_w = jax.random.normal(ks[4], (R + 2 * N, DIN), dtype=jnp.float32) * s
        dt_proj_w = jax.random.normal(ks[5], (DIN, R), dtype=jnp.float32) * s
        dt_bias = jax.random.normal(ks[6], (DIN,), dtype=jnp.float32) * 0.5 - 4.0
        A_log = jnp.log(jnp.broadcast_to(jnp.arange(1, N + 1, dtype=jnp.float32)[None, :], (DIN, N)))
        D_param = jnp.ones((DIN,), dtype=jnp.float32)
        out_proj_w = jax.random.normal(ks[7], (H, DIN), dtype=jnp.float32) * s
        dt_ln_w = jnp.ones((R,), dtype=jnp.float32)
        B_ln_w = jnp.ones((N,), dtype=jnp.float32)
        C_ln_w = jnp.ones((N,), dtype=jnp.float32)
        return dict(hidden_states=hidden_states, in_proj_w=in_proj_w, conv_w=conv_w, conv_b=conv_b, x_proj_w=x_proj_w, dt_proj_w=dt_proj_w, dt_bias=dt_bias, A_log=A_log, D_param=D_param, out_proj_w=out_proj_w, dt_ln_w=dt_ln_w, B_ln_w=B_ln_w, C_ln_w=C_ln_w)
    _L1_attn_in = _L1_attn_setup()

    def _L1_ffn_setup():
        import jax, jax.numpy as jnp
        import numpy as np
        B, S, D_IN, D_OUT = (2, 256, 512, 512)
        E, K, R = (8, 2, 16)
        SCALING = 32.0 / 16.0
        key = jax.random.key(seed)
        ks = jax.random.split(key, 6)
        x = jax.random.normal(ks[0], (B, S, D_IN), dtype=jnp.float32)
        gate_w = jax.random.normal(ks[1], (E, D_IN), dtype=jnp.float32) * 0.02
        base_w = jax.random.normal(ks[2], (D_OUT, D_IN), dtype=jnp.float32) * 0.02
        base_b = jax.random.normal(ks[3], (D_OUT,), dtype=jnp.float32) * 0.02
        lora_A = jax.random.normal(ks[4], (E, R, D_IN), dtype=jnp.float32) * 0.02
        lora_B = jax.random.normal(ks[5], (E, D_OUT, R), dtype=jnp.float32) * 0.02
        return {'x': x, 'gate_w': gate_w, 'base_w': base_w, 'base_b': base_b, 'lora_A': lora_A, 'lora_B': lora_B}
    _L1_ffn_in = _L1_ffn_setup()
    _d = {'L0_attn_x': _L0_attn_in['x'], 'L0_attn_wq': _L0_attn_in['wq'], 'L0_attn_wk': _L0_attn_in['wk'], 'L0_attn_wv': _L0_attn_in['wv'], 'L0_attn_wo': _L0_attn_in['wo'], 'L0_ffn_weight': _L0_ffn_in['weight'], 'L0_ffn_bias': _L0_ffn_in['bias'], 'L0_ffn_centroids': _L0_ffn_in['centroids'], 'L0_ffn_assignments': _L0_ffn_in['assignments'], 'L1_attn_in_proj_w': _L1_attn_in['in_proj_w'], 'L1_attn_conv_w': _L1_attn_in['conv_w'], 'L1_attn_conv_b': _L1_attn_in['conv_b'], 'L1_attn_x_proj_w': _L1_attn_in['x_proj_w'], 'L1_attn_dt_proj_w': _L1_attn_in['dt_proj_w'], 'L1_attn_dt_bias': _L1_attn_in['dt_bias'], 'L1_attn_A_log': _L1_attn_in['A_log'], 'L1_attn_D_param': _L1_attn_in['D_param'], 'L1_attn_out_proj_w': _L1_attn_in['out_proj_w'], 'L1_attn_dt_ln_w': _L1_attn_in['dt_ln_w'], 'L1_attn_B_ln_w': _L1_attn_in['B_ln_w'], 'L1_attn_C_ln_w': _L1_attn_in['C_ln_w'], 'L1_ffn_gate_w': _L1_ffn_in['gate_w'], 'L1_ffn_base_w': _L1_ffn_in['base_w'], 'L1_ffn_base_b': _L1_ffn_in['base_b'], 'L1_ffn_lora_A': _L1_ffn_in['lora_A'], 'L1_ffn_lora_B': _L1_ffn_in['lora_B']}
    _x0 = _d['L0_attn_x']
    _d['L0_attn_x'] = jax.random.normal(jax.random.fold_in(jax.random.key(seed), 1), (2, 1024, 512), dtype=_x0.dtype)
    del _x0
    return _d

def reference(L0_attn_x, L0_attn_wq, L0_attn_wk, L0_attn_wv, L0_attn_wo, L0_ffn_weight, L0_ffn_bias, L0_ffn_centroids, L0_ffn_assignments, L1_attn_in_proj_w, L1_attn_conv_w, L1_attn_conv_b, L1_attn_x_proj_w, L1_attn_dt_proj_w, L1_attn_dt_bias, L1_attn_A_log, L1_attn_D_param, L1_attn_out_proj_w, L1_attn_dt_ln_w, L1_attn_B_ln_w, L1_attn_C_ln_w, L1_ffn_gate_w, L1_ffn_base_w, L1_ffn_base_b, L1_ffn_lora_A, L1_ffn_lora_B):

    def _L0_attn_ref(x, wq, wk, wv, wo):
        import jax, jax.numpy as jnp
        import numpy as np
        B, S, D = (2, 256, 512)
        H = 32
        HD = D // H
        THETA = 10000.0

        def _rope_cos_sin(seq_len, head_dim, theta=THETA):
            inv = 1.0 / theta ** (np.arange(0, head_dim, 2)[:head_dim // 2].astype(np.float32) / head_dim)
            t = np.arange(seq_len)
            f = np.outer(t, inv).astype(np.float32)
            return (jnp.asarray(np.cos(f)), jnp.asarray(np.sin(f)))

        def _apply_rotary(x, cos, sin):
            xr = x.astype(jnp.float32).reshape(*x.shape[:-1], HD // 2, 2)
            x0, x1 = (xr[..., 0], xr[..., 1])
            c = cos[None, :, None, :]
            s = sin[None, :, None, :]
            o0 = x0 * c - x1 * s
            o1 = x0 * s + x1 * c
            return jnp.stack((o0, o1), axis=-1).reshape(*x.shape[:-1], HD)
        b, s, d = x.shape
        q = (x @ wq).reshape(b, s, H, HD)
        k = (x @ wk).reshape(b, s, H, HD)
        v = (x @ wv).reshape(b, s, H, HD)
        cos, sin = _rope_cos_sin(s, HD)
        q = _apply_rotary(q, cos, sin)
        k = _apply_rotary(k, cos, sin)
        scale = 1.0 / jnp.sqrt(jnp.float32(HD))
        scores = jnp.einsum('bqhd,bkhd->bhqk', q, k) * scale
        causal = jnp.tril(jnp.ones((s, s), dtype=bool))
        scores = jnp.where(causal[None, None], scores, jnp.finfo(scores.dtype).min)
        probs = jax.nn.softmax(scores, axis=-1)
        out = jnp.einsum('bhqk,bkhd->bqhd', probs, v).reshape(b, s, d)
        return out @ wo

    def _L0_ffn_ref(input, weight, bias, centroids, assignments):
        import jax, jax.numpy as jnp
        import numpy as np
        IN_F = 512
        OUT_F = 512
        N_CLUSTERS = 64
        THRESHOLD = 0.01
        TEMPERATURE = 0.1
        BATCH, SEQ = (4, 256)
        shape = input.shape
        x = input.reshape(-1, shape[-1])
        dots = jax.nn.softmax(x @ centroids.T / TEMPERATURE, axis=-1)
        hits = dots > THRESHOLD
        query_sel = jnp.any(hits, axis=1)
        cluster_sel = jnp.any(hits, axis=0)
        row_sel = cluster_sel[assignments]
        dense = x @ weight.T + bias
        out = jnp.where(query_sel[:, None] & row_sel[None, :], dense, jnp.zeros((), dense.dtype))
        return out.reshape(*shape[:-1], -1)

    def _L1_attn_ref(hidden_states, in_proj_w, conv_w, conv_b, x_proj_w, dt_proj_w, dt_bias, A_log, D_param, out_proj_w, dt_ln_w, B_ln_w, C_ln_w):
        import jax, jax.numpy as jnp
        import numpy as np
        from jax import lax
        H = 512
        DIN = 1024
        N = 16
        K = 4
        R = 32
        B_SZ = 2
        L = 256
        EPS = 1e-06

        def rmsnorm(x, w):
            return x * lax.rsqrt(jnp.mean(x * x, axis=-1, keepdims=True) + EPS) * w

        def _selective_scan(x, dt, A, Bm, Cm):
            xT = jnp.transpose(x, (2, 0, 1))
            dtT = jnp.transpose(dt, (2, 0, 1))
            BT = jnp.transpose(Bm, (2, 0, 1))
            CT = jnp.transpose(Cm, (2, 0, 1))

            def step(h, inp):
                x_t, dt_t, B_t, C_t = inp
                dA = jnp.exp(dt_t[..., None] * A)
                dBx = dt_t[..., None] * B_t[:, None, :] * x_t[..., None]
                h = dA * h + dBx
                y = jnp.einsum('bdn,bn->bd', h, C_t)
                return (h, y)
            h0 = jnp.zeros((x.shape[0], x.shape[1], A.shape[1]), dtype=x.dtype)
            _, ys = lax.scan(step, h0, (xT, dtT, BT, CT))
            return jnp.transpose(ys, (1, 2, 0))
        proj = hidden_states @ in_proj_w
        x, z = jnp.split(proj, 2, axis=-1)
        x = jnp.transpose(x, (0, 2, 1))
        z = jnp.transpose(z, (0, 2, 1))
        Lq = x.shape[-1]
        xp = jnp.pad(x, ((0, 0), (0, 0), (K - 1, 0)))
        xc = conv_b[None, :, None]
        for k in range(K):
            xc = xc + conv_w[None, :, k:k + 1] * xp[:, :, k:k + Lq]
        xc = jax.nn.silu(xc)
        ssm_p = jnp.einsum('bdl,ed->ble', xc, x_proj_w)
        dt_r = rmsnorm(ssm_p[..., :R], dt_ln_w)
        Bm = rmsnorm(ssm_p[..., R:R + N], B_ln_w)
        Cm = rmsnorm(ssm_p[..., R + N:], C_ln_w)
        dt = jnp.einsum('blr,dr->bdl', dt_r, dt_proj_w)
        dt = jax.nn.softplus(dt + dt_bias[None, :, None])
        A = -jnp.exp(A_log)
        Bm = jnp.transpose(Bm, (0, 2, 1))
        Cm = jnp.transpose(Cm, (0, 2, 1))
        ys = _selective_scan(xc, dt, A, Bm, Cm)
        y = (ys + D_param[None, :, None] * xc) * jax.nn.silu(z)
        return jnp.einsum('bdl,hd->blh', y, out_proj_w)

    def _L1_ffn_ref(x, gate_w, base_w, base_b, lora_A, lora_B):
        import jax, jax.numpy as jnp
        import numpy as np
        B, S, D_IN, D_OUT = (2, 256, 512, 512)
        E, K, R = (8, 2, 16)
        SCALING = 32.0 / 16.0
        gate_logits = jnp.einsum('bsd,ed->bse', x, gate_w)
        weights, selected = jax.lax.top_k(gate_logits, K)
        weights = jax.nn.softmax(weights.astype(jnp.float32), axis=2).astype(x.dtype)
        result = jnp.einsum('bsd,od->bso', x, base_w) + base_b
        w_full = jnp.sum(jax.nn.one_hot(selected, E, dtype=x.dtype) * weights[..., None], axis=2)
        low = jnp.einsum('bsd,erd->ebsr', x, lora_A)
        lora_out = jnp.einsum('ebsr,eor,bse->bso', low, lora_B, w_full)
        result = result + SCALING * lora_out
        return result
    x = L0_attn_x
    x = x + _layernorm(_L0_attn_ref(_layernorm(x, axis=-1), L0_attn_wq, L0_attn_wk, L0_attn_wv, L0_attn_wo), axis=-1)
    x = x + _layernorm(_L0_ffn_ref(_layernorm(x, axis=-1), L0_ffn_weight, L0_ffn_bias, L0_ffn_centroids, L0_ffn_assignments), axis=-1)
    x = x + _layernorm(_L1_attn_ref(_layernorm(x, axis=-1), L1_attn_in_proj_w, L1_attn_conv_w, L1_attn_conv_b, L1_attn_x_proj_w, L1_attn_dt_proj_w, L1_attn_dt_bias, L1_attn_A_log, L1_attn_D_param, L1_attn_out_proj_w, L1_attn_dt_ln_w, L1_attn_B_ln_w, L1_attn_C_ln_w), axis=-1)
    x = x + _layernorm(_L1_ffn_ref(_layernorm(x, axis=-1), L1_ffn_gate_w, L1_ffn_base_w, L1_ffn_base_b, L1_ffn_lora_A, L1_ffn_lora_B), axis=-1)
    return x

_drawn_inputs = setup_inputs


def setup_inputs(seed=0):
    import zlib

    import numpy as np

    out = dict(_drawn_inputs(seed))
    spreads = {'L1_attn_D_param': (1.0, 0.2),
     'L1_attn_dt_ln_w': (1.0, 0.6),
     'L1_attn_B_ln_w': (1.0, 0.2),
     'L1_attn_C_ln_w': (1.0, 0.547)}
    factors = {'L0_ffn_bias': 2.945, 'L1_attn_dt_proj_w': 4.483, 'L1_ffn_base_b': 2.984}
    for name, (base, spread) in spreads.items():
        noise = np.random.default_rng([zlib.crc32(name.encode()), seed]).standard_normal(out[name].shape)
        drawn = base * np.exp(spread * noise) if base else spread * noise
        out[name] = jnp.asarray(drawn.astype(out[name].dtype))
    for name, factor in factors.items():
        out[name] = (out[name] * factor).astype(out[name].dtype)
    return out
```

```python
from collections import namedtuple
from contextlib import ExitStack

import concourse.bass as bass
from concourse import mybir

ALU = mybir.AluOpType
ACT = mybir.ActivationFunctionType
AX = mybir.AxisListType
F32 = mybir.dt.float32
BF16 = mybir.dt.bfloat16
I32 = mybir.dt.int32
ds = bass.ds

P = 128
D = 512
KC = D // P
B = 2
S = 1024
ST = S // P
BLK = 512
NB = B * S // BLK
TB = BLK // P
H = 32
HD = D // H
HH = H // 2
HC = HH * HD
QH = 4
NQ = HH // QH
GH = P // HD
NSPLIT = 6
OUTS = QH + 1
QK = NSPLIT * HD
Q_PARTS = (0, 0, 0, 1, 1, 2)
K_PARTS = (0, 1, 2, 0, 1, 0)
VW = 32
LN_EPS = 1e-5


def semaphores(nc, ctx, stage, names):
    return namedtuple(stage, names)(*(ctx.enter_context(nc.semaphore(f"{stage}_{name}")) for name in names.split()))


def clear(nc, sems):
    with nc.Block() as block:
        @block.sync
        def _(sp):
            for s in sems:
                sp.sem_clear(s)


def max_units():
    return [(h, i, p) for i in range(ST) for h in range(QH) for p in range(1 + (i >= 4))]


MAX_UNITS = max_units()
MAX_AT = (11, 9, 8, 7, 6, 5, 2, 0)
NMAX = len(MAX_UNITS) + 1
NPROJ = 2 * 2 * 2 + ST
RD = NPROJ
RDQ = QH * ST + 2
O_AT = 5


def rd_exp(q, j, h):
    return RD + q * RDQ + QH * j + h + 1 + (1 if j > O_AT else 0)


def attention_stage(nc, ctx, ps, x, w_qkv, rope, ident, masks, att_o, att_l):
    with ExitStack() as mem:
        def sb(name, shape, dt=F32):
            return mem.enter_context(nc.sbuf_tensor(name, shape, dt))

        ident_f = sb("ident_f", [P, P])
        ident_b = sb("ident_b", [P, P], BF16)
        mask_f = sb("mask_f", [P, 2, P])
        mask_b = sb("mask_b", [P, 2, P], BF16)
        cos_sin = sb("cos_sin", [P, 2, S])
        xnT = sb("xnT", [P, KC, S])
        w3 = sb("w3", [P, 3, KC, HC])
        q6 = sb("q6", [QK + 3, HH, S], BF16)
        k6 = sb("k6", [QK + 3, HH, S], BF16)
        vh = sb("vh", [P, ST, HH, VW])
        va = sb("va", [P, ST, QH * VW])
        probs = sb("probs", [P, 2, QH, S])
        o_sb = sb("o_sb", [P, S])
        q_raw = sb("q_raw", [P, 2, BLK])
        q_swap = sb("q_swap", [P, 2, BLK])
        t_cos = sb("t_cos", [P, 2, BLK])
        t_sin = sb("t_sin", [P, 2, BLK])
        q_rot = sb("q_rot", [P, 2, BLK])
        q_rest = sb("q_rest", [P, 2, BLK])
        parts = sb("parts", [P, 2, 3, BLK], BF16)
        mx = sb("mx", [P, 2, QH, ST])
        nm = sb("nm", [P, QH, ST])
        m_rest = sb("m_rest", [QH * ST, P])
        m_parts = sb("m_parts", [QH * ST, NQ, 3, P], BF16)
        st6 = sb("st6", [P, ST, 6])
        mv = sb("mv", [P, ST, 2])
        lnv = sb("lnv", [P, ST])
        rstd = sb("rstd", [P, ST])
        xt = probs[:, 0, :, :].rearrange("p a (t d) -> p (a t) d", d=D)

        o_ps = ps[:, 0:2, :].rearrange("p a n -> p (a n)")
        st_ps = [ps[:, 2 + 2 * i:4 + 2 * i, :].rearrange("p a n -> p (a n)") for i in range(2)]
        mx_ps = [ps[:, 6 + i, :] for i in range(2)]

        scratch = nc.dram_tensor("split_parts", (2, 3, GH, HD, S), BF16, kind="Internal").ap()
        c = semaphores(nc, ctx, "ac", "const cast")
        with nc.Block() as block:
            @block.sync
            def _(sp):
                sp.dma_start(ident_f[:], ident).then_inc(c.const, 16)
                sp.dma_start(mask_f[:], masks).then_inc(c.const, 16)
                sp.dma_start(cos_sin[:], rope).then_inc(c.const, 16)
                sp.wait_ge(c.const, 48)

            @block.vector
            def _(dve):
                dve.wait_ge(c.const, 48)
                dve.tensor_copy(ident_b[:], ident_f[:])
                dve.tensor_copy(mask_b[:], mask_f[:])
                dve.memset(k6[QK:QK + 3, :, :], 1.0)

            @block.gpsimd
            def _(pool):
                pool.memset(vh[:, :, :, HD:VW], 1.0)

            @block.scalar
            def _(act):
                act.preload_act_table_set("natural_log_exp_and_others")

        n = semaphores(nc, ctx, "an", "x0 x1 stats aggr lnv rstd xn tr ev")
        a = semaphores(nc, ctx, "aa", "w proj act_rd swap sin rot hi rest mid lo rep0 rep1 kept0 kept1 scores "
                 "max max_rd m_ready m_in m_chain m_split va pv out")
        with nc.Fori(0, B) as b:
            with nc.Block() as block:
                @block.sync
                def _(sp):
                    for g, s in enumerate((n.x0, n.x1)):
                        sp.dma_start(xt[:, TB * g:TB * g + TB, :],
                                     x[ds(b * 2 + g, 1), :, :].rearrange("a (t p) d -> p (a t) d", p=P)).then_inc(s, 16)

                @block.vector
                def _(dve):
                    for t in range(ST):
                        if t % TB == 0:
                            dve.wait_ge((n.x0, n.x1)[t // TB], 16)
                        dve.bn_stats(st6[:, t, :], xt[:, t, :]).then_inc(n.stats, 1)
                    for t in range(ST):
                        dve.wait_ge(n.stats, t + 1)
                        dve.bn_aggr(mv[:, t, :], st6[:, t, :]).then_inc(n.aggr, 1)
                    dve.wait_ge(n.rstd, 1)
                    for t in range(ST):
                        dve.tensor_scalar(xt[:, t, :], xt[:, t, :], mv[:, t, 0:1], rstd[:, t:t + 1],
                                          ALU.subtract, ALU.mult).then_inc(n.xn, 1)

                @block.scalar
                def _(act):
                    act.wait_ge(n.aggr, ST)
                    act.activation(lnv[:], mv[:, :, 1], ACT.Ln, bias=LN_EPS).then_inc(n.lnv, 1)
                    act.wait_ge(n.lnv, 1)
                    act.activation(rstd[:], lnv[:], ACT.Exp, scale=-0.5).then_inc(n.rstd, 1)
                    for t in range(ST):
                        act.wait_ge(n.tr, t + 1)
                        act.activation(xnT[:, :, t * P:t * P + P],
                                       ps[:, t % 4, :].rearrange("p (c n) -> p c n", c=KC), ACT.Copy).then_inc(n.ev, 1)

                @block.tensor
                def _(pe):
                    for t in range(ST):
                        pe.wait_ge(n.xn, t + 1)
                        if t >= 4:
                            pe.wait_ge(n.ev, t - 3)
                        for k in range(KC):
                            mm = pe.transpose(ps[:, t % 4, k * P:k * P + P], xt[:, t, k * P:k * P + P], ident_f[:])
                        mm.then_inc(n.tr, 1)

            with nc.Fori(0, 2) as hf:
                units = [(w, g, tb) for g in range(2) for w in (1, 0) for tb in range(2)]
                NU = len(units)
                rep, kept = (a.rep0, a.rep1), (a.kept0, a.kept1)

                with nc.Block() as block:
                    @block.sync
                    def _(sp):
                        sp.dma_start(w3[:], w_qkv[ds(hf, 1), :, :, :, :].rearrange("a p w c n -> (a p) w c n")).then_inc(a.w, 16)
                        for u, (w, g, tb) in enumerate(units):
                            pair = u // 2
                            sp.wait_ge(a.lo, u + 1)
                            if pair >= 2:
                                sp.wait_ge(rep[pair % 2], 16 * NSPLIT * (pair // 2))
                            sp.dma_start(scratch[pair % 2, :, :, :, tb * BLK:tb * BLK + BLK].rearrange("s h r t -> (h r) s t"),
                                         parts[:, tb, :, :]).then_inc(kept[tb], 16)
                            if tb == 0:
                                continue
                            for s in kept:
                                sp.wait_ge(s, 16 * (pair + 1))
                            for r, part in enumerate((Q_PARTS, K_PARTS)[w]):
                                sp.dma_start((q6, k6)[w][r * HD:r * HD + HD, g * GH:g * GH + GH, :],
                                             scratch[pair % 2, part].rearrange("h r t -> r h t")).then_inc(rep[pair % 2], 16)

                        def send_max(q):
                            sp.wait_ge(a.m_split, q + 1)
                            for r in range(3):
                                sp.dma_start(q6[QK + r:QK + r + 1, ds(q * QH, QH), :].rearrange("o h (i n) -> o (h i) n", n=P),
                                             m_parts[:, ds(q, 1), r, :]).then_inc(a.m_in, 16)

                        def send_out(q):
                            sp.wait_ge(a.act_rd, RD + RDQ * (q + 1))
                            for h in range(QH):
                                sp.dma_start(att_o[ds(hf * HH + q * QH + h, 1), :, ds(b * S, S)].rearrange("a r t -> (a r) t"),
                                             o_sb[VW * h:VW * h + HD, :]).then_inc(a.out, 16)
                            sp.dma_start(att_l[ds(hf * HH + q * QH, QH), ds(b * S, S)],
                                         o_sb[HD:P:VW, :]).then_inc(a.out, 16)

                        send_max(0)
                        with sp.Fori(0, NQ - 1) as q:
                            send_max(q + 1)
                            send_out(q)
                        send_out(NQ - 1)
                        sp.wait_ge(a.out, 16 * OUTS * NQ)

                    @block.tensor
                    def _(pe):
                        pe.wait_ge(a.w, 16)
                        for u, (w, g, tb) in enumerate(units):
                            if u >= 4:
                                pe.wait_ge(a.act_rd, u - 3)
                            for k in range(KC):
                                mm = pe.matmul(ps[:, 2 + u % 4, :], w3[:, w, k, g * P:g * P + P],
                                               xnT[:, k, tb * BLK:tb * BLK + BLK], start=(k == 0), stop=(k == KC - 1))
                            mm.then_inc(a.proj, 1)
                        for t in range(ST):
                            u = NU + t
                            pe.wait_ge(a.act_rd, u - 3)
                            for k in range(KC):
                                mm = pe.matmul(ps[:, 2 + u % 4, 0:HC], xnT[:, k, t * P:t * P + P], w3[:, 2, k, :],
                                               start=(k == 0), stop=(k == KC - 1))
                            mm.then_inc(a.proj, 1)

                        def max_unit(q, n):
                            h, i, p = MAX_UNITS[n]
                            lo, hi = 512 * p, min(512 * p + 512, (i + 1) * P)
                            if n >= 2:
                                pe.wait_ge(a.max_rd, q * NMAX + n - 1)
                            else:
                                pe.wait_ge(a.max_rd, q * NMAX)
                            diag = hi == (i + 1) * P
                            mm = pe.matmul(mx_ps[n % 2][:, 0:hi - lo], q6[0:QK, ds(q * QH + h, 1), i * P:i * P + P],
                                           k6[0:QK, ds(q * QH + h, 1), lo:hi], start=True, stop=not diag)
                            if diag:
                                mm = pe.matmul(mx_ps[n % 2][:, i * P - lo:hi - lo], ident_b[:], mask_b[:, 0, :],
                                               start=False, stop=True)
                            mm.then_inc(a.max, 1)

                        def max_turn(q):
                            pe.wait_ge(a.m_ready, q + 1)
                            pe.wait_ge(a.max_rd, q * NMAX + NMAX - 2)
                            pe.transpose(mx_ps[0][0:QH * ST, 0:P], nm[:].rearrange("p h i -> p (h i)"),
                                         ident_f[:]).then_inc(a.max, 1)

                        def scores(q, j, h):
                            slot = st_ps[(QH * j + h) % 2]
                            n = QH * j + h
                            if n >= 2:
                                pe.wait_ge(a.act_rd, rd_exp(q, (n - 2) // QH, (n - 2) % QH))
                            elif n == 0:
                                pe.wait_ge(a.act_rd, RD + q * RDQ)
                            for lo, hi in ((j * P, 512), (512, S)) if j < 4 else ((j * P, S),):
                                diag = lo == j * P
                                mm = pe.matmul(slot[:, lo:hi], k6[:, ds(q * QH + h, 1), j * P:j * P + P],
                                               q6[:, ds(q * QH + h, 1), lo:hi], start=True, stop=not diag)
                                if diag:
                                    mm = pe.matmul(slot[:, lo:lo + P], ident_b[:], mask_b[:, 1, :], start=False, stop=True)
                            mm.then_inc(a.scores, 1)

                        def weigh(q, j):
                            pe.wait_ge(a.act_rd, rd_exp(q, j, QH - 1))
                            if j == 0:
                                pe.wait_ge(a.va, q + 1)
                            for half, last in ((0, 3), (1, 7)):
                                lo, hi = max(512 * half, j * P), 512 * half + 512
                                if lo >= hi:
                                    continue
                                for h in range(QH):
                                    mm = pe.matmul(o_ps[VW * h:VW * h + VW, lo:hi], va[:, j, VW * h:VW * h + VW],
                                                   probs[:, j % 2, h, lo:hi], start=(j == 0), stop=(j == last))
                            mm.then_inc(a.pv, 1)

                        def quad(q, ahead):
                            n = 0
                            pe.wait_ge(a.m_in, 48 * (q + 1))
                            for j in range(ST):
                                until = n + MAX_AT[j]
                                for h in range(QH):
                                    scores(q, j, h)
                                    if h == 1 and j:
                                        weigh(q, j - 1)
                                    while ahead and n < until - (MAX_AT[j] * (QH - 1 - h)) // QH:
                                        max_unit(q + 1, n)
                                        n += 1
                                if j == 6 and ahead:
                                    max_turn(q + 1)
                            weigh(q, ST - 1)

                        for s in rep:
                            pe.wait_ge(s, 16 * NSPLIT * NU // 4)
                        pe.wait_ge(a.act_rd, RD)
                        for n in range(NMAX - 1):
                            h, i, p = MAX_UNITS[n]
                            lo, hi = 512 * p, min(512 * p + 512, (i + 1) * P)
                            if n >= 2:
                                pe.wait_ge(a.max_rd, n - 1)
                            diag = hi == (i + 1) * P
                            mm = pe.matmul(mx_ps[n % 2][:, 0:hi - lo], q6[0:QK, h, i * P:i * P + P], k6[0:QK, h, lo:hi],
                                           start=True, stop=not diag)
                            if diag:
                                mm = pe.matmul(mx_ps[n % 2][:, i * P - lo:hi - lo], ident_b[:], mask_b[:, 0, :],
                                               start=False, stop=True)
                            mm.then_inc(a.max, 1)
                        max_turn(0)
                        with pe.Fori(0, NQ - 1) as q:
                            quad(q, True)
                        quad(NQ - 1, False)

                    @block.scalar
                    def _(act):
                        def take(u):
                            act.wait_ge(a.proj, u + 1)
                            if u < NU:
                                if u >= 2:
                                    act.wait_ge(a.swap, u - 1)
                                act.activation(q_raw[:, u % 2, :], ps[:, 2 + u % 4, :], ACT.Copy,
                                               scale=HD ** -0.5 if units[u][0] == 0 else 1.0).then_inc(a.act_rd, 1)
                            else:
                                act.activation(vh[:, u - NU, :, 0:HD],
                                               ps[:, 2 + u % 4, 0:HC].rearrange("p (h d) -> p h d", d=HD),
                                               ACT.Copy).then_inc(a.act_rd, 1)

                        take(0)
                        for u in range(NU):
                            take(u + 1)
                            act.wait_ge(a.rot, u + 1)
                            if u >= 2:
                                act.wait_ge(kept[u % 2], 16 * (u // 2))
                            act.activation(parts[:, u % 2, 0, :], q_rot[:, u % 2, :], ACT.Copy).then_inc(a.hi, 1)
                            act.wait_ge(a.rest, u + 1)
                            act.activation(parts[:, u % 2, 1, :], q_rest[:, u % 2, :], ACT.Copy).then_inc(a.mid, 1)
                        for u in range(NU + 1, NPROJ):
                            take(u)

                        def exps(q, j):
                            for h in range(QH):
                                if h == 0 and isinstance(q, int) and q == 0:
                                    if j >= 2:
                                        act.wait_ge(a.pv, j - 1)
                                elif h == 0:
                                    act.wait_ge(a.pv, q * ST + j - 1)
                                act.wait_ge(a.scores, q * (QH * ST) + QH * j + h + 1)
                                act.activation(probs[:, j % 2, h, j * P:S], st_ps[(QH * j + h) % 2][:, j * P:S],
                                               ACT.Exp).then_inc(a.act_rd, 1)

                        def quad(q):
                            first = isinstance(q, int) and q == 0
                            for j in range(ST):
                                exps(q, j)
                                if j == O_AT:
                                    act.wait_ge(a.pv, q * ST + 4)
                                    if not first:
                                        act.wait_ge(a.out, q * (16 * OUTS))
                                    act.activation(o_sb[:, 0:512], o_ps[:, 0:512], ACT.Copy).then_inc(a.act_rd, 1)
                            act.wait_ge(a.pv, q * ST + ST)
                            act.activation(o_sb[:, 512:S], o_ps[:, 512:S], ACT.Copy).then_inc(a.act_rd, 1)

                        quad(0)
                        with act.Fori(1, NQ) as q:
                            quad(q)

                    @block.vector
                    def _(dve):
                        swap = [p ^ 1 for p in range(32)]

                        def turn(u):
                            tb = units[u][2]
                            dve.wait_ge(a.act_rd, u + 1)
                            if u >= 2:
                                dve.wait_ge(a.sin, u - 1)
                            dve.tensor_tensor(t_cos[:, u % 2, :], q_raw[:, u % 2, :], cos_sin[:, 0, tb * BLK:tb * BLK + BLK],
                                              ALU.mult)
                            dve.stream_shuffle(q_swap[:, u % 2, :], q_raw[:, u % 2, :], swap).then_inc(a.swap, 1)

                        turn(0)
                        for u in range(NU):
                            dve.wait_ge(a.sin, u + 1)
                            dve.wait_ge(a.swap, u + 1)
                            if u >= 2:
                                dve.wait_ge(a.hi, u - 1)
                            dve.tensor_tensor(q_rot[:, u % 2, :], t_cos[:, u % 2, :], t_sin[:, u % 2, :], ALU.add).then_inc(a.rot, 1)
                            if u + 1 < NU:
                                turn(u + 1)
                            dve.wait_ge(a.hi, u + 1)
                            if u >= 2:
                                dve.wait_ge(a.lo, u - 1)
                            dve.tensor_tensor(q_rest[:, u % 2, :], q_rot[:, u % 2, :], parts[:, u % 2, 0, :],
                                              ALU.subtract).then_inc(a.rest, 1)
                            dve.wait_ge(a.mid, u + 1)
                            dve.tensor_tensor(parts[:, u % 2, 2, :], q_rest[:, u % 2, :], parts[:, u % 2, 1, :],
                                              ALU.subtract).then_inc(a.lo, 1)

                        def maxima(q):
                            for n, (h, i, p) in enumerate(MAX_UNITS):
                                w = min(512, (i + 1) * P - 512 * p)
                                out = nm[:, h, i:i + 1] if i < 4 else mx[:, p, h, i:i + 1]
                                dve.wait_ge(a.max, q * NMAX + n + 1)
                                dve.tensor_reduce(out, mx_ps[n % 2][:, 0:w], AX.X, ALU.max, negate=True).then_inc(a.max_rd, 1)
                            dve.wait_ge(a.max_rd, q * NMAX + NMAX - 1)
                            dve.tensor_tensor(nm[:, :, 4:ST], mx[:, 0, :, 4:ST],
                                              mx[:, 1, :, 4:ST], ALU.min).then_inc(a.m_ready, 1)
                            turned = mx_ps[0][0:QH * ST, 0:P]
                            hi, mid, lo = (m_parts[:, ds(q, 1), r, :].rearrange("p a n -> p (a n)") for r in range(3))
                            dve.wait_ge(a.max, q * NMAX + NMAX)
                            dve.tensor_copy(hi, turned).then_inc(a.m_chain, 1)
                            dve.wait_ge(a.m_chain, q * 2 + 1)
                            dve.tensor_tensor(m_rest[:], turned, hi, ALU.subtract).then_inc(a.max_rd, 1)
                            dve.wait_ge(a.max_rd, q * NMAX + NMAX)
                            dve.tensor_copy(mid, m_rest[:]).then_inc(a.m_chain, 1)
                            dve.wait_ge(a.m_chain, q * 2 + 2)
                            dve.tensor_tensor(lo, m_rest[:], mid, ALU.subtract).then_inc(a.m_split, 1)

                        maxima(0)
                        with dve.Fori(1, NQ) as q:
                            maxima(q)

                    @block.gpsimd
                    def _(pool):
                        for u, (w, g, tb) in enumerate(units):
                            pool.wait_ge(a.swap, u + 1)
                            if u >= 2:
                                pool.wait_ge(a.rot, u - 1)
                            pool.tensor_tensor(t_sin[:, u % 2, :], q_swap[:, u % 2, :], cos_sin[:, 1, tb * BLK:tb * BLK + BLK],
                                               ALU.mult).then_inc(a.sin, 1)

                        def values(q):
                            pool.tensor_copy(va[:].rearrange("p j n -> p j n"),
                                             vh[:, :, ds(q * QH, QH), :].rearrange("p j h v -> p j (h v)")).then_inc(a.va, 1)

                        pool.wait_ge(a.act_rd, NPROJ)
                        values(0)
                        with pool.Fori(1, NQ) as q:
                            pool.wait_ge(a.pv, q * ST)
                            values(q)

                clear(nc, a)
            clear(nc, n)
        clear(nc, c)


def tok(t, b, i):
    return t[:, ds(b * ST + i, 1), :].rearrange("p a n -> p (a n)")


def layernorm_tail(act, mv, lnv, rstd, t, aggr, lnv_done, rstd_done, n):
    act.wait_ge(aggr, n)
    act.activation(lnv[:, t:t + 1], mv[:, t, 1:2], ACT.Ln, bias=LN_EPS).then_inc(lnv_done, 1)
    act.wait_ge(lnv_done, n)
    act.activation(rstd[:, t:t + 1], lnv[:, t:t + 1], ACT.Exp, scale=-0.5).then_inc(rstd_done, 1)


def layernorm_stats(dve, src, st6, mv, t, stats, aggr, n):
    dve.bn_stats(st6[:, t, :], src).then_inc(stats, 1)
    dve.wait_ge(stats, n)
    dve.bn_aggr(mv[:, t, :], st6[:, t, :]).then_inc(aggr, 1)


def softmax_sums_stage(nc, ctx, att_l, inv_l):
    s = semaphores(nc, ctx, "l", "load inv store")
    with ExitStack() as mem:
        sums = mem.enter_context(nc.sbuf_tensor("sums", [P, BLK], F32))
        inv = mem.enter_context(nc.sbuf_tensor("inv", [P, BLK], F32))
        with nc.Block() as block:
            @block.sync
            def _(sp):
                sp.dma_start(sums[:], att_l.rearrange("h (a t) -> h a t", t=BLK)).then_inc(s.load, 16)
                sp.wait_ge(s.inv, 1)
                sp.dma_start(inv_l.rearrange("h (a t) -> h a t", t=BLK), inv[:]).then_inc(s.store, 16)
                sp.wait_ge(s.store, 16)

            @block.vector
            def _(dve):
                dve.wait_ge(s.load, 16)
                dve.reciprocal(inv[:], sums[:]).then_inc(s.inv, 1)

        clear(nc, s)


NC = 64
HIT = 0.01
TEMPERATURE = 0.1


def dense_stage(nc, ctx, ps, keep, x1, dn, x, att_o, inv_l, wo, w_dense, w_cent, bias):
    w = semaphores(nc, ctx, "dw", "load zero")
    s = semaphores(nc, ctx, "d", "o0 o1 x div y st1 ag1 ln1 rs1 up x1 st2 ag2 ln2 rs2 xn tr ev "
                   "dn lg dn_rd top nb exp inv hit lg_rd")
    with ExitStack() as mem:
        def sb(name, shape, dt=F32):
            return mem.enter_context(nc.sbuf_tensor(name, shape, dt))

        wo_sb = sb("wo_sb", [P, KC, D])
        wd_sb = sb("wd_sb", [P, KC, D])
        wc_sb = sb("wc_sb", [P, KC, NC])
        bias_sb = sb("bias_sb", [P, D])
        oT = sb("oT", [P, KC, S])
        lT = sb("lT", [P, KC, S])
        x_sb = sb("x_sb", [P, ST, D])
        up = sb("up", [P, 2, D])
        xn = sb("xn", [P, 2, D])
        xnT = sb("d_xnT", [P, ST, KC, P])
        st1, mv1, ln1, rs1 = sb("st1", [P, ST, 6]), sb("mv1", [P, ST, 2]), sb("ln1", [P, ST]), sb("rs1", [P, ST])
        st2, mv2, ln2, rs2 = sb("st2", [P, ST, 6]), sb("mv2", [P, ST, 2]), sb("ln2", [P, ST]), sb("rs2", [P, ST])
        top, nb = sb("top", [P, ST]), sb("nb", [P, ST])
        ex, tot, inv = sb("ex", [P, ST, NC]), sb("tot", [P, ST]), sb("d_inv", [P, ST])
        hit = sb("hit", [P, ST, NC])

        with nc.Block() as block:
            @block.sync
            def _(sp):
                for dst, src in ((wo_sb, wo), (wd_sb, w_dense), (wc_sb, w_cent)):
                    sp.dma_start(dst[:], src.rearrange("(c p) n -> p c n", p=P)).then_inc(w.load, 16)
                sp.dma_start(bias_sb[:], bias.rearrange("(a n) -> a n", a=1).broadcast_to([P, D])).then_inc(w.load, 16)
                sp.wait_ge(w.load, 64)

            @block.scalar
            def _(act):
                act.preload_act_table_set("natural_log_exp_and_others")

            @block.vector
            def _(dve):
                dve.memset(keep.hits[:], 0.0).then_inc(w.zero, 1)
                dve.wait_ge(w.zero, 1)

        with nc.Fori(0, B) as b:
            with nc.Block() as block:
                @block.sync
                def _(sp):
                    for c in range(KC):
                        sp.dma_start(oT[:, c, :], att_o[GH * c:GH * c + GH, :, ds(b * S, S)]
                                     .rearrange("h r t -> (h r) t")).then_inc(s.o0, 16)
                    for c in range(KC):
                        sp.dma_start(lT[:, c, :], inv_l[GH * c:GH * c + GH, ds(b * S, S)].unsqueeze(1)
                                     .broadcast_to([GH, HD, S])).then_inc(s.o1, 16)
                    for g in range(2):
                        sp.dma_start(x_sb[:, TB * g:TB * g + TB, :], x[ds(b * 2 + g, 1), :, :]
                                     .rearrange("a (t p) d -> p (a t) d", p=P)).then_inc(s.x, 16)

                @block.tensor
                def _(pe):
                    pe.wait_ge(s.div, 1)
                    for i in range(ST + 4):
                        if i < ST:
                            if i >= 2:
                                pe.wait_ge(s.up, i - 1)
                            for k in range(KC):
                                mm = pe.matmul(ps[:, i % 2, :], oT[:, k, i * P:i * P + P], wo_sb[:, k, :],
                                               start=(k == 0), stop=(k == KC - 1))
                            mm.then_inc(s.y, 1)
                        t = i - 3
                        if 0 <= t < ST:
                            pe.wait_ge(s.xn, t + 1)
                            if t >= 2:
                                pe.wait_ge(s.ev, t - 1)
                            for k in range(KC):
                                mm = pe.transpose(ps[:, 2 + t % 2, k * P:k * P + P], xn[:, t % 2, k * P:k * P + P],
                                                  keep.ident[:])
                            mm.then_inc(s.tr, 1)
                        t = i - 4
                        if 0 <= t < ST:
                            pe.wait_ge(s.ev, t + 1)
                            if t >= 2:
                                pe.wait_ge(s.dn_rd, t - 1)
                            for k in range(KC):
                                mm = pe.matmul(ps[:, 4 + t % 2, :], xnT[:, t, k, :], wd_sb[:, k, :],
                                               start=(k == 0), stop=(k == KC - 1))
                            mm.then_inc(s.dn, 1)
                            if t >= 2:
                                pe.wait_ge(s.lg_rd, t - 1)
                            for k in range(KC):
                                mm = pe.matmul(ps[:, 6 + t % 2, 0:NC], xnT[:, t, k, :], wc_sb[:, k, :],
                                               start=(k == 0), stop=(k == KC - 1))
                            mm.then_inc(s.lg, 1)

                @block.scalar
                def _(act):
                    for i in range(ST + 4):
                        if i < ST:
                            layernorm_tail(act, mv1, ln1, rs1, i, s.ag1, s.ln1, s.rs1, i + 1)
                        t = i - 2
                        if 0 <= t < ST:
                            layernorm_tail(act, mv2, ln2, rs2, t, s.ag2, s.ln2, s.rs2, t + 1)
                        t = i - 3
                        if 0 <= t < ST:
                            act.wait_ge(s.tr, t + 1)
                            act.activation(xnT[:, t, :, :].rearrange("p c n -> p (c n)"), ps[:, 2 + t % 2, :],
                                           ACT.Copy).then_inc(s.ev, 1)
                        t = i - 4
                        if 0 <= t < ST:
                            act.wait_ge(s.nb, t + 1)
                            act.activation(ex[:, t, :], ps[:, 6 + t % 2, 0:NC], ACT.Exp, bias=nb[:, t:t + 1],
                                           scale=1.0 / TEMPERATURE, accum_out=tot[:, t:t + 1]).then_inc(s.exp, 1)

                @block.gpsimd
                def _(pool):
                    for t in range(ST):
                        if t % TB == 0:
                            pool.wait_ge(s.x, 32)
                        pool.wait_ge(s.up, t + 1)
                        pool.tensor_tensor(tok(x1, b, t), x_sb[:, t, :], up[:, t % 2, :], ALU.add).then_inc(s.x1, 1)

                @block.vector
                def _(dve):
                    dve.wait_ge(s.o0, 16 * KC)
                    dve.wait_ge(s.o1, 16 * KC)
                    dve.tensor_tensor(oT[:], oT[:], lT[:], ALU.mult).then_inc(s.div, 1)
                    for i in range(ST + 4):
                        if i < ST:
                            dve.wait_ge(s.y, i + 1)
                            layernorm_stats(dve, ps[:, i % 2, :], st1, mv1, i, s.st1, s.ag1, i + 1)
                            dve.wait_ge(s.ag1, i + 1)
                            dve.wait_ge(s.rs1, i + 1)
                            if i >= 2:
                                dve.wait_ge(s.x1, i - 1)
                            dve.tensor_scalar(up[:, i % 2, :], ps[:, i % 2, :], mv1[:, i, 0:1], rs1[:, i:i + 1],
                                              ALU.subtract, ALU.mult).then_inc(s.up, 1)
                        t = i - 1
                        if 0 <= t < ST:
                            dve.wait_ge(s.x1, t + 1)
                            layernorm_stats(dve, tok(x1, b, t), st2, mv2, t, s.st2, s.ag2, t + 1)
                        t = i - 2
                        if 0 <= t < ST:
                            dve.wait_ge(s.rs2, t + 1)
                            if t >= 2:
                                dve.wait_ge(s.tr, t - 1)
                            dve.tensor_scalar(xn[:, t % 2, :], tok(x1, b, t), mv2[:, t, 0:1], rs2[:, t:t + 1],
                                              ALU.subtract, ALU.mult).then_inc(s.xn, 1)
                        t = i - 4
                        if 0 <= t < ST:
                            dve.wait_ge(s.lg, t + 1)
                            dve.tensor_reduce(top[:, t:t + 1], ps[:, 6 + t % 2, 0:NC], AX.X, ALU.max).then_inc(s.top, 1)
                            dve.wait_ge(s.top, t + 1)
                            dve.tensor_scalar(nb[:, t:t + 1], top[:, t:t + 1], -1.0 / TEMPERATURE, None,
                                              ALU.mult).then_inc(s.nb, 1)
                            dve.wait_ge(s.dn, t + 1)
                            dve.tensor_tensor(tok(dn, b, t), ps[:, 4 + t % 2, :], bias_sb[:], ALU.add).then_inc(s.dn_rd, 1)
                            dve.wait_ge(s.exp, t + 1)
                            dve.reciprocal(inv[:, t:t + 1], tot[:, t:t + 1]).then_inc(s.inv, 1)
                            dve.wait_ge(s.inv, t + 1)
                            dve.tensor_scalar(hit[:, t, :], ex[:, t, :], inv[:, t:t + 1], HIT,
                                              ALU.mult, ALU.is_gt).then_inc(s.lg_rd, 1)
                            dve.wait_ge(s.lg_rd, t + 1)
                            dve.tensor_reduce(keep.query_hit[:, ds(b * ST + t, 1)], hit[:, t, :], AX.X, ALU.max)
                            if t:
                                dve.wait_ge(s.hit, t)
                            dve.tensor_tensor(keep.hits[:], keep.hits[:], hit[:, t, :], ALU.max).then_inc(s.hit, 1)
            clear(nc, s)
        clear(nc, w)


def rows_stage(nc, ctx, ps, keep, assignments, cluster_ids):
    s = semaphores(nc, ctx, "r", "load ones count sel own one_hot rows")
    with ExitStack() as mem:
        def sb(name, shape, dt=F32):
            return mem.enter_context(nc.sbuf_tensor(name, shape, dt))

        ids = sb("ids", [NC, 1])
        asg_i = sb("asg_i", [NC, D], I32)
        asg = sb("asg", [NC, D])
        one_hot = sb("one_hot", [NC, D])
        ones = sb("ones", [P, P])
        sel = sb("sel", [NC, 1])
        sel_b = sb("sel_b", [NC, P])
        with nc.Block() as block:
            @block.sync
            def _(sp):
                sp.dma_start(ids[:], cluster_ids).then_inc(s.load, 16)
                sp.dma_start(asg_i[:], assignments.rearrange("(a n) -> a n", a=1).broadcast_to([NC, D])).then_inc(s.load, 16)

            @block.tensor
            def _(pe):
                pe.wait_ge(s.ones, 1)
                pe.matmul(ps[0:NC, 0, 0:1], keep.hits[:], ones[:, 0:1], start=True, stop=True).then_inc(s.count, 1)
                pe.wait_ge(s.one_hot, 1)
                pe.wait_ge(s.sel, 2)
                pe.matmul(ps[:, 1, :], sel_b[:], one_hot[:], start=True, stop=True).then_inc(s.rows, 1)

            @block.vector
            def _(dve):
                dve.memset(ones[:], 1.0).then_inc(s.ones, 1)
                dve.wait_ge(s.load, 32)
                dve.tensor_copy(asg[:], asg_i[:]).then_inc(s.own, 1)
                dve.wait_ge(s.own, 1)
                dve.tensor_scalar(one_hot[:], asg[:], ids[:, 0:1], None, ALU.is_equal).then_inc(s.one_hot, 1)
                dve.wait_ge(s.count, 1)
                dve.tensor_scalar(sel[:], ps[0:NC, 0, 0:1], 0.0, None, ALU.is_gt).then_inc(s.sel, 1)
                dve.wait_ge(s.sel, 1)
                dve.wait_ge(s.ones, 1)
                dve.tensor_scalar(sel_b[:], ones[0:NC, :], sel[:, 0:1], None, ALU.mult).then_inc(s.sel, 1)
                dve.wait_ge(s.rows, 1)
                dve.tensor_copy(keep.rows[:], ps[:, 1, :]).then_inc(s.own, 1)
                dve.wait_ge(s.own, 2)

        clear(nc, s)


def input_stage(nc, ctx, ps, keep, x2, dn, xnT, x2_out):
    s = semaphores(nc, ctx, "n", "masked st1 ag1 ln1 rs1 up x2 st2 ag2 ln2 rs2 xn tr ev store")
    T = B * ST
    with ExitStack() as mem:
        def sb(name, shape, dt=F32):
            return mem.enter_context(nc.sbuf_tensor(name, shape, dt))

        up = sb("n_up", [P, 2, D])
        xn = sb("n_xn", [P, 2, D])
        st1, mv1, ln1, rs1 = sb("n_st1", [P, T, 6]), sb("n_mv1", [P, T, 2]), sb("n_ln1", [P, T]), sb("n_rs1", [P, T])
        st2, mv2, ln2, rs2 = sb("n_st2", [P, T, 6]), sb("n_mv2", [P, T, 2]), sb("n_ln2", [P, T]), sb("n_rs2", [P, T])

        with nc.Block() as block:
            @block.sync
            def _(sp):
                for g in range(NB):
                    sp.wait_ge(s.x2, TB * (g + 1))
                    sp.dma_start(x2_out[g].rearrange("(t p) d -> p t d", p=P),
                                 x2[:, TB * g:TB * g + TB, :]).then_inc(s.store, 16)
                sp.wait_ge(s.store, 16 * NB)

            @block.tensor
            def _(pe):
                for t in range(T):
                    pe.wait_ge(s.xn, t + 1)
                    if t >= 4:
                        pe.wait_ge(s.ev, t - 3)
                    for k in range(KC):
                        mm = pe.transpose(ps[:, t % 4, k * P:k * P + P], xn[:, t % 2, k * P:k * P + P], keep.ident[:])
                    mm.then_inc(s.tr, 1)

            @block.scalar
            def _(act):
                act.preload_act_table_set("natural_log_exp_and_others")
                for i in range(T + 6):
                    if i < T:
                        layernorm_tail(act, mv1, ln1, rs1, i, s.ag1, s.ln1, s.rs1, i + 1)
                    t = i - 3
                    if 0 <= t < T:
                        layernorm_tail(act, mv2, ln2, rs2, t, s.ag2, s.ln2, s.rs2, t + 1)
                    t = i - 5
                    if 0 <= t < T:
                        act.wait_ge(s.tr, t + 1)
                        act.activation(xnT[:, :, t * P:t * P + P], ps[:, t % 4, :].rearrange("p (c n) -> p c n", c=KC),
                                       ACT.Copy).then_inc(s.ev, 1)

            @block.gpsimd
            def _(pool):
                for t in range(T):
                    pool.wait_ge(s.up, t + 1)
                    pool.tensor_tensor(x2[:, t, :], x2[:, t, :], up[:, t % 2, :], ALU.add).then_inc(s.x2, 1)

            @block.vector
            def _(dve):
                for i in range(T + 4):
                    if i < T:
                        dve.scalar_tensor_tensor(dn[:, i, :], dn[:, i, :], keep.query_hit[:, i:i + 1],
                                                 keep.rows[:], ALU.mult, ALU.mult).then_inc(s.masked, 1)
                        dve.wait_ge(s.masked, i + 1)
                        layernorm_stats(dve, dn[:, i, :], st1, mv1, i, s.st1, s.ag1, i + 1)
                    t = i - 1
                    if 0 <= t < T:
                        dve.wait_ge(s.rs1, t + 1)
                        dve.wait_ge(s.ag1, t + 1)
                        if t >= 2:
                            dve.wait_ge(s.x2, t - 1)
                        dve.tensor_scalar(up[:, t % 2, :], dn[:, t, :], mv1[:, t, 0:1], rs1[:, t:t + 1],
                                          ALU.subtract, ALU.mult).then_inc(s.up, 1)
                    t = i - 3
                    if 0 <= t < T:
                        dve.wait_ge(s.x2, t + 1)
                        layernorm_stats(dve, x2[:, t, :], st2, mv2, t, s.st2, s.ag2, t + 1)
                    t = i - 4
                    if 0 <= t < T:
                        dve.wait_ge(s.rs2, t + 1)
                        dve.wait_ge(s.ag2, t + 1)
                        if t >= 2:
                            dve.wait_ge(s.tr, t - 1)
                        dve.tensor_scalar(xn[:, t % 2, :], x2[:, t, :], mv2[:, t, 0:1], rs2[:, t:t + 1],
                                          ALU.subtract, ALU.mult).then_inc(s.xn, 1)
        clear(nc, s)


DI = 1024
MT = DI // P
NS = 16
RK = 32
CONV = 4
NX = RK + 2 * NS
RMS_EPS = 1e-6
ROWS_AT_ONCE = 4
NBC = 2 * NS // ROWS_AT_ONCE
RING = 4
SPB = S // BLK


def tile(t, m):
    return t[:, m, :] if isinstance(m, int) else t[:, ds(m, 1), :].rearrange("p a n -> p (a n)")


def col(t, m, n=None):
    if n is not None:
        return tile(t, m)[:, n:n + 1]
    return t[:, m:m + 1] if isinstance(m, int) else t[:, ds(m, 1)]


def scan_stage(nc, ctx, ps, keep, xnT, w_in, conv_w, conv_b, w_x, norm_w, w_dt, a_log, d_par, bc, y_out):
    w = semaphores(nc, ctx, "mw", "load a neg ones")
    s = semaphores(nc, ctx, "m", "wx0 wx1 wz0 wz1 px padded head tap conv xc pz zs xp sq red twice lnx rsx n1 n2 "
                   "turned dt_in bc_sb bc_out dtm dt_sel skip_sel ab ex lg dts u skip da dbx h carry hc ys gate y0 y1")
    bc_load = [ctx.enter_context(nc.semaphore(f"m_bc{i}")) for i in range(NBC)]
    wx, wz, y_store = (s.wx0, s.wx1), (s.wz0, s.wz1), (s.y0, s.y1)
    PY, PX, PZ, PDT, PXP, PTR = 0, 2, 3, 4, 5, 6
    with ExitStack() as mem:
        def sb(name, shape, dt=F32):
            return mem.enter_context(nc.sbuf_tensor(name, shape, dt))

        cw = sb("cw", [P, MT, CONV])
        cb = sb("cb", [P, MT])
        xw = sb("xw", [P, MT, NX])
        nw = sb("nw", [P, NX])
        dtw = sb("dtw", [RK + 1, DI])
        na = sb("na", [P, MT, NS])
        dp = sb("dp", [P, MT])
        skip = sb("skip", [P, 2, P])
        dtm_w = sb("dtm_w", [RK + 1, 2, P])
        conv_carry = sb("conv_carry", [P, MT, CONV - 1])
        state = sb("state", [P, MT, NS])
        bcb = sb("bcb", [P, 2 * NS, BLK])
        xc = sb("xc", [P, MT, BLK])
        sz = sb("sz", [P, MT, BLK])
        dts = sb("dts", [P, 2, BLK])
        u = sb("u", [P, 2, BLK])
        soft = sb("soft", [P, BLK])
        wxr = sb("wxr", [P, 2, KC, P])
        wzr = sb("wzr", [P, 2, KC, P])
        pad = sb("pad", [P, 2, BLK + CONV - 1])
        acc = sb("acc", [P, 2, BLK])
        sq = sb("sq", [P, TB, NX])
        red = sb("red", [P, TB, 4])
        lnx = sb("lnx", [P, TB, 4])
        rsx = sb("rsx", [P, TB, 4])
        ssm = sb("ssm", [P, TB, NX])
        dtT = sb("dtT", [RK + 1, BLK])
        bcT = sb("bcT", [NX, BLK])
        da = sb("da", [P, RING, BLK])
        dbx = sb("dbx", [P, RING, BLK])
        hs = sb("hs", [P, RING, BLK])
        hc = sb("hc", [P, RING, BLK])
        yo = sb("yo", [P, 2, BLK])

        with nc.Block() as block:
            @block.sync
            def _(sp):
                for dst, src in ((cw[:], conv_w.rearrange("(m p) k -> p m k", p=P)),
                                 (cb[:], conv_b),
                                 (xw[:], w_x.rearrange("(m p) n -> p m n", p=P)),
                                 (nw[:], norm_w.rearrange("(a n) -> a n", a=1).broadcast_to([P, NX])),
                                 (dtw[:], w_dt),
                                 (na[:], a_log.rearrange("(m p) n -> p m n", p=P)),
                                 (dp[:], d_par)):
                    sp.dma_start(dst, src).then_inc(w.load, 16)
                sp.wait_ge(w.load, 16 * 7)

            @block.gpsimd
            def _(pool):
                pool.memset(dtT[RK:RK + 1, :], 1.0).then_inc(w.ones, 1)
                pool.wait_ge(w.ones, 1)

            @block.scalar
            def _(act):
                act.wait_ge(w.load, 16 * 7)
                act.activation(na[:], na[:], ACT.Exp).then_inc(w.a, 1)

            @block.vector
            def _(dve):
                dve.wait_ge(w.a, 1)
                dve.tensor_scalar(na[:], na[:], -1.0, None, ALU.mult).then_inc(w.neg, 1)
                dve.wait_ge(w.neg, 1)
        clear(nc, w)

        def turns(eng, k, turn):
            if k < 0:
                for m in range(MT):
                    turn(k, m, m % 2)
                return
            apart = 3 if k == 0 else 1
            for m in range(apart):
                turn(k, m, m % 2)
            with eng.Fori(0, (MT - 1 - apart) // 2) as i:
                for step in range(2):
                    turn(k, i * 2 + (apart + step), (apart + step) % 2)
            turn(k, MT - 1, 1)

        def kind(k, m):
            first, last = isinstance(m, int) and m == 0, isinstance(m, int) and m == MT - 1
            return k >= 0, k < NB - 1, (k >= 0 if first else k < NB - 1), first, last

        with nc.Block() as block:
            @block.sync
            def _(sp):
                def load(k, m, par):
                    T = k * MT + m
                    _, px, pz, first, _ = kind(k, m)
                    if px:
                        if from_on(T + MT, 2):
                            sp.wait_ge(s.px, T + MT - 1)
                        sp.dma_start(wxr[:, par, :, :], weight_tile(m)).then_inc(wx[par], 16)
                    if pz:
                        if from_on(T + MT - 1, 2):
                            sp.wait_ge(s.pz, T + MT - 2)
                        sp.dma_start(wzr[:, 1 - par, :, :], weight_tile(2 * MT - 1 if first else m + (MT - 1))).then_inc(wz[1 - par], 16)

                def weight_tile(i):
                    return w_in[i] if isinstance(i, int) else w_in[ds(i, 1), :, :, :].rearrange("a p c n -> (a p) c n")

                def turn(k, m, par):
                    scans, px, _, first, last = kind(k, m)
                    if last and px:
                        load(k + 1, 0, 0)
                    elif not last:
                        load(k, m + 1, 1 - par)
                    if scans and from_on(k * MT + m, 1):
                        store(k, m, par)
                    if last and px:
                        broadcast(k + 1)

                def store(k, m, par):
                    first = isinstance(m, int) and m == 0
                    sp.wait_ge(s.gate, k * MT + m)
                    kb, mb = (k - 1, MT - 1) if first else (k, m - 1)
                    dst = y_out[kb, :, mb, :] if isinstance(mb, int) else y_out[kb, :, ds(mb, 1), :].rearrange("p a n -> p (a n)")
                    sp.dma_start(dst, yo[:, 1 - par, :]).then_inc(y_store[1 - par], 16)

                def broadcast(j):
                    sp.wait_ge(s.bc_sb, j + 1)
                    if j:
                        for q in bc_load:
                            sp.wait_ge(q, 16 * j)
                    sp.dma_start(bc[:, :], bcT[RK:NX, :]).then_inc(s.bc_out, 16)
                    sp.wait_ge(s.bc_out, 16 * (j + 1))
                    for i in range(NBC):
                        n = (i // 2) * ROWS_AT_ONCE
                        row = (i % 2) * NS + n
                        if j:
                            sp.wait_ge((s.dbx, s.hc)[i % 2], ((j * MT) - 1) * NS + n + ROWS_AT_ONCE)
                        sp.dma_start(bcb[:, row:row + ROWS_AT_ONCE, :], bc[row:row + ROWS_AT_ONCE, :].unsqueeze(0)
                                     .broadcast_to([P, ROWS_AT_ONCE, BLK])).then_inc(bc_load[i], 16)

                load(-1, 0, 0)
                for k in range(-1, NB):
                    turns(sp, k, turn)
                store(NB, 0, 0)
                for q in y_store:
                    sp.wait_ge(q, 16 * NB * MT // 2)

            @block.tensor
            def _(pe):
                def project_x(k, m, par, c):
                    T = k * MT + m
                    if c == 0:
                        pe.wait_ge(wx[par], weights(k, m, par))
                        if from_on(T + MT, 1):
                            pe.wait_ge(s.tap, T + MT)
                            pe.wait_ge(s.padded, T + MT)
                    mm = pe.matmul(ps[:, PX, :], wxr[:, par, c, :], xnT[:, c, (k + 1) * BLK:(k + 2) * BLK],
                                   start=(c == 0), stop=(c == KC - 1))
                    if c == KC - 1:
                        mm.then_inc(s.px, 1)

                def project_z(k, m, par, c):
                    T = k * MT + m
                    first = kind(k, m)[3]
                    j = k if first else k + 1
                    if c == 0:
                        pe.wait_ge(wz[1 - par], weights_z(k, m, par))
                        if from_on(T + MT - 1, 1):
                            pe.wait_ge(s.zs, T + MT - 1)
                    mm = pe.matmul(ps[:, PZ, :], wzr[:, 1 - par, c, :], xnT[:, c, j * BLK:(j + 1) * BLK],
                                   start=(c == 0), stop=(c == KC - 1))
                    if c == KC - 1:
                        mm.then_inc(s.pz, 1)

                def step_sizes(q, par, first):
                    if from_on(q, 1):
                        pe.wait_ge(s.dts, q)
                    if first:
                        pe.wait_ge(s.dt_in, q // MT + 1)
                    pe.wait_ge(s.dt_sel, q + 1)
                    pe.matmul(ps[:, PDT, :], dtm_w[:, par, :], dtT[:], start=True, stop=True).then_inc(s.dtm, 1)

                def turn(k, m, par):
                    T = k * MT + m
                    scans, px, pz, first, last = kind(k, m)
                    if scans:
                        if from_on(T, 2):
                            pe.wait_ge(s.gate, T - 1)
                        pe.wait_ge(s.skip_sel, T + 1)
                        pe.matmul(ps[:, PY + par, :], skip[:, par, :], tile(xc, m), start=True, stop=False).then_inc(s.skip, 1)
                    for n in range(NS):
                        if px and n < KC:
                            project_x(k, m, par, n)
                        if pz and KC < n <= 2 * KC:
                            project_z(k, m, par, n - KC - 1)
                        if scans and not last and n == KC:
                            step_sizes(T + 1, 1 - par, False)
                        if last and px and n == 11:
                            pe.wait_ge(s.xc, (k + 2) * MT)
                            for t in range(TB):
                                for i in range(MT):
                                    mm = pe.matmul(ps[:, PXP, t * NX:t * NX + NX], xc[:, i, t * P:t * P + P], xw[:, i, :],
                                                   start=(i == 0), stop=(i == MT - 1))
                            mm.then_inc(s.xp, 1)
                        if last and px and n == NS - 1:
                            pe.wait_ge(s.n2, k + 2)
                            for t in range(TB):
                                mm = pe.transpose(ps[0:NX, PTR, t * P:t * P + P], ssm[:, t, :], keep.ident[:])
                            mm.then_inc(s.turned, 1)
                        if scans:
                            pe.wait_ge(s.hc, T * NS + n + 1)
                            pe.matmul(ps[:, PY + par, :], keep.ident[:], hc[:, n % RING, :],
                                      start=False, stop=(n == NS - 1)).then_inc(s.ys, 1)
                    if last and px:
                        step_sizes(T + 1, 0, True)

                for k in range(-1, NB):
                    turns(pe, k, turn)

            @block.scalar
            def _(act):
                def take_x(k, m, par):
                    U = (k + 1) * MT + m
                    act.wait_ge(s.px, U + 1)
                    if from_on(U, 2):
                        act.wait_ge(s.conv, CONV * (U - 1))
                        act.wait_ge(s.xc, U - 1)
                    act.activation(pad[:, par, CONV - 1:], ps[:, PX, :], ACT.Copy).then_inc(s.padded, 1)
                    act.activation(acc[:, par, :], ps[:, PX, :], ACT.Identity, bias=col(cb, m),
                                   scale=col(cw, m, CONV - 1)).then_inc(s.tap, 1)

                def silus(k, m, par):
                    T = k * MT + m
                    scans, px, pz, first, last = kind(k, m)
                    if pz:
                        act.wait_ge(s.pz, T + MT)
                        if from_on(T, 1):
                            act.wait_ge(s.gate, T)
                        act.activation(tile(sz, MT - 1 if first else m - 1), ps[:, PZ, :], ACT.Silu).then_inc(s.zs, 1)
                    if px:
                        act.wait_ge(s.conv, CONV * (T + MT + 1))
                        if scans:
                            act.wait_ge(s.skip, T + 1)
                            act.wait_ge(s.u, T + 1)
                        act.activation(tile(xc, m), acc[:, par, :], ACT.Silu).then_inc(s.xc, 1)
                    if px or pz:
                        act.preload_act_table_set("natural_log_exp_and_others")

                def softplus(q):
                    act.wait_ge(s.dtm, q + 1)
                    if from_on(q, 1):
                        act.wait_ge(s.dts, q)
                    act.activation(soft[:], ps[:, PDT, :], ACT.Abs).then_inc(s.ab, 1)
                    act.wait_ge(s.ab, q + 1)
                    act.activation(soft[:], soft[:], ACT.Exp, scale=-1.0).then_inc(s.ex, 1)
                    act.wait_ge(s.ex, q + 1)
                    act.activation(soft[:], soft[:], ACT.Ln, bias=1.0).then_inc(s.lg, 1)

                def keep_state(T, m, n):
                    act.wait_ge(s.h, T * NS + n + 1)
                    act.activation(col(state, m, n), hs[:, n % RING, BLK - 1:BLK], ACT.Copy).then_inc(s.carry, 1)

                def turn(k, m, par):
                    T = k * MT + m
                    scans, px, pz, first, last = kind(k, m)
                    for n in range(NS):
                        if px and n == (8 if last else 9):
                            take_x(k, m, par)
                        if n == (12 if last else 14):
                            silus(k, m, par)
                        if scans and not last and n == 10:
                            softplus(T + 1)
                        if last and px and n == NS - 1:
                            act.wait_ge(s.xp, k + 2)
                            act.activation(sq[:].rearrange("p t n -> p (t n)"), ps[:, PXP, 0:TB * NX],
                                           ACT.Square).then_inc(s.sq, 1)
                        if scans:
                            if n == 0:
                                act.wait_ge(s.dts, T + 1)
                            if n >= RING or from_on(T, 1):
                                act.wait_ge(s.h, T * NS + n + 1 - RING)
                            act.activation(da[:, n % RING, :], dts[:, par, :], ACT.Exp,
                                           scale=col(na, m, n)).then_inc(s.da, 1)
                            if n < RING - 1:
                                if keeps((k - 1) if first else k) and from_on(T, 1):
                                    keep_state(T - 1, MT - 1 if first else m - 1, NS + n + 1 - RING)
                            elif keeps(k):
                                keep_state(T, m, n + 1 - RING)
                    if last and px:
                        act.wait_ge(s.twice, k + 2)
                        act.activation(lnx[:, :, 0:2], red[:, :, 0:2], ACT.Ln, bias=RMS_EPS, scale=1.0 / RK)
                        act.activation(lnx[:, :, 2:4], red[:, :, 2:4], ACT.Ln, bias=RMS_EPS,
                                       scale=1.0 / NS).then_inc(s.lnx, 1)
                        act.wait_ge(s.lnx, k + 2)
                        act.activation(rsx[:], lnx[:], ACT.Exp, scale=-0.5).then_inc(s.rsx, 1)
                        act.wait_ge(s.turned, k + 2)
                        if k >= 0:
                            act.wait_ge(s.dtm, (k + 1) * MT)
                        act.activation(dtT[0:RK, :], ps[0:RK, PTR, :], ACT.Copy).then_inc(s.dt_in, 1)
                        softplus(T + 1)

                act.preload_act_table_set("natural_log_exp_and_others")
                for k in range(-1, NB):
                    turns(act, k, turn)

            @block.gpsimd
            def _(pool):
                def drive(q, m, par):
                    pool.wait_ge(s.dts, q + 1)
                    if from_on(q, 2):
                        pool.wait_ge(s.dbx, (q - 1) * NS)
                    pool.tensor_tensor(u[:, par, :], dts[:, par, :], tile(xc, m), ALU.mult).then_inc(s.u, 1)

                def turn(k, m, par):
                    T = k * MT + m
                    scans, px, pz, first, last = kind(k, m)
                    if scans:
                        for n in range(NS):
                            pool.wait_ge(s.h, T * NS + n + 1)
                            if first and n % ROWS_AT_ONCE == 0:
                                pool.wait_ge(bc_load[2 * (n // ROWS_AT_ONCE) + 1], 16 * (k + 1))
                            if n >= RING or from_on(T, 1):
                                pool.wait_ge(s.ys, T * NS + n + 1 - RING)
                            pool.tensor_tensor(hc[:, n % RING, :], hs[:, n % RING, :], bcb[:, NS + n, :],
                                               ALU.mult).then_inc(s.hc, 1)
                            if not last and n == 11:
                                drive(T + 1, m + 1, 1 - par)
                    if last and px:
                        pool.wait_ge(s.xc, (k + 2) * MT)
                        drive(T + 1, 0, 0)

                for k in range(-1, NB):
                    turns(pool, k, turn)

            @block.vector
            def _(dve):
                def head(k, m, par):
                    U = (k + 1) * MT + m
                    if from_on(U, 2):
                        dve.wait_ge(s.conv, CONV * (U - 1))
                    if (k + 1) % SPB == 0:
                        dve.memset(pad[:, par, 0:CONV - 1], 0.0).then_inc(s.head, 1)
                    else:
                        dve.tensor_copy(pad[:, par, 0:CONV - 1], tile(conv_carry, m)).then_inc(s.head, 1)

                def tap(k, m, par, i):
                    U = (k + 1) * MT + m
                    if i == 0:
                        dve.wait_ge(s.padded, U + 1)
                        dve.wait_ge(s.tap, U + 1)
                        dve.wait_ge(s.head, U + 1)
                    else:
                        dve.wait_ge(s.conv, CONV * U + i)
                    dve.scalar_tensor_tensor(acc[:, par, :], pad[:, par, i:i + BLK], col(cw, m, i), acc[:, par, :],
                                             ALU.mult, ALU.add).then_inc(s.conv, 1)
                    if i == CONV - 2:
                        dve.tensor_copy(tile(conv_carry, m), pad[:, par, BLK:BLK + CONV - 1]).then_inc(s.conv, 1)

                def steps(q, par):
                    dve.wait_ge(s.lg, q + 1)
                    if from_on(q, 2):
                        dve.wait_ge(s.da, (q - 1) * NS)
                        dve.wait_ge(s.u, q - 1)
                    dve.scalar_tensor_tensor(dts[:, par, :], ps[:, PDT, :], 0.0, soft[:], ALU.max, ALU.add).then_inc(s.dts, 1)

                def gate(T, m, par):
                    dve.wait_ge(s.ys, (T + 1) * NS)
                    dve.wait_ge(s.zs, T + 1)
                    if from_on(T, 2):
                        dve.wait_ge(y_store[par], 8 * (T - par))
                    dve.tensor_tensor(yo[:, par, :], ps[:, PY + par, :], tile(sz, m), ALU.mult).then_inc(s.gate, 1)

                def drive(k, m, par, n):
                    T = k * MT + m
                    if kind(k, m)[3] and n % ROWS_AT_ONCE == 0:
                        dve.wait_ge(bc_load[2 * (n // ROWS_AT_ONCE)], 16 * (k + 1))
                    if n >= RING or from_on(T, 1):
                        dve.wait_ge(s.h, T * NS + n + 1 - RING)
                    dve.tensor_tensor(dbx[:, n % RING, :], u[:, par, :], bcb[:, n, :], ALU.mult).then_inc(s.dbx, 1)

                def select(q, m, par):
                    if from_on(q, 2):
                        dve.wait_ge(s.dtm, q - 1)
                        dve.wait_ge(s.skip, q - 1)
                    dve.tensor_copy(dtm_w[:, par, :], dtw[:, m * P:m * P + P] if isinstance(m, int)
                                    else dtw[:, ds(m * P, P)]).then_inc(s.dt_sel, 1)
                    dve.tensor_scalar(skip[:, par, :], keep.ident[:], col(dp, m), None, ALU.mult).then_inc(s.skip_sel, 1)

                def turn(k, m, par):
                    T = k * MT + m
                    scans, px, pz, first, last = kind(k, m)
                    zero_start = k % SPB == 0
                    for n in range(NS):
                        if scans:
                            if n == 0:
                                dve.wait_ge(s.u, T + 1)
                                drive(k, m, par, 0)
                            if n + 1 < NS:
                                drive(k, m, par, n + 1)
                            dve.wait_ge(s.da, T * NS + n + 1)
                            dve.wait_ge(s.dbx, T * NS + n + 1)
                            if n >= RING or from_on(T, 1):
                                dve.wait_ge(s.hc, T * NS + n + 1 - RING)
                            kept = carried(k, m, n)
                            if kept is not None:
                                dve.wait_ge(s.carry, kept)
                            dve.tensor_tensor_scan(hs[:, n % RING, :], da[:, n % RING, :], dbx[:, n % RING, :],
                                                   0.0 if zero_start else col(state, m, n), ALU.mult, ALU.add).then_inc(s.h, 1)
                        if px and n == 0:
                            head(k, m, par)
                        if scans and n == 2 and from_on(T, 1):
                            gate(T - 1, MT - 1 if first else m - 1, 1 - par)
                        at = 6 if last else 7
                        if px and at <= n < at + CONV - 1:
                            tap(k, m, par, n - at)
                        if n == 0 and (scans and not last or last and px):
                            select(T + 1, 0 if last else m + 1, 1 - par)
                        if scans and not last and n == 10:
                            steps(T + 1, 1 - par)
                        if last and px and n == 12:
                            dve.wait_ge(s.sq, k + 2)
                            dve.tensor_reduce(red[:], sq[:].rearrange("p t (g i) -> p t g i", i=NS), AX.X, ALU.add).then_inc(s.red, 1)
                            dve.wait_ge(s.red, k + 2)
                            dve.tensor_tensor(sq[:, :, 0:2], red[:, :, 0:1].broadcast_to([P, TB, 2]),
                                              red[:, :, 1:2].broadcast_to([P, TB, 2]), ALU.add).then_inc(s.n1, 1)
                            dve.wait_ge(s.n1, 2 * (k + 1) + 1)
                            dve.tensor_copy(red[:, :, 0:2], sq[:, :, 0:2]).then_inc(s.twice, 1)
                        if last and px and n == 14:
                            dve.wait_ge(s.rsx, k + 2)
                            dve.tensor_tensor(ssm[:].rearrange("p t (g i) -> p t g i", i=NS),
                                              ps[:, PXP, 0:TB * NX].rearrange("p (t g i) -> p t g i", i=NS, g=4),
                                              rsx[:].unsqueeze(3).broadcast_to([P, TB, 4, NS]), ALU.mult).then_inc(s.n1, 1)
                            dve.wait_ge(s.n1, 2 * (k + 2))
                            dve.tensor_tensor(ssm[:], ssm[:], nw[:].unsqueeze(1).broadcast_to([P, TB, NX]),
                                              ALU.mult).then_inc(s.n2, 1)
                    if last and px:
                        dve.wait_ge(s.turned, k + 2)
                        if k >= 0:
                            dve.wait_ge(s.bc_out, 16 * (k + 1))
                        dve.tensor_copy(bcT[RK:NX, :], ps[RK:NX, PTR, :]).then_inc(s.bc_sb, 1)
                        steps(T + 1, 0)

                for k in range(-1, NB):
                    turns(dve, k, turn)
                gate(NB * MT - 1, MT - 1, 1)
        clear(nc, (*s, *bc_load))


def from_on(count, n):
    return not isinstance(count, int) or count >= n


def keeps(k):
    return k >= 0 and k % SPB < SPB - 1


def weights(k, m, par):
    return 8 * ((k + 1) * MT + m - par) + 16


def weights_z(k, m, par):
    return 8 * ((k + 1) * MT + m - 1 - (1 - par)) + 16


def carried(k, m, n):
    first = isinstance(m, int) and m == 0
    if not keeps((k - 1) if first and n < RING else k):
        return None
    return k // SPB * (SPB - 1) * MT * NS + (k % SPB * MT + m) * NS + n + 1 - RING


NE = 8
RE = 16
SCALING = 2.0
NL = NE * RE


def out_stage(nc, ctx, ps, keep, x2_in, y_in, w_out, w_gate_low, w_base, base_b, w_up, expert_ids, out):
    w = semaphores(nc, ctx, "tw", "load")
    s = semaphores(nc, ctx, "t", "y x o st1 ag1 ln1 rs1 up x3 st2 ag2 ln2 rs2 xn tr ev gl top idx pick wt sum inv "
                   "scl ltr lev base bs st3 ag3 ln3 rs3 up3 fin store")
    with ExitStack() as mem:
        def sb(name, shape, dt=F32):
            return mem.enter_context(nc.sbuf_tensor(name, shape, dt))

        wo = sb("t_wo", [P, MT, D])
        wgl = sb("wgl", [P, KC, NE + NL])
        wb = sb("wb", [P, KC, D])
        wu = sb("wu", [NL, D])
        bb = sb("bb", [P, D])
        eid = sb("eid", [P, NE])
        y = sb("t_y", [P, MT, BLK])
        x3 = sb("x3", [P, TB, D])
        up = sb("t_up", [P, 2, D])
        xn = sb("t_xn", [P, 2, D])
        xnT = sb("t_xnT", [P, TB, KC, P])
        st1, mv1, ln1, rs1 = sb("t_st1", [P, TB, 6]), sb("t_mv1", [P, TB, 2]), sb("t_ln1", [P, TB]), sb("t_rs1", [P, TB])
        st2, mv2, ln2, rs2 = sb("t_st2", [P, TB, 6]), sb("t_mv2", [P, TB, 2]), sb("t_ln2", [P, TB]), sb("t_rs2", [P, TB])
        st3, mv3, ln3, rs3 = sb("t_st3", [P, TB, 6]), sb("t_mv3", [P, TB, 2]), sb("t_ln3", [P, TB]), sb("t_rs3", [P, TB])
        logit = sb("logit", [P, TB, NE])
        top = sb("t_top", [P, TB, 8])
        idx = sb("t_idx", [P, TB, 8], mybir.dt.uint32)
        idf = sb("t_idf", [P, TB, 2])
        gap = sb("gap", [P, TB])
        wt = sb("t_wt", [P, TB, 2])
        mix = sb("t_mix", [P, TB, NE])
        mix1 = sb("t_mix1", [P, TB, NE])
        low = sb("t_low", [P, TB, NL])
        lowT = sb("t_lowT", [NL, TB, P])
        res = sb("t_res", [P, 2, D])
        up3 = sb("t_up3", [P, 2, D])
        fin = sb("t_fin", [P, TB, D])

        with nc.Block() as block:
            @block.sync
            def _(sp):
                for dst, src in ((wo[:], w_out.rearrange("(m p) n -> p m n", p=P)),
                                 (wgl[:], w_gate_low.rearrange("(c p) n -> p c n", p=P)),
                                 (wb[:], w_base.rearrange("(c p) n -> p c n", p=P)),
                                 (wu[:], w_up),
                                 (bb[:], base_b.rearrange("(a n) -> a n", a=1).broadcast_to([P, D])),
                                 (eid[:], expert_ids)):
                    sp.dma_start(dst, src).then_inc(w.load, 16)
                sp.wait_ge(w.load, 16 * 6)

        with nc.Fori(0, NB) as blk:
            with nc.Block() as block:
                @block.sync
                def _(sp):
                    sp.dma_start(y[:], y_in[ds(blk, 1), :, :, :].rearrange("a p m n -> (a p) m n")).then_inc(s.y, 16)
                    sp.dma_start(x3[:], x2_in[ds(blk, 1), :, :].rearrange("a (t p) d -> p (a t) d", p=P)).then_inc(s.x, 16)
                    sp.wait_ge(s.fin, TB)
                    sp.dma_start(out[ds(blk, 1), :, :].rearrange("a (t p) d -> p (a t) d", p=P), fin[:]).then_inc(s.store, 16)
                    sp.wait_ge(s.store, 16)

                @block.tensor
                def _(pe):
                    pe.wait_ge(s.y, 16)
                    for i in range(TB + 4):
                        if i < TB:
                            if i >= 2:
                                pe.wait_ge(s.up, i - 1)
                            for m in range(MT):
                                mm = pe.matmul(ps[:, i % 2, :], y[:, m, i * P:i * P + P], wo[:, m, :],
                                               start=(m == 0), stop=(m == MT - 1))
                            mm.then_inc(s.o, 1)
                        t = i - 2
                        if 0 <= t < TB:
                            pe.wait_ge(s.xn, t + 1)
                            for k in range(KC):
                                mm = pe.transpose(ps[:, 2, k * P:k * P + P], xn[:, t % 2, k * P:k * P + P], keep.ident[:])
                            mm.then_inc(s.tr, 1)
                            pe.wait_ge(s.ev, t + 1)
                            if t >= 1:
                                pe.wait_ge(s.scl, t)
                            for k in range(KC):
                                mm = pe.matmul(ps[:, 3, 0:NE + NL], xnT[:, t, k, :], wgl[:, k, :],
                                               start=(k == 0), stop=(k == KC - 1))
                            mm.then_inc(s.gl, 1)
                            if t >= 2:
                                pe.wait_ge(s.bs, t - 1)
                            for k in range(KC):
                                pe.matmul(ps[:, 4 + t % 2, :], xnT[:, t, k, :], wb[:, k, :], start=(k == 0), stop=False)
                            pe.wait_ge(s.scl, t + 1)
                            pe.transpose(ps[:, 6, 0:P], low[:, t, :], keep.ident[:]).then_inc(s.ltr, 1)
                            pe.wait_ge(s.lev, t + 1)
                            pe.matmul(ps[:, 4 + t % 2, :], lowT[:, t, :], wu[:], start=False, stop=True).then_inc(s.base, 1)

                @block.scalar
                def _(act):
                    for i in range(TB + 3):
                        if i < TB:
                            layernorm_tail(act, mv1, ln1, rs1, i, s.ag1, s.ln1, s.rs1, i + 1)
                        t = i - 1
                        if 0 <= t < TB:
                            layernorm_tail(act, mv2, ln2, rs2, t, s.ag2, s.ln2, s.rs2, t + 1)
                        t = i - 2
                        if 0 <= t < TB:
                            act.wait_ge(s.tr, t + 1)
                            act.activation(xnT[:, t, :, :].rearrange("p c n -> p (c n)"), ps[:, 2, :], ACT.Copy).then_inc(s.ev, 1)
                            act.wait_ge(s.pick, t + 1)
                            act.activation(wt[:, t, 1:2], gap[:, t:t + 1], ACT.Exp).then_inc(s.wt, 1)
                            act.wait_ge(s.ltr, t + 1)
                            act.activation(lowT[:, t, :], ps[:, 6, 0:P], ACT.Copy).then_inc(s.lev, 1)
                            layernorm_tail(act, mv3, ln3, rs3, t, s.ag3, s.ln3, s.rs3, t + 1)

                @block.gpsimd
                def _(pool):
                    pool.wait_ge(s.x, 16)
                    for i in range(TB + 2):
                        if i < TB:
                            pool.wait_ge(s.up, i + 1)
                            pool.tensor_tensor(x3[:, i, :], x3[:, i, :], up[:, i % 2, :], ALU.add).then_inc(s.x3, 1)
                        t = i - 2
                        if 0 <= t < TB:
                            pool.wait_ge(s.up3, t + 1)
                            pool.wait_ge(s.x3, t + 1)
                            pool.tensor_tensor(fin[:, t, :], x3[:, t, :], up3[:, t % 2, :], ALU.add).then_inc(s.fin, 1)

                @block.vector
                def _(dve):
                    for i in range(TB + 3):
                        if i < TB:
                            dve.wait_ge(s.o, i + 1)
                            layernorm_stats(dve, ps[:, i % 2, :], st1, mv1, i, s.st1, s.ag1, i + 1)
                            dve.wait_ge(s.ag1, i + 1)
                            dve.wait_ge(s.rs1, i + 1)
                            if i >= 2:
                                dve.wait_ge(s.x3, i - 1)
                            dve.tensor_scalar(up[:, i % 2, :], ps[:, i % 2, :], mv1[:, i, 0:1], rs1[:, i:i + 1],
                                              ALU.subtract, ALU.mult).then_inc(s.up, 1)
                        t = i - 1
                        if 0 <= t < TB:
                            dve.wait_ge(s.x3, t + 1)
                            layernorm_stats(dve, x3[:, t, :], st2, mv2, t, s.st2, s.ag2, t + 1)
                            dve.wait_ge(s.ag2, t + 1)
                            dve.wait_ge(s.rs2, t + 1)
                            if t >= 2:
                                dve.wait_ge(s.tr, t - 1)
                            dve.tensor_scalar(xn[:, t % 2, :], x3[:, t, :], mv2[:, t, 0:1], rs2[:, t:t + 1],
                                              ALU.subtract, ALU.mult).then_inc(s.xn, 1)
                        t = i - 2
                        if 0 <= t < TB:
                            dve.wait_ge(s.gl, t + 1)
                            dve.tensor_copy(logit[:, t, :], ps[:, 3, 0:NE]).then_inc(s.top, 1)
                            dve.wait_ge(s.top, 3 * t + 1)
                            dve.max(top[:, t, :], logit[:, t, :]).then_inc(s.top, 1)
                            dve.wait_ge(s.top, 3 * t + 2)
                            dve.max_index(idx[:, t, :], top[:, t, :], logit[:, t, :]).then_inc(s.top, 1)
                            dve.tensor_tensor(gap[:, t:t + 1], top[:, t, 1:2], top[:, t, 0:1], ALU.subtract).then_inc(s.pick, 1)
                            dve.wait_ge(s.top, 3 * t + 3)
                            dve.tensor_copy(idf[:, t, :], idx[:, t, 0:2]).then_inc(s.idx, 1)
                            dve.wait_ge(s.wt, t + 1)
                            dve.tensor_scalar(gap[:, t:t + 1], wt[:, t, 1:2], 1.0, None, ALU.add).then_inc(s.sum, 1)
                            dve.wait_ge(s.sum, 5 * t + 1)
                            dve.reciprocal(wt[:, t, 0:1], gap[:, t:t + 1]).then_inc(s.sum, 1)
                            dve.wait_ge(s.sum, 5 * t + 2)
                            dve.tensor_tensor(wt[:, t, 1:2], wt[:, t, 1:2], wt[:, t, 0:1], ALU.mult).then_inc(s.sum, 1)
                            dve.wait_ge(s.idx, t + 1)
                            dve.wait_ge(s.sum, 5 * t + 3)
                            for k, m in enumerate((mix, mix1)):
                                dve.tensor_scalar(m[:, t, :], eid[:], idf[:, t, k:k + 1], wt[:, t, k:k + 1],
                                                  ALU.is_equal, ALU.mult).then_inc(s.sum, 1)
                            dve.wait_ge(s.sum, 5 * t + 5)
                            dve.tensor_tensor(mix[:, t, :], mix[:, t, :], mix1[:, t, :], ALU.add).then_inc(s.inv, 1)
                            dve.wait_ge(s.inv, t + 1)
                            dve.scalar_tensor_tensor(low[:, t, :].rearrange("p (e r) -> p e r", r=RE),
                                                     ps[:, 3, NE:NE + NL].rearrange("p (e r) -> p e r", r=RE), SCALING,
                                                     mix[:, t, :].unsqueeze(2).broadcast_to([P, NE, RE]),
                                                     ALU.mult, ALU.mult).then_inc(s.scl, 1)
                            dve.wait_ge(s.base, t + 1)
                            dve.tensor_tensor(res[:, t % 2, :], ps[:, 4 + t % 2, :], bb[:], ALU.add).then_inc(s.bs, 1)
                            dve.wait_ge(s.bs, t + 1)
                            layernorm_stats(dve, res[:, t % 2, :], st3, mv3, t, s.st3, s.ag3, t + 1)
                            dve.wait_ge(s.ag3, t + 1)
                            dve.wait_ge(s.rs3, t + 1)
                            if t >= 2:
                                dve.wait_ge(s.fin, t - 1)
                            dve.tensor_scalar(up3[:, t % 2, :], res[:, t % 2, :], mv3[:, t, 0:1], rs3[:, t:t + 1],
                                              ALU.subtract, ALU.mult).then_inc(s.up3, 1)
            clear(nc, s)
        clear(nc, w)


_W = ["L0_attn_x", "w_qkv", "L0_attn_wo", "w_dense", "w_cent", "L0_ffn_bias", "L0_ffn_assignments", "w_in",
      "L1_attn_conv_w", "conv_b", "w_x", "norm_w", "w_dt", "L1_attn_A_log",
      "d_skip", "w_out", "w_gate_low", "w_base", "L1_ffn_base_b", "w_up",
      "rope", "ident", "masks", "cluster_ids", "expert_ids"]


def run(stage, nc, *args):
    with ExitStack() as ctx:
        stage(nc, ctx, *args)


def two_layers(nc, t, out):
    def scratch(name, shape):
        return nc.dram_tensor(name, shape, F32, kind="Internal").ap()

    att_o, att_l, inv_l = scratch("att_o", (H, HD, B * S)), scratch("att_l", (H, B * S)), scratch("inv_l", (H, B * S))
    x2 = scratch("x2_d", (NB, BLK, D))
    y = scratch("y_d", (NB, P, MT, BLK))
    bc = scratch("bc_d", (2 * NS, BLK))
    with ExitStack() as ctx:
        ps = ctx.enter_context(nc.psum_tensor("ps", [P, 8, 512], F32))
        run(attention_stage, nc, ps, t["L0_attn_x"], t["w_qkv"], t["rope"], t["ident"], t["masks"], att_o, att_l)
        run(softmax_sums_stage, nc, att_l, inv_l)
        keep = namedtuple("always", "ident")(ctx.enter_context(nc.sbuf_tensor("keep_ident", [P, P], F32)))
        k = semaphores(nc, ctx, "k", "ident")
        with nc.Block() as block:
            @block.sync
            def _(sp):
                sp.dma_start(keep.ident[:], t["ident"]).then_inc(k.ident, 16)
                sp.wait_ge(k.ident, 16)
        xnT = ctx.enter_context(nc.sbuf_tensor("scan_in", [P, KC, B * S], F32))
        with ExitStack() as mem:
            x1 = mem.enter_context(nc.sbuf_tensor("x1", [P, B * ST, D], F32))
            dense = mem.enter_context(nc.sbuf_tensor("dense", [P, B * ST, D], F32))
            found = namedtuple("found", "ident hits query_hit rows")(
                keep.ident,
                mem.enter_context(nc.sbuf_tensor("keep_hits", [P, NC], F32)),
                mem.enter_context(nc.sbuf_tensor("keep_query_hit", [P, B * ST], F32)),
                mem.enter_context(nc.sbuf_tensor("keep_rows", [P, D], F32)))
            run(dense_stage, nc, ps, found, x1, dense, t["L0_attn_x"], att_o, inv_l, t["L0_attn_wo"], t["w_dense"],
                t["w_cent"], t["L0_ffn_bias"])
            run(rows_stage, nc, ps, found, t["L0_ffn_assignments"], t["cluster_ids"])
            run(input_stage, nc, ps, found, x1, dense, xnT, x2)
        run(scan_stage, nc, ps, keep, xnT, t["w_in"], t["L1_attn_conv_w"], t["conv_b"], t["w_x"],
            t["norm_w"], t["w_dt"], t["L1_attn_A_log"], t["d_skip"], bc, y)
        run(out_stage, nc, ps, keep, x2, y, t["w_out"], t["w_gate_low"], t["w_base"], t["L1_ffn_base_b"], t["w_up"],
                  t["expert_ids"], out)


def rope_tables(np):
    inv = 1.0 / 10000.0 ** (np.arange(0, HD, 2)[:HD // 2].astype(np.float32) / HD)
    f = np.outer(np.arange(S), inv).astype(np.float32)
    d = np.arange(P) % HD
    sign = np.where(d % 2 == 0, np.float32(-1), np.float32(1))[:, None]
    return np.stack([np.cos(f).T[d // 2], np.sin(f).T[d // 2] * sign], 1).astype(np.float32)


def kernel(**inputs):
    import numpy as np
    import concourse.bacc as _bacc
    from concourse import mybir as _mybir
    from concourse.bass_utils import run_bass_kernel_spmd as _run

    t = {k: np.asarray(v) for k, v in inputs.items()}
    wqkv = np.stack([t["L0_attn_wq"], t["L0_attn_wk"], t["L0_attn_wv"]])
    t["w_qkv"] = wqkv.reshape(3, KC, P, 2, HC).transpose(3, 2, 0, 1, 4)
    t["w_dense"] = t["L0_ffn_weight"].T
    t["w_cent"] = t["L0_ffn_centroids"].T
    t["w_in"] = t["L1_attn_in_proj_w"].reshape(KC, P, 2 * MT, P).transpose(2, 1, 0, 3)
    t["w_x"] = t["L1_attn_x_proj_w"].T
    t["norm_w"] = np.concatenate([t["L1_attn_dt_ln_w"], t["L1_attn_B_ln_w"], t["L1_attn_C_ln_w"]])
    t["w_dt"] = np.concatenate([t["L1_attn_dt_proj_w"].T, t["L1_attn_dt_bias"][None]])
    for name, source in (("conv_b", "L1_attn_conv_b"), ("d_skip", "L1_attn_D_param")):
        t[name] = t[source].reshape(MT, P).T
    t["w_out"] = t["L1_attn_out_proj_w"].T
    t["w_gate_low"] = np.concatenate([t["L1_ffn_gate_w"].T, t["L1_ffn_lora_A"].reshape(NL, D).T], 1)
    t["w_base"] = t["L1_ffn_base_w"].T
    t["w_up"] = t["L1_ffn_lora_B"].transpose(0, 2, 1).reshape(NL, D)
    t["L0_attn_x"] = t["L0_attn_x"].reshape(NB, BLK, D)
    t["rope"] = rope_tables(np)
    t["ident"] = np.eye(P, dtype=np.float32)
    late = np.triu(np.full((P, P), -1e30, np.float32), 1)
    t["masks"] = np.stack([late, late.T], 1)
    t["cluster_ids"] = np.arange(NC, dtype=np.float32)[:, None]
    t["expert_ids"] = np.tile(np.arange(NE, dtype=np.float32), (P, 1))

    nc = _bacc.Bacc("TRN2", target_bir_lowering=False, num_devices=1)
    arrays, aps = {}, {}
    for name in _W:
        a = np.ascontiguousarray(t[name])
        arrays[f"in_{name}"] = a
        aps[name] = nc.dram_tensor(f"in_{name}", a.shape, _mybir.dt.from_np(a.dtype), kind="ExternalInput").ap()
    out = nc.dram_tensor("out_0", (NB, BLK, D), F32, kind="ExternalOutput").ap()
    two_layers(nc, aps, out)
    r = _run(nc, [arrays], core_ids=[0])
    return r.results[0]["out_0"].reshape(B, S, D)
```

```python
from collections import namedtuple
from contextlib import ExitStack

import concourse.bass as bass
from concourse import mybir

ALU = mybir.AluOpType
ACT = mybir.ActivationFunctionType
AX = mybir.AxisListType
F32 = mybir.dt.float32
BF16 = mybir.dt.bfloat16
I32 = mybir.dt.int32
ds = bass.ds

P = 128
D = 512
KC = D // P
B = 2
S = 1024
ST = S // P
BLK = 512
NB = B * S // BLK
TB = BLK // P
H = 32
HD = D // H
HH = H // 2
HC = HH * HD
QH = 4
NQ = HH // QH
GH = P // HD
NSPLIT = 6
OUTS = QH + 1
QK = NSPLIT * HD
Q_PARTS = (0, 0, 0, 1, 1, 2)
K_PARTS = (0, 1, 2, 0, 1, 0)
VW = 32
LN_EPS = 1e-5


def semaphores(nc, ctx, stage, names):
    return namedtuple(stage, names)(*(ctx.enter_context(nc.semaphore(f"{stage}_{name}")) for name in names.split()))


def clear(nc, sems):
    with nc.Block() as block:
        @block.sync
        def _(sp):
            for s in sems:
                sp.sem_clear(s)


SCORE_UNITS = [(j, h, k) for j, k in enumerate((1, 1, 1, 1, 2, 2, 4, 4)) for h in range(0, QH, k)]
VALUE_UNITS = [(j, half) for j in range(ST) for half in range(j // TB, 2)]
MAX_UNITS = [(i, p, h, k) for i, ks in enumerate(((4,), (2,), (1,), (1,), (1, 4), (1, 2), (1, 1), (1, 1)))
             for p, k in enumerate(ks) for h in range(0, QH, k)]
ORDER = "SMMSMSMMSMSMMSMWMMSSMWMMSSMMWMSMSMWMMSWMMSSMMWMSMSMWMSMMWSTSWMSMMWMSMWMWM"
EARLY = ORDER[ORDER.index("T"):].count("M")
NW = len(VALUE_UNITS)
NMAX = len(MAX_UNITS) + 1
NPROJ = 2 * 2 * 2 + ST
RD = NPROJ
RDQ = len(SCORE_UNITS) + 2
COPY_AFTER = (VALUE_UNITS.index((TB - 1, 0)), NW - 1)


def reads_behind():
    counts, n, w = [], 0, 0
    for what in ORDER:
        if what == "S":
            n += 1
            counts.append(n)
        elif what == "W":
            n += w in COPY_AFTER
            w += 1
    return counts


READS = reads_behind()
LAST_SCORE = [max(u for u, (j, h, k) in enumerate(SCORE_UNITS) if j == t) for t in range(ST)]


BESIDE = 12


def first_bank(n):
    if n < BESIDE:
        return 6 + n % 2, max(0, n - 1)
    banks = (6, 7, 2, 3, 4, 5)
    r = n - BESIDE
    return banks[r % 6], n - 5 if r >= 6 else n - 1 if r < 2 else 0


def max_width(i, p):
    return min(BLK, (i + 1) * P - BLK * p)


def score_at(j, x):
    return j * P if j < TB else x * (BLK if j < 6 else S - j * P)


def attention_stage(nc, ctx, ps, ident_f, x, w_qkv, rope, ident, masks, att_o, att_l):
    with ExitStack() as mem:
        def sb(name, shape, dt=F32):
            return mem.enter_context(nc.sbuf_tensor(name, shape, dt))

        ident_b = sb("ident_b", [P, P], BF16)
        mask_f = sb("mask_f", [P, 2, P])
        mask_b = sb("mask_b", [P, 2, P], BF16)
        cos_sin = sb("cos_sin", [P, 2, S])
        xnT = sb("xnT", [P, KC, S])
        w3 = sb("w3", [P, 3, KC, HC])
        q6 = sb("q6", [QK + 3, HH, S], BF16)
        k6 = sb("k6", [QK + 3, HH, S], BF16)
        vh = sb("vh", [P, ST, HH, VW])
        va = sb("va", [P, ST, QH * VW])
        probs = sb("probs", [P, 2, QH, S])
        o_sb = sb("o_sb", [P, S])
        ones3 = sb("ones3", [3, S], BF16)
        q_raw = sb("q_raw", [P, 2, BLK])
        q_swap = sb("q_swap", [P, 2, BLK])
        t_cos = sb("t_cos", [P, 2, BLK])
        t_sin = sb("t_sin", [P, 2, BLK])
        q_rot = sb("q_rot", [P, 2, BLK])
        q_rest = sb("q_rest", [P, 2, BLK])
        parts = sb("parts", [P, 2, 3, BLK], BF16)
        mx = sb("mx", [P, 2, QH, ST])
        nm = sb("nm", [P, QH, ST])
        m_rest = sb("m_rest", [QH * ST, P])
        m_parts = sb("m_parts", [QH * ST, NQ, 3, P], BF16)
        st6 = sb("st6", [P, ST, 6])
        mv = sb("mv", [P, ST, 2])
        lnv = sb("lnv", [P, ST])
        rstd = sb("rstd", [P, ST])
        xt = probs[:, 0, :, :].rearrange("p a (t d) -> p (a t) d", d=D)

        o_ps = ps[:, 0:2, :].rearrange("p a n -> p (a n)")
        st_ps = [ps[:, 2 + 2 * i:4 + 2 * i, :].rearrange("p a n -> p (a n)") for i in range(2)]
        mx_ps = [ps[:, 6 + i, :] for i in range(2)]

        scratch = nc.dram_tensor("split_parts", (2, 3, GH, HD, S), BF16, kind="Internal").ap()
        c = semaphores(nc, ctx, "ac", "const w ones ones_in")
        with nc.Block() as block:
            @block.sync
            def _(sp):
                sp.dma_start(ident_f[:], ident).then_inc(c.const, 16)
                sp.dma_start(mask_f[:], masks).then_inc(c.const, 16)
                sp.dma_start(cos_sin[:], rope).then_inc(c.const, 16)
                sp.dma_start(w3[:], w_qkv[0]).then_inc(c.w, 16)
                sp.wait_ge(c.ones, 1)
                sp.dma_start(k6[QK:QK + 3, :, :], ones3[:].unsqueeze(1).broadcast_to([3, HH, S])).then_inc(c.ones_in, 16)
                sp.wait_ge(c.const, 48)
                sp.wait_ge(c.ones_in, 16)
                sp.wait_ge(c.w, 16)

            @block.vector
            def _(dve):
                dve.memset(ones3[:], 1.0).then_inc(c.ones, 1)
                dve.wait_ge(c.const, 48)
                dve.tensor_copy(ident_b[:], ident_f[:])
                dve.tensor_copy(mask_b[:], mask_f[:])

            @block.gpsimd
            def _(pool):
                pool.memset(vh[:, :, :, HD:VW], 1.0)

            @block.scalar
            def _(act):
                act.preload_act_table_set("natural_log_exp_and_others")

        n = semaphores(nc, ctx, "an", "x0 x1 stats aggr lnv rstd xn tr ev")
        a = semaphores(nc, ctx, "aa", "w proj act_rd swap sin rot hi rest mid lo rep0 rep1 kept0 kept1 scores "
                 "max max_rd m_ready m_in m_chain m_split va pv out")
        with nc.Fori(0, B) as b:
            with nc.Block() as block:
                @block.sync
                def _(sp):
                    for g, s in enumerate((n.x0, n.x1)):
                        sp.dma_start(xt[:, TB * g:TB * g + TB, :],
                                     x[ds(b * 2 + g, 1), :, :].rearrange("a (t p) d -> p (a t) d", p=P)).then_inc(s, 16)

                @block.vector
                def _(dve):
                    def normalise(g):
                        dve.wait_ge(n.rstd, g + 1)
                        for t in range(TB * g, TB * g + TB):
                            dve.tensor_scalar(xt[:, t, :], xt[:, t, :], mv[:, t, 0:1], rstd[:, t:t + 1],
                                              ALU.subtract, ALU.mult).then_inc(n.xn, 1)

                    for g in range(2):
                        dve.wait_ge((n.x0, n.x1)[g], 16)
                        for t in range(TB * g, TB * g + TB):
                            dve.bn_stats(st6[:, t, :], xt[:, t, :]).then_inc(n.stats, 1)
                        for t in range(TB * g, TB * g + TB):
                            dve.wait_ge(n.stats, t + 1)
                            dve.bn_aggr(mv[:, t, :], st6[:, t, :]).then_inc(n.aggr, 1)
                        if g:
                            normalise(0)
                    normalise(1)

                @block.scalar
                def _(act):
                    for g in range(2):
                        four = slice(TB * g, TB * g + TB)
                        act.wait_ge(n.aggr, TB * (g + 1))
                        act.activation(lnv[:, four], mv[:, four, 1], ACT.Ln, bias=LN_EPS).then_inc(n.lnv, 1)
                        act.wait_ge(n.lnv, g + 1)
                        act.activation(rstd[:, four], lnv[:, four], ACT.Exp, scale=-0.5).then_inc(n.rstd, 1)
                    for t in range(ST):
                        act.wait_ge(n.tr, t + 1)
                        act.activation(xnT[:, :, t * P:t * P + P],
                                       ps[:, t % 4, :].rearrange("p (c n) -> p c n", c=KC), ACT.Copy).then_inc(n.ev, 1)

                @block.tensor
                def _(pe):
                    for t in range(ST):
                        pe.wait_ge(n.xn, t + 1)
                        if t >= 4:
                            pe.wait_ge(n.ev, t - 3)
                        for k in range(KC):
                            mm = pe.transpose(ps[:, t % 4, k * P:k * P + P], xt[:, t, k * P:k * P + P], ident_f[:])
                        mm.then_inc(n.tr, 1)

            with nc.Fori(0, 2) as hf:
                units = [(w, g, tb) for g in range(2) for w in (1, 0) for tb in range(2)]
                NU = len(units)
                rep, kept = (a.rep0, a.rep1), (a.kept0, a.kept1)

                with nc.Block() as block:
                    @block.sync
                    def _(sp):
                        for u, (w, g, tb) in enumerate(units):
                            pair = u // 2
                            sp.wait_ge(a.lo, u + 1)
                            if pair >= 2:
                                sp.wait_ge(rep[pair % 2], 16 * NSPLIT * (pair // 2))
                            sp.dma_start(scratch[pair % 2, :, :, :, tb * BLK:tb * BLK + BLK].rearrange("s h r t -> (h r) s t"),
                                         parts[:, tb, :, :]).then_inc(kept[tb], 16)
                            if tb == 0:
                                continue
                            for s in kept:
                                sp.wait_ge(s, 16 * (pair + 1))
                            for r, part in enumerate((Q_PARTS, K_PARTS)[w]):
                                sp.dma_start((q6, k6)[w][r * HD:r * HD + HD, g * GH:g * GH + GH, :],
                                             scratch[pair % 2, part].rearrange("h r t -> r h t")).then_inc(rep[pair % 2], 16)

                        def send_max(q):
                            sp.wait_ge(a.m_split, q + 1)
                            for r in range(3):
                                sp.dma_start(q6[QK + r:QK + r + 1, ds(q * QH, QH), :].rearrange("o h (i n) -> o (h i) n", n=P),
                                             m_parts[:, ds(q, 1), r, :]).then_inc(a.m_in, 16)

                        def send_out(q):
                            sp.wait_ge(a.act_rd, RD + RDQ * (q + 1))
                            for h in range(QH):
                                sp.dma_start(att_o[ds(hf * HH + q * QH + h, 1), :, ds(b * S, S)].rearrange("a r t -> (a r) t"),
                                             o_sb[VW * h:VW * h + HD, :]).then_inc(a.out, 16)
                            sp.dma_start(att_l[ds(hf * HH + q * QH, QH), ds(b * S, S)],
                                         o_sb[HD:P:VW, :]).then_inc(a.out, 16)

                        sp.wait_ge(a.proj, NPROJ)
                        sp.dma_start(w3[:], w_qkv[ds(1 - hf, 1), :, :, :, :].rearrange("a p w c n -> (a p) w c n")).then_inc(a.w, 16)
                        send_max(0)
                        with sp.Fori(0, NQ - 1) as q:
                            send_max(q + 1)
                            send_out(q)
                        send_out(NQ - 1)
                        sp.wait_ge(a.out, 16 * OUTS * NQ)
                        sp.wait_ge(a.w, 16)

                    @block.tensor
                    def _(pe):
                        for u, (w, g, tb) in enumerate(units):
                            if u >= 4:
                                pe.wait_ge(a.act_rd, u - 3)
                            for k in range(KC):
                                mm = pe.matmul(ps[:, 2 + u % 4, :], w3[:, w, k, g * P:g * P + P],
                                               xnT[:, k, tb * BLK:tb * BLK + BLK], start=(k == 0), stop=(k == KC - 1))
                            mm.then_inc(a.proj, 1)

                        def values(t):
                            u = NU + t
                            pe.wait_ge(a.act_rd, u - 3)
                            for k in range(KC):
                                mm = pe.matmul(ps[:, 2 + u % 4, 0:HC], xnT[:, k, t * P:t * P + P], w3[:, 2, k, :],
                                               start=(k == 0), stop=(k == KC - 1))
                            mm.then_inc(a.proj, 1)

                        def max_unit(q, n):
                            i, p, h, heads = MAX_UNITS[n]
                            w = max_width(i, p)
                            bank = mx_ps[n % 2]
                            if isinstance(q, int) and q == 0:
                                b, read = first_bank(n)
                                bank = ps[:, b, :]
                                if n >= BESIDE:
                                    pe.wait_ge(a.act_rd, RD)
                                if read:
                                    pe.wait_ge(a.max_rd, read)
                            elif n >= 2:
                                pe.wait_ge(a.max_rd, q * NMAX + n - 1)
                            else:
                                pe.wait_ge(a.max_rd, q * NMAX)
                            diag = BLK * p + w == (i + 1) * P
                            for x in range(heads):
                                mm = pe.matmul(bank[:, x * w:x * w + w], q6[0:QK, ds(q * QH + (h + x), 1), i * P:i * P + P],
                                               k6[0:QK, ds(q * QH + (h + x), 1), BLK * p:BLK * p + w], start=True, stop=not diag)
                                if diag:
                                    mm = pe.matmul(bank[:, x * w + w - P:x * w + w], ident_b[:], mask_b[:, 0, :],
                                                   start=False, stop=True)
                            mm.then_inc(a.max, 1)

                        def max_turn(q):
                            pe.wait_ge(a.m_ready, q + 1)
                            pe.wait_ge(a.max_rd, q * NMAX + NMAX - 1)
                            pe.transpose(mx_ps[0][0:QH * ST, 0:P], nm[:].rearrange("p h i -> p (h i)"),
                                         ident_f[:]).then_inc(a.max, 1)

                        def scores(q, u):
                            j, h, heads = SCORE_UNITS[u]
                            slot = st_ps[u % 2]
                            if u >= 2:
                                pe.wait_ge(a.act_rd, q * RDQ + RD + READS[u - 2])
                            elif not (isinstance(q, int) and q == 0):
                                pe.wait_ge(a.act_rd, q * RDQ + RD - RDQ + READS[u - 2])
                            for x in range(heads):
                                for lo, hi in ((j * P, BLK), (BLK, S)) if j < TB else ((j * P, S),):
                                    at = score_at(j, x) + lo - j * P
                                    diag = lo == j * P
                                    mm = pe.matmul(slot[:, at:at + hi - lo], k6[:, ds(q * QH + (h + x), 1), j * P:j * P + P],
                                                   q6[:, ds(q * QH + (h + x), 1), lo:hi], start=True, stop=not diag)
                                    if diag:
                                        mm = pe.matmul(slot[:, at:at + P], ident_b[:], mask_b[:, 1, :], start=False, stop=True)
                            mm.then_inc(a.scores, 1)

                        def weigh(q, n):
                            j, half = VALUE_UNITS[n]
                            pe.wait_ge(a.act_rd, q * RDQ + RD + READS[LAST_SCORE[j]])
                            if n == 0:
                                pe.wait_ge(a.va, q + 1)
                            lo, hi = max(BLK * half, j * P), BLK * half + BLK
                            for h in range(QH):
                                mm = pe.matmul(o_ps[VW * h:VW * h + VW, lo:hi], va[:, j, VW * h:VW * h + VW],
                                               probs[:, j % 2, h, lo:hi], start=(j == 0), stop=(n in COPY_AFTER))
                            mm.then_inc(a.pv, 1)

                        def quad(q, ahead):
                            s, w, m, turned = 0, 0, EARLY, 0
                            pe.wait_ge(a.m_in, q * 48 + 48)
                            for what in ORDER:
                                if what == "S":
                                    scores(q, s)
                                    s += 1
                                elif what == "W":
                                    weigh(q, w)
                                    w += 1
                                elif turned < ahead:
                                    if what == "M":
                                        max_unit(q + 1 + turned, m)
                                        m += 1
                                    else:
                                        max_turn(q + 1)
                                        m, turned = 0, 1

                        for t in range(TB):
                            values(t)
                        for s in rep:
                            pe.wait_ge(s, 16 * NSPLIT)
                        for m in range(len(MAX_UNITS)):
                            if m < BESIDE and m % (BESIDE // TB) == 0:
                                values(TB + m // (BESIDE // TB))
                            max_unit(0, m)
                        max_turn(0)
                        for m in range(EARLY):
                            max_unit(1, m)
                        for s in rep:
                            pe.wait_ge(s, 16 * NSPLIT * 2)
                        pe.wait_ge(a.act_rd, RD)
                        with pe.Fori(0, NQ - 2) as q:
                            quad(q, 2)
                        quad(NQ - 2, 1)
                        quad(NQ - 1, 0)

                    @block.scalar
                    def _(act):
                        def take(u):
                            act.wait_ge(a.proj, u + 1)
                            if u < NU:
                                if u >= 2:
                                    act.wait_ge(a.swap, u - 1)
                                act.activation(q_raw[:, u % 2, :], ps[:, 2 + u % 4, :], ACT.Copy,
                                               scale=HD ** -0.5 if units[u][0] == 0 else 1.0).then_inc(a.act_rd, 1)
                            else:
                                act.activation(vh[:, u - NU, :, 0:HD],
                                               ps[:, 2 + u % 4, 0:HC].rearrange("p (h d) -> p h d", d=HD),
                                               ACT.Copy).then_inc(a.act_rd, 1)

                        take(0)
                        for u in range(NU):
                            take(u + 1)
                            act.wait_ge(a.rot, u + 1)
                            if u >= 2:
                                act.wait_ge(kept[u % 2], 16 * (u // 2))
                            act.activation(parts[:, u % 2, 0, :], q_rot[:, u % 2, :], ACT.Copy).then_inc(a.hi, 1)
                            act.wait_ge(a.rest, u + 1)
                            act.activation(parts[:, u % 2, 1, :], q_rest[:, u % 2, :], ACT.Copy).then_inc(a.mid, 1)
                        for u in range(NU + 1, NPROJ):
                            take(u)

                        def exps(q, u):
                            first = isinstance(q, int) and q == 0
                            j, h, heads = SCORE_UNITS[u]
                            w = S - j * P
                            if j >= 2:
                                act.wait_ge(a.pv, q * NW + VALUE_UNITS.index((j - 2, 1)) + 1)
                            elif not first:
                                act.wait_ge(a.pv, q * NW + j - 1)
                            act.wait_ge(a.scores, q * len(SCORE_UNITS) + u + 1)
                            if heads == 1:
                                out, scored = probs[:, j % 2, h, j * P:S], st_ps[u % 2][:, j * P:S]
                            else:
                                out = probs[:, j % 2, h:h + heads, j * P:S]
                                if j < 6:
                                    scored = st_ps[u % 2].rearrange("p (x n) -> p x n", x=2)[:, :, 0:w]
                                else:
                                    scored = st_ps[u % 2][:, 0:heads * w].rearrange("p (x n) -> p x n", x=heads)
                            act.activation(out, scored, ACT.Exp).then_inc(a.act_rd, 1)

                        def quad(q):
                            first = isinstance(q, int) and q == 0
                            s, w = 0, 0
                            for what in ORDER:
                                if what == "S":
                                    exps(q, s)
                                    s += 1
                                elif what == "W":
                                    if w in COPY_AFTER:
                                        half = COPY_AFTER.index(w)
                                        act.wait_ge(a.pv, q * NW + w + 1)
                                        if half == 0 and not first:
                                            act.wait_ge(a.out, q * (16 * OUTS))
                                        act.activation(o_sb[:, BLK * half:BLK * half + BLK], o_ps[:, BLK * half:BLK * half + BLK],
                                                       ACT.Copy).then_inc(a.act_rd, 1)
                                    w += 1

                        quad(0)
                        with act.Fori(1, NQ) as q:
                            quad(q)

                    @block.vector
                    def _(dve):
                        swap = [p ^ 1 for p in range(32)]

                        def turn(u):
                            tb = units[u][2]
                            dve.wait_ge(a.act_rd, u + 1)
                            if u >= 2:
                                dve.wait_ge(a.sin, u - 1)
                            dve.tensor_tensor(t_cos[:, u % 2, :], q_raw[:, u % 2, :], cos_sin[:, 0, tb * BLK:tb * BLK + BLK],
                                              ALU.mult)
                            dve.stream_shuffle(q_swap[:, u % 2, :], q_raw[:, u % 2, :], swap).then_inc(a.swap, 1)

                        turn(0)
                        for u in range(NU):
                            dve.wait_ge(a.sin, u + 1)
                            dve.wait_ge(a.swap, u + 1)
                            if u >= 2:
                                dve.wait_ge(a.hi, u - 1)
                            dve.tensor_tensor(q_rot[:, u % 2, :], t_cos[:, u % 2, :], t_sin[:, u % 2, :], ALU.add).then_inc(a.rot, 1)
                            if u + 1 < NU:
                                turn(u + 1)
                            dve.wait_ge(a.hi, u + 1)
                            if u >= 2:
                                dve.wait_ge(a.lo, u - 1)
                            dve.tensor_tensor(q_rest[:, u % 2, :], q_rot[:, u % 2, :], parts[:, u % 2, 0, :],
                                              ALU.subtract).then_inc(a.rest, 1)
                            dve.wait_ge(a.mid, u + 1)
                            dve.tensor_tensor(parts[:, u % 2, 2, :], q_rest[:, u % 2, :], parts[:, u % 2, 1, :],
                                              ALU.subtract).then_inc(a.lo, 1)

                        def maxima(q):
                            for n, (i, p, h, heads) in enumerate(MAX_UNITS):
                                w = max_width(i, p)
                                out = nm[:, h:h + heads, i:i + 1] if i < TB else mx[:, p, h:h + heads, i:i + 1]
                                dve.wait_ge(a.max, q * NMAX + n + 1)
                                if n == 0 and not (isinstance(q, int) and q == 0):
                                    dve.wait_ge(a.m_ready, q)
                                bank = ps[:, first_bank(n)[0], :] if isinstance(q, int) and q == 0 else mx_ps[n % 2]
                                dve.tensor_reduce(out, bank[:, 0:heads * w].rearrange("p (x n) -> p x n", x=heads),
                                                  AX.X, ALU.max, negate=True).then_inc(a.max_rd, 1)
                            dve.wait_ge(a.max_rd, q * NMAX + NMAX - 1)
                            dve.tensor_tensor(nm[:, :, 4:ST], mx[:, 0, :, 4:ST],
                                              mx[:, 1, :, 4:ST], ALU.min).then_inc(a.m_ready, 1)
                            turned = mx_ps[0][0:QH * ST, 0:P]
                            hi, mid, lo = (m_parts[:, ds(q, 1), r, :].rearrange("p a n -> p (a n)") for r in range(3))
                            dve.wait_ge(a.max, q * NMAX + NMAX)
                            dve.tensor_copy(hi, turned).then_inc(a.m_chain, 1)
                            dve.wait_ge(a.m_chain, q * 2 + 1)
                            dve.tensor_tensor(m_rest[:], turned, hi, ALU.subtract).then_inc(a.max_rd, 1)
                            dve.wait_ge(a.max_rd, q * NMAX + NMAX)
                            dve.tensor_copy(mid, m_rest[:]).then_inc(a.m_chain, 1)
                            dve.wait_ge(a.m_chain, q * 2 + 2)
                            dve.tensor_tensor(lo, m_rest[:], mid, ALU.subtract).then_inc(a.m_split, 1)

                        maxima(0)
                        with dve.Fori(1, NQ) as q:
                            maxima(q)

                    @block.gpsimd
                    def _(pool):
                        for u, (w, g, tb) in enumerate(units):
                            pool.wait_ge(a.swap, u + 1)
                            if u >= 2:
                                pool.wait_ge(a.rot, u - 1)
                            pool.tensor_tensor(t_sin[:, u % 2, :], q_swap[:, u % 2, :], cos_sin[:, 1, tb * BLK:tb * BLK + BLK],
                                               ALU.mult).then_inc(a.sin, 1)

                        def values(q):
                            pool.tensor_copy(va[:].rearrange("p j n -> p j n"),
                                             vh[:, :, ds(q * QH, QH), :].rearrange("p j h v -> p j (h v)")).then_inc(a.va, 1)

                        pool.wait_ge(a.act_rd, NPROJ)
                        values(0)
                        with pool.Fori(1, NQ) as q:
                            pool.wait_ge(a.pv, q * NW)
                            values(q)

                clear(nc, a)
            clear(nc, n)
        clear(nc, c)


def layernorm_tail(act, mv, lnv, rstd, t, aggr, lnv_done, rstd_done, n):
    act.wait_ge(aggr, n)
    act.activation(lnv[:, t:t + 1], mv[:, t, 1:2], ACT.Ln, bias=LN_EPS).then_inc(lnv_done, 1)
    act.wait_ge(lnv_done, n)
    act.activation(rstd[:, t:t + 1], lnv[:, t:t + 1], ACT.Exp, scale=-0.5).then_inc(rstd_done, 1)


def layernorm_stats(dve, src, st6, mv, t, stats, aggr, n):
    dve.bn_stats(st6[:, t, :], src).then_inc(stats, 1)
    dve.wait_ge(stats, n)
    dve.bn_aggr(mv[:, t, :], st6[:, t, :]).then_inc(aggr, 1)


NC = 64
HIT = 0.01
TEMPERATURE = 0.1


def dense_stage(nc, ctx, ps, keep, x1, dn, x, att_o, att_l, wo, w_dense, w_cent, bias,
                assignments, cluster_ids, later):
    s = semaphores(nc, ctx, "d", "wo w o0 o1 l0 l1 x0 x1 lnl inv div y st1 ag1 ln1 rs1 up add st2 ag2 ln2 rs2 xn tr ev "
                   "dn lg dn_rd top nb exp tot hit hits query later ids ones numbers one_hot count sel spread rows row_mask")
    o_load, l_load, x_load = (s.o0, s.o1), (s.l0, s.l1), (s.x0, s.x1)
    T = B * ST
    with ExitStack() as mem:
        def sb(name, shape, dt=F32):
            return mem.enter_context(nc.sbuf_tensor(name, shape, dt))

        wo_sb = sb("wo_sb", [P, KC, D])
        wd_sb = sb("wd_sb", [P, KC, D])
        wc_sb = sb("wc_sb", [P, KC, NC])
        bias_sb = sb("bias_sb", [P, D])
        oT = sb("oT", [P, 2, KC, BLK])
        lT = sb("lT", [P, 2, KC, BLK])
        x_sb = sb("x_sb", [P, 2 * TB, D])
        up = sb("up", [P, 2, D])
        xn = sb("xn", [P, 2, D])
        xnT = sb("d_xnT", [P, 4, KC, P])
        st1, mv1, ln1, rs1 = sb("st1", [P, T, 6]), sb("mv1", [P, T, 2]), sb("ln1", [P, T]), sb("rs1", [P, T])
        st2, mv2, ln2, rs2 = sb("st2", [P, T, 6]), sb("mv2", [P, T, 2]), sb("ln2", [P, T]), sb("rs2", [P, T])
        top, nb = sb("top", [P, T]), sb("nb", [P, T])
        ex, tot, inv = sb("ex", [P, 2, NC]), sb("tot", [P, T]), sb("d_inv", [P, T])
        hit = sb("hit", [P, 2, NC])
        ids = sb("ids", [NC, 1])
        assigned, numbers, one_hot = sb("assigned", [NC, D], I32), sb("numbers", [NC, D]), sb("one_hot", [NC, D])
        ones, chosen, chosen_b = sb("ones", [P, P]), sb("chosen", [NC, 1]), sb("chosen_b", [NC, P])

        with nc.Block() as block:
            @block.sync
            def _(sp):
                def load_block(g):
                    if g >= 2:
                        sp.wait_ge(s.y, TB * (g - 1))
                    for c in range(KC):
                        sp.dma_start(oT[:, g % 2, c, :], att_o[GH * c:GH * c + GH, :, g * BLK:g * BLK + BLK]
                                     .rearrange("h r t -> (h r) t")).then_inc(o_load[g % 2], 16)
                        sp.dma_start(lT[:, g % 2, c, :], att_l[GH * c:GH * c + GH, g * BLK:g * BLK + BLK].unsqueeze(1)
                                     .broadcast_to([GH, HD, BLK])).then_inc(l_load[g % 2], 16)
                    if g >= 2:
                        sp.wait_ge(s.add, TB * (g - 1))
                    sp.dma_start(x_sb[:, g % 2 * TB:g % 2 * TB + TB, :],
                                 x[g].rearrange("(t p) d -> p t d", p=P)).then_inc(x_load[g % 2], 16)

                sp.dma_start(wo_sb[:], wo.rearrange("(c p) n -> p c n", p=P)).then_inc(s.wo, 16)
                load_block(0)
                for dst, src in ((wd_sb, w_dense), (wc_sb, w_cent)):
                    sp.dma_start(dst[:], src.rearrange("(c p) n -> p c n", p=P)).then_inc(s.w, 16)
                sp.dma_start(bias_sb[:], bias.rearrange("(a n) -> a n", a=1).broadcast_to([P, D])).then_inc(s.w, 16)
                for g in range(1, NB):
                    load_block(g)
                sp.dma_start(ids[:], cluster_ids).then_inc(s.ids, 16)
                sp.dma_start(assigned[:], assignments.rearrange("(a n) -> a n", a=1).broadcast_to([NC, D])).then_inc(s.ids, 16)
                for dst, src in later:
                    sp.dma_start(dst, src).then_inc(s.later, 16)
                sp.wait_ge(s.later, 16 * len(later))

            @block.tensor
            def _(pe):
                pe.wait_ge(s.wo, 16)
                for i in range(T + 3):
                    if i < T:
                        if i % TB == 0:
                            pe.wait_ge(s.div, KC * (i // TB + 1))
                        if i >= 2:
                            pe.wait_ge(s.up, i - 1)
                        for k in range(KC):
                            mm = pe.matmul(ps[:, i % 2, :], oT[:, i // TB % 2, k, i % TB * P:i % TB * P + P], wo_sb[:, k, :],
                                           start=(k == 0), stop=(k == KC - 1))
                        mm.then_inc(s.y, 1)
                    t = i - 2
                    if 0 <= t < T:
                        pe.wait_ge(s.xn, t + 1)
                        if t >= 2:
                            pe.wait_ge(s.ev, t - 1)
                        for k in range(KC):
                            mm = pe.transpose(ps[:, 2 + t % 2, k * P:k * P + P], xn[:, t % 2, k * P:k * P + P], keep.ident[:])
                        mm.then_inc(s.tr, 1)
                    t = i - 3
                    if 0 <= t < T:
                        if t == 0:
                            pe.wait_ge(s.w, 48)
                        pe.wait_ge(s.ev, t + 1)
                        if t >= 2:
                            pe.wait_ge(s.exp, t - 1)
                        for k in range(KC):
                            mm = pe.matmul(ps[:, 6 + t % 2, 0:NC], xnT[:, t % 4, k, :], wc_sb[:, k, :],
                                           start=(k == 0), stop=(k == KC - 1))
                        mm.then_inc(s.lg, 1)
                        if t >= 2:
                            pe.wait_ge(s.dn_rd, t - 1)
                        for k in range(KC):
                            mm = pe.matmul(ps[:, 4 + t % 2, :], xnT[:, t % 4, k, :], wd_sb[:, k, :],
                                           start=(k == 0), stop=(k == KC - 1))
                        mm.then_inc(s.dn, 1)
                pe.wait_ge(s.hits, T + 1)
                pe.matmul(ps[0:NC, 0, 0:1], keep.hits[:], ones[:, 0:1], start=True, stop=True).then_inc(s.count, 1)
                pe.wait_ge(s.one_hot, 1)
                pe.wait_ge(s.spread, 1)
                pe.matmul(ps[:, 1, :], chosen_b[:], one_hot[:], start=True, stop=True).then_inc(s.rows, 1)

            @block.scalar
            def _(act):
                def invert(g):
                    act.wait_ge(l_load[g % 2], 16 * KC * (g // 2 + 1))
                    for c in range(KC):
                        act.activation(lT[:, g % 2, c, :], lT[:, g % 2, c, :], ACT.Ln).then_inc(s.lnl, 1)
                    for c in range(KC):
                        act.wait_ge(s.lnl, KC * g + c + 1)
                        act.activation(lT[:, g % 2, c, :], lT[:, g % 2, c, :], ACT.Exp, scale=-1.0).then_inc(s.inv, 1)

                act.preload_act_table_set("natural_log_exp_and_others")
                invert(0)
                for i in range(T + 4):
                    if i % TB == 1 and i // TB + 1 < NB:
                        invert(i // TB + 1)
                    if i < T:
                        layernorm_tail(act, mv1, ln1, rs1, i, s.ag1, s.ln1, s.rs1, i + 1)
                    t = i - 4
                    if 0 <= t < T:
                        act.wait_ge(s.nb, t + 1)
                        if t >= 2:
                            act.wait_ge(s.hit, t - 1)
                        act.activation(ex[:, t % 2, :], ps[:, 6 + t % 2, 0:NC], ACT.Exp, bias=nb[:, t:t + 1],
                                       scale=1.0 / TEMPERATURE, accum_out=tot[:, t:t + 1]).then_inc(s.exp, 1)
                    if i < T:
                        layernorm_tail(act, mv2, ln2, rs2, i, s.ag2, s.ln2, s.rs2, i + 1)
                    t = i - 2
                    if 0 <= t < T:
                        act.wait_ge(s.tr, t + 1)
                        if t >= 4:
                            act.wait_ge(s.dn, t - 3)
                        act.activation(xnT[:, t % 4, :, :].rearrange("p c n -> p (c n)"), ps[:, 2 + t % 2, :],
                                       ACT.Copy).then_inc(s.ev, 1)

            @block.gpsimd
            def _(pool):
                for t in range(T):
                    if t % TB == 0:
                        pool.wait_ge(x_load[t // TB % 2], 16 * (t // TB // 2 + 1))
                    pool.wait_ge(s.up, t + 1)
                    pool.tensor_tensor(x1[:, t, :], x_sb[:, t % (2 * TB), :], up[:, t % 2, :], ALU.add).then_inc(s.add, 1)

            @block.vector
            def _(dve):
                def divide(g):
                    dve.wait_ge(o_load[g % 2], 16 * KC * (g // 2 + 1))
                    for c in range(KC):
                        dve.wait_ge(s.inv, KC * g + c + 1)
                        dve.tensor_tensor(oT[:, g % 2, c, :], oT[:, g % 2, c, :], lT[:, g % 2, c, :], ALU.mult).then_inc(s.div, 1)

                dve.memset(keep.hits[:], 0.0).then_inc(s.hits, 1)
                dve.memset(ones[:], 1.0).then_inc(s.ones, 1)
                divide(0)
                for i in range(T + 4):
                    t = i - 4
                    if i % TB == 2 and i // TB + 1 < NB:
                        divide(i // TB + 1)
                    if 0 <= t < T:
                        dve.wait_ge(s.lg, t + 1)
                        dve.tensor_reduce(top[:, t:t + 1], ps[:, 6 + t % 2, 0:NC], AX.X, ALU.max).then_inc(s.top, 1)
                    if i < T:
                        dve.wait_ge(s.y, i + 1)
                        layernorm_stats(dve, ps[:, i % 2, :], st1, mv1, i, s.st1, s.ag1, i + 1)
                    if 0 <= t < T:
                        dve.wait_ge(s.top, t + 1)
                        dve.tensor_scalar(nb[:, t:t + 1], top[:, t:t + 1], -1.0 / TEMPERATURE, None,
                                          ALU.mult).then_inc(s.nb, 1)
                        dve.wait_ge(s.dn, t + 1)
                        dve.tensor_tensor(dn[:, t, :], ps[:, 4 + t % 2, :], bias_sb[:], ALU.add).then_inc(s.dn_rd, 1)
                    if i < T:
                        dve.wait_ge(s.ag1, i + 1)
                        dve.wait_ge(s.rs1, i + 1)
                        if i >= 2:
                            dve.wait_ge(s.add, i - 1)
                        dve.tensor_scalar(up[:, i % 2, :], ps[:, i % 2, :], mv1[:, i, 0:1], rs1[:, i:i + 1],
                                          ALU.subtract, ALU.mult).then_inc(s.up, 1)
                    if 0 <= t < T:
                        dve.wait_ge(s.exp, t + 1)
                        dve.reciprocal(inv[:, t:t + 1], tot[:, t:t + 1]).then_inc(s.tot, 1)
                        dve.wait_ge(s.tot, t + 1)
                        if t >= 2:
                            dve.wait_ge(s.hits, t)
                            dve.wait_ge(s.query, t - 1)
                        dve.tensor_scalar(hit[:, t % 2, :], ex[:, t % 2, :], inv[:, t:t + 1], HIT,
                                          ALU.mult, ALU.is_gt).then_inc(s.hit, 1)
                        dve.wait_ge(s.hit, t + 1)
                        dve.tensor_reduce(keep.query_hit[:, t:t + 1], hit[:, t % 2, :], AX.X, ALU.max).then_inc(s.query, 1)
                        dve.wait_ge(s.hits, t + 1)
                        dve.tensor_tensor(keep.hits[:], keep.hits[:], hit[:, t % 2, :], ALU.max).then_inc(s.hits, 1)
                    if i < T:
                        dve.wait_ge(s.add, i + 1)
                        layernorm_stats(dve, x1[:, i, :], st2, mv2, i, s.st2, s.ag2, i + 1)
                        dve.wait_ge(s.ag2, i + 1)
                        dve.wait_ge(s.rs2, i + 1)
                        if i >= 2:
                            dve.wait_ge(s.tr, i - 1)
                        dve.tensor_scalar(xn[:, i % 2, :], x1[:, i, :], mv2[:, i, 0:1], rs2[:, i:i + 1],
                                          ALU.subtract, ALU.mult).then_inc(s.xn, 1)
                dve.wait_ge(s.ids, 32)
                dve.tensor_copy(numbers[:], assigned[:]).then_inc(s.numbers, 1)
                dve.wait_ge(s.numbers, 1)
                dve.tensor_scalar(one_hot[:], numbers[:], ids[:, 0:1], None, ALU.is_equal).then_inc(s.one_hot, 1)
                dve.wait_ge(s.count, 1)
                dve.tensor_scalar(chosen[:], ps[0:NC, 0, 0:1], 0.0, None, ALU.is_gt).then_inc(s.sel, 1)
                dve.wait_ge(s.sel, 1)
                dve.tensor_scalar(chosen_b[:], ones[0:NC, :], chosen[:, 0:1], None, ALU.mult).then_inc(s.spread, 1)
                dve.wait_ge(s.rows, 1)
                dve.tensor_copy(keep.rows[:], ps[:, 1, :]).then_inc(s.row_mask, 1)
        clear(nc, s)


DI = 1024
MT = DI // P
NS = 16
RK = 32
CONV = 4
NX = RK + 2 * NS
RMS_EPS = 1e-6
ROWS_AT_ONCE = 4
NBC = 2 * NS // ROWS_AT_ONCE
X2_LAG = 5
RING = 4
SPB = S // BLK


def tile(t, m):
    return t[:, m, :] if isinstance(m, int) else t[:, ds(m, 1), :].rearrange("p a n -> p (a n)")


def col(t, m, n=None):
    if n is not None:
        return tile(t, m)[:, n:n + 1]
    return t[:, m:m + 1] if isinstance(m, int) else t[:, ds(m, 1)]


def scan_weights(nc, ctx, t):
    def sb(name, shape, dt=F32):
        return ctx.enter_context(nc.sbuf_tensor(name, shape, dt))

    w = namedtuple("weights", "cw cb xw nw mean dtw na dp")(
        sb("cw", [P, MT, CONV]), sb("cb", [P, MT]), sb("xw", [P, MT, NX]), sb("nw", [NX, 1]), sb("mean", [NX, NX]),
        sb("dtw", [RK + 1, DI]), sb("na", [P, MT, NS]), sb("dp", [P, MT]))
    return w, ((w.cw[:], t["L1_attn_conv_w"].rearrange("(m p) k -> p m k", p=P)),
               (w.cb[:], t["conv_b"]),
               (w.xw[:], t["w_x"].rearrange("(m p) n -> p m n", p=P)),
               (w.nw[:], t["norm_w"]),
               (w.mean[:], t["mean"]),
               (w.dtw[:], t["w_dt"]),
               (w.na[:], t["L1_attn_A_log"].rearrange("(m p) n -> p m n", p=P)),
               (w.dp[:], t["d_skip"]))


def scan_stage(nc, ctx, ps, keep, work, xnT, weights_in, w_in, bc, x2_out, y_out):
    r = semaphores(nc, ctx, "r", "a neg dt_ones")
    i1 = semaphores(nc, ctx, "n", "masked st1 ag1 ln1 rs1 up x2 st2 ag2 ln2 rs2 xn tr ev store")
    s = semaphores(nc, ctx, "m", "wx0 wx1 wz0 wz1 px padded head tap conv xc pz zs xw_sel xp sq mean lnx rsx "
                   "dt_in bc_sb bc_out dtm dt_sel skip_sel ab ex lg dts u skip da dbx h carry hc ys gate y0 y1")
    bc_load = [ctx.enter_context(nc.semaphore(f"m_bc{i}")) for i in range(NBC)]
    wx, wz, y_store = (s.wx0, s.wx1), (s.wz0, s.wz1), (s.y0, s.y1)
    PY, PX, PZ, PDT, PXP, PMEAN = 0, (2, 7), 3, 4, 5, 6
    with ExitStack() as mem:
        def sb(name, shape, dt=F32):
            return mem.enter_context(nc.sbuf_tensor(name, shape, dt))

        cw, cb, xw, nw, mean, dtw, na, dp = weights_in
        skip = sb("skip", [P, 2, P])
        dtm_w = sb("dtm_w", [RK + 1, 2, P])
        conv_carry = sb("conv_carry", [P, MT, CONV - 1])
        state = sb("state", [P, MT, NS])
        x2 = work[:, 0:B * ST, :]
        dn = work[:, B * ST:2 * B * ST, :]
        bcb = work
        xc = sb("xc", [P, MT, BLK])
        sz = sb("sz", [P, MT, BLK])
        dts = sb("dts", [P, 2, BLK])
        u = sb("u", [P, 2, BLK])
        soft = keep.rows
        wxr = sb("wxr", [P, 2, KC, P])
        wzr = sb("wzr", [P, 2, KC, P])
        pad = sb("pad", [P, 2, BLK + CONV - 1])
        acc = sb("acc", [P, 2, BLK])
        xw_one = sb("xw_one", [P, 2, P])
        dtT = sb("dtT", [RK + 1, BLK])
        bcT = sb("bcT", [NX, BLK])
        da = sb("da", [P, RING, BLK])
        dbx = sb("dbx", [P, RING, BLK])
        hs = sb("hs", [P, RING, BLK])
        hc = sb("hc", [P, RING, BLK])
        yo = sb("yo", [P, 2, BLK])
        T2 = B * ST
        st1, mv1, ln1, rs1 = sb("n_st1", [P, T2, 6]), sb("n_mv1", [P, T2, 2]), sb("n_ln1", [P, T2]), sb("n_rs1", [P, T2])
        st2, mv2, ln2, rs2 = sb("n_st2", [P, T2, 6]), sb("n_mv2", [P, T2, 2]), sb("n_ln2", [P, T2]), sb("n_rs2", [P, T2])
        up, xn = da[:, 0:2, :], dbx[:, 0:2, :]

        def turns(eng, k, turn):
            apart = 3 if k == 0 else 1
            for m in range(apart):
                turn(k, m, m % 2)
            with eng.Fori(0, (MT - 1 - apart) // 2) as i:
                for step in range(2):
                    turn(k, i * 2 + (apart + step), (apart + step) % 2)
            turn(k, MT - 1, 1)

        def start(x2_tile, turn):
            m = 0
            for i in range(T2 + X2_LAG):
                x2_tile(i)
                if i >= TB + X2_LAG - 1 and (i - TB - X2_LAG + 1) % 2 == 0:
                    turn(-1, m, m % 2)
                    m += 1
            for m in range(m, MT):
                turn(-1, m, m % 2)

        def kind(k, m):
            first, last = isinstance(m, int) and m == 0, isinstance(m, int) and m == MT - 1
            return k >= 0, k < NB - 1, (k >= 0 if first else k < NB - 1), first, last

        with nc.Block() as block:
            @block.sync
            def _(sp):
                def load(k, m, par):
                    T = k * MT + m
                    _, px, pz, first, _ = kind(k, m)
                    if px:
                        if from_on(T + MT, 2):
                            sp.wait_ge(s.px, T + MT - 1)
                        sp.dma_start(wxr[:, par, :, :], weight_tile(m)).then_inc(wx[par], 16)
                    if pz:
                        if from_on(T + MT - 1, 2):
                            sp.wait_ge(s.pz, T + MT - 2)
                        sp.dma_start(wzr[:, 1 - par, :, :], weight_tile(2 * MT - 1 if first else m + (MT - 1))).then_inc(wz[1 - par], 16)

                def weight_tile(i):
                    return w_in[i] if isinstance(i, int) else w_in[ds(i, 1), :, :, :].rearrange("a p c n -> (a p) c n")

                def turn(k, m, par):
                    scans, px, _, first, last = kind(k, m)
                    if last and px:
                        load(k + 1, 0, 0)
                    elif not last:
                        load(k, m + 1, 1 - par)
                    if scans and from_on(k * MT + m, 1):
                        store(k, m, par)
                    if last and px:
                        broadcast(k + 1)

                def store(k, m, par):
                    first = isinstance(m, int) and m == 0
                    sp.wait_ge(s.gate, k * MT + m)
                    kb, mb = (k - 1, MT - 1) if first else (k, m - 1)
                    dst = y_out[kb, :, mb, :] if isinstance(mb, int) else y_out[kb, :, ds(mb, 1), :].rearrange("p a n -> p (a n)")
                    sp.dma_start(dst, yo[:, 1 - par, :]).then_inc(y_store[1 - par], 16)

                def broadcast(j):
                    sp.wait_ge(s.bc_sb, j + 1)
                    if j == 0:
                        sp.wait_ge(i1.store, 16 * NB)
                    if j:
                        for q in bc_load:
                            sp.wait_ge(q, 16 * j)
                    sp.dma_start(bc[:, :], bcT[RK:NX, :]).then_inc(s.bc_out, 16)
                    sp.wait_ge(s.bc_out, 16 * (j + 1))
                    for i in range(NBC):
                        n = (i // 2) * ROWS_AT_ONCE
                        row = (i % 2) * NS + n
                        if j:
                            sp.wait_ge((s.dbx, s.hc)[i % 2], ((j * MT) - 1) * NS + n + ROWS_AT_ONCE)
                        sp.dma_start(bcb[:, row:row + ROWS_AT_ONCE, :], bc[row:row + ROWS_AT_ONCE, :].unsqueeze(0)
                                     .broadcast_to([P, ROWS_AT_ONCE, BLK])).then_inc(bc_load[i], 16)

                def x2_tile(i):
                    t = i - X2_LAG
                    if 0 <= t and t % TB == TB - 1:
                        sp.wait_ge(i1.x2, t + 1)
                        sp.dma_start(x2_out[t // TB].rearrange("(t p) d -> p t d", p=P),
                                     x2[:, t + 1 - TB:t + 1, :]).then_inc(i1.store, 16)

                load(-1, 0, 0)
                start(x2_tile, turn)
                for k in range(NB):
                    turns(sp, k, turn)
                sp.wait_ge(i1.store, 16 * NB)
                store(NB, 0, 0)
                for q in y_store:
                    sp.wait_ge(q, 16 * NB * MT // 2)

            @block.tensor
            def _(pe):
                def project_x(k, m, par, c):
                    T = k * MT + m
                    if c == 0:
                        pe.wait_ge(wx[par], weights(k, m, par))
                        if k < 0:
                            pe.wait_ge(i1.ev, TB)
                        if from_on(T + MT, 2):
                            pe.wait_ge(s.tap, T + MT - 1)
                            pe.wait_ge(s.padded, T + MT - 1)
                    mm = pe.matmul(ps[:, PX[par], :], wxr[:, par, c, :], xnT[:, c, (k + 1) * BLK:(k + 2) * BLK],
                                   start=(c == 0), stop=(c == KC - 1))
                    if c == KC - 1:
                        mm.then_inc(s.px, 1)

                def project_z(k, m, par, c):
                    T = k * MT + m
                    first = kind(k, m)[3]
                    j = k if first else k + 1
                    if c == 0:
                        pe.wait_ge(wz[1 - par], weights_z(k, m, par))
                        if from_on(T + MT - 1, 1):
                            pe.wait_ge(s.zs, T + MT - 1)
                    mm = pe.matmul(ps[:, PZ, :], wzr[:, 1 - par, c, :], xnT[:, c, j * BLK:(j + 1) * BLK],
                                   start=(c == 0), stop=(c == KC - 1))
                    if c == KC - 1:
                        mm.then_inc(s.pz, 1)

                def step_sizes(q, par, first):
                    if from_on(q, 1):
                        pe.wait_ge(s.dts, q)
                    if first:
                        pe.wait_ge(s.dt_in, q // MT + 1)
                    pe.wait_ge(s.dt_sel, q + 1)
                    pe.matmul(ps[:, PDT, :], dtm_w[:, par, :], dtT[:], start=True, stop=True).then_inc(s.dtm, 1)

                def turn(k, m, par):
                    T = k * MT + m
                    scans, px, pz, first, last = kind(k, m)
                    if scans:
                        if from_on(T, 2):
                            pe.wait_ge(s.gate, T - 1)
                        pe.wait_ge(s.skip_sel, T + 1)
                        pe.matmul(ps[:, PY + par, :], skip[:, par, :], tile(xc, m), start=True, stop=False).then_inc(s.skip, 1)
                    for n in range(NS):
                        for c in ((n,) if not last else (2 * n, 2 * n + 1)):
                            if px and c < KC:
                                project_x(k, m, par, c)
                        c = n - (NS - KC if last else KC + 1)
                        if pz and 0 <= c < KC:
                            project_z(k, m, par, c)
                        if scans and not last and n == KC:
                            step_sizes(T + 1, 1 - par, False)
                        if px and n == (9 if last else NS - 1):
                            pe.wait_ge(s.xc, T + MT + 1)
                            pe.wait_ge(s.xw_sel, T + MT + 1)
                            if first and scans:
                                pe.wait_ge(s.dt_in, k + 1)
                                pe.wait_ge(s.bc_sb, k + 1)
                            pe.matmul(ps[:, PXP, :], xw_one[:, par, :], tile(xc, m), start=first, stop=last).then_inc(s.xp, 1)
                        if last and px and n == 10:
                            pe.wait_ge(s.sq, k + 2)
                            pe.matmul(ps[0:NX, PMEAN, :], mean[:], soft[0:NX, :], start=True, stop=True).then_inc(s.mean, 1)
                        if last and px and n == 12:
                            step_sizes(T + 1, 0, True)
                        if scans:
                            pe.wait_ge(s.hc, T * NS + n + 1)
                            pe.matmul(ps[:, PY + par, :], keep.ident[:], hc[:, n % RING, :],
                                      start=False, stop=(n == NS - 1)).then_inc(s.ys, 1)

                def x2_tile(i):
                    t = i - X2_LAG
                    if 0 <= t < T2:
                        pe.wait_ge(i1.xn, t + 1)
                        if t >= 2:
                            pe.wait_ge(i1.ev, t - 1)
                        for k in range(KC):
                            mm = pe.transpose(ps[:, PY + t % 2, k * P:k * P + P], xn[:, t % 2, k * P:k * P + P], keep.ident[:])
                        mm.then_inc(i1.tr, 1)

                start(x2_tile, turn)
                pe.wait_ge(i1.ev, T2)
                for k in range(NB):
                    turns(pe, k, turn)

            @block.scalar
            def _(act):
                def take_x(k, m, par):
                    U = (k + 1) * MT + m
                    act.wait_ge(s.px, U + 1)
                    if from_on(U, 2):
                        act.wait_ge(s.conv, CONV * (U - 1))
                        act.wait_ge(s.xc, U - 1)
                    act.activation(pad[:, par, CONV - 1:], ps[:, PX[par], :], ACT.Copy).then_inc(s.padded, 1)
                    act.activation(acc[:, par, :], ps[:, PX[par], :], ACT.Identity, bias=col(cb, m),
                                   scale=col(cw, m, CONV - 1)).then_inc(s.tap, 1)

                def silu_z(T, m):
                    act.wait_ge(s.pz, T + MT)
                    if from_on(T, 1):
                        act.wait_ge(s.gate, T)
                    act.activation(tile(sz, m), ps[:, PZ, :], ACT.Silu).then_inc(s.zs, 1)

                def silus(k, m, par):
                    T = k * MT + m
                    scans, px, pz, first, last = kind(k, m)
                    if px:
                        act.wait_ge(s.conv, CONV * (T + MT + 1))
                        if scans:
                            act.wait_ge(s.skip, T + 1)
                            act.wait_ge(s.u, T + 1)
                        act.activation(tile(xc, m), acc[:, par, :], ACT.Silu).then_inc(s.xc, 1)
                    if pz and not last:
                        silu_z(T, MT - 1 if first else m - 1)
                    if px or pz:
                        act.preload_act_table_set("natural_log_exp_and_others")

                def select(q, m, par):
                    if from_on(q, 2):
                        act.wait_ge(s.dtm, q - 1)
                        act.wait_ge(s.skip, q - 1)
                    act.activation(dtm_w[:, par, :], dtw[:, m * P:m * P + P] if isinstance(m, int)
                                   else dtw[:, ds(m * P, P)], ACT.Copy).then_inc(s.dt_sel, 1)
                    act.activation(skip[:, par, :], keep.ident[:], ACT.Copy, scale=col(dp, m)).then_inc(s.skip_sel, 1)

                def softplus(q):
                    act.wait_ge(s.dtm, q + 1)
                    if from_on(q, 1):
                        act.wait_ge(s.dts, q)
                    act.activation(soft[:], ps[:, PDT, :], ACT.Abs).then_inc(s.ab, 1)
                    act.wait_ge(s.ab, q + 1)
                    act.activation(soft[:], soft[:], ACT.Exp, scale=-1.0).then_inc(s.ex, 1)
                    act.wait_ge(s.ex, q + 1)
                    act.activation(soft[:], soft[:], ACT.Ln, bias=1.0).then_inc(s.lg, 1)

                def keep_state(T, m, n):
                    act.wait_ge(s.h, T * NS + n + 1)
                    act.activation(col(state, m, n), hs[:, n % RING, BLK - 1:BLK], ACT.Copy).then_inc(s.carry, 1)

                def turn(k, m, par):
                    T = k * MT + m
                    scans, px, pz, first, last = kind(k, m)
                    for n in range(NS):
                        if first and scans and n == 4:
                            silu_z(T - 1, MT - 2)
                            act.preload_act_table_set("natural_log_exp_and_others")
                        if px and n == (8 if last else 9):
                            take_x(k, m, par)
                        if n == 5 and (scans and not last or last and px):
                            select(T + 1, 0 if last else m + 1, 1 - par)
                        if n == (10 if last else 14):
                            silus(k, m, par)
                        if scans and not last and n == 10:
                            softplus(T + 1)
                        if px and n == 5:
                            if k < 0 and first:
                                act.wait_ge(r.dt_ones, 2)
                            if from_on(T + MT, 2):
                                act.wait_ge(s.xp, T + MT - 1)
                            act.activation(xw_one[:, par, 0:NX], tile(xw, m), ACT.Copy).then_inc(s.xw_sel, 1)
                        if last and px and n == 11:
                            act.wait_ge(s.xp, (k + 2) * MT)
                            act.activation(soft[0:NX, :], ps[0:NX, PXP, :], ACT.Square).then_inc(s.sq, 1)
                        if last and px and n == 13:
                            act.wait_ge(s.mean, k + 2)
                            act.activation(soft[0:NX, :], ps[0:NX, PMEAN, :], ACT.Ln, bias=RMS_EPS).then_inc(s.lnx, 1)
                            act.wait_ge(s.lnx, k + 2)
                            act.activation(soft[0:NX, :], soft[0:NX, :], ACT.Exp, scale=-0.5).then_inc(s.rsx, 1)
                        if last and px and n == 15:
                            act.wait_ge(s.dt_in, k + 2)
                            act.wait_ge(s.bc_sb, k + 2)
                            softplus(T + 1)
                        if scans:
                            if n == 0:
                                act.wait_ge(s.dts, T + 1)
                            if n >= RING or from_on(T, 1):
                                act.wait_ge(s.h, T * NS + n + 1 - RING)
                            act.activation(da[:, n % RING, :], dts[:, par, :], ACT.Exp,
                                           scale=col(na, m, n)).then_inc(s.da, 1)
                            if n < RING - 1:
                                if keeps((k - 1) if first else k) and from_on(T, 1):
                                    keep_state(T - 1, MT - 1 if first else m - 1, NS + n + 1 - RING)
                            elif keeps(k):
                                keep_state(T, m, n + 1 - RING)

                def x2_tile(i):
                    if i < T2:
                        layernorm_tail(act, mv1, ln1, rs1, i, i1.ag1, i1.ln1, i1.rs1, i + 1)
                    t = i - 3
                    if 0 <= t < T2:
                        layernorm_tail(act, mv2, ln2, rs2, t, i1.ag2, i1.ln2, i1.rs2, t + 1)
                    t = i - X2_LAG
                    if 0 <= t < T2:
                        act.wait_ge(i1.tr, t + 1)
                        act.activation(xnT[:, :, t * P:t * P + P], ps[:, PY + t % 2, :].rearrange("p (c n) -> p c n", c=KC),
                                       ACT.Copy).then_inc(i1.ev, 1)

                act.preload_act_table_set("natural_log_exp_and_others")
                act.activation(na[:], na[:], ACT.Exp).then_inc(r.a, 1)
                start(x2_tile, turn)
                act.wait_ge(r.neg, 1)
                for k in range(NB):
                    turns(act, k, turn)

            @block.gpsimd
            def _(pool):
                def drive(q, m, par):
                    pool.wait_ge(s.dts, q + 1)
                    if from_on(q, 2):
                        pool.wait_ge(s.dbx, (q - 1) * NS)
                    pool.tensor_tensor(u[:, par, :], dts[:, par, :], tile(xc, m), ALU.mult).then_inc(s.u, 1)

                def turn(k, m, par):
                    T = k * MT + m
                    scans, px, pz, first, last = kind(k, m)
                    if scans:
                        for n in range(NS):
                            pool.wait_ge(s.h, T * NS + n + 1)
                            if first and n % ROWS_AT_ONCE == 0:
                                pool.wait_ge(bc_load[2 * (n // ROWS_AT_ONCE) + 1], 16 * (k + 1))
                            if n >= RING or from_on(T, 1):
                                pool.wait_ge(s.ys, T * NS + n + 1 - RING)
                            pool.tensor_tensor(hc[:, n % RING, :], hs[:, n % RING, :], bcb[:, NS + n, :],
                                               ALU.mult).then_inc(s.hc, 1)
                            if not last and n == 11:
                                drive(T + 1, m + 1, 1 - par)
                            if last and px and n == 14:
                                next_block(k)
                    elif last and px:
                        next_block(k)

                def next_block(k):
                    pool.wait_ge(s.xc, (k + 2) * MT)
                    drive((k + 1) * MT, 0, 0)

                def x2_tile(i):
                    t = i - 1
                    if 0 <= t < T2:
                        pool.wait_ge(i1.up, t + 1)
                        pool.tensor_tensor(x2[:, t, :], x2[:, t, :], up[:, t % 2, :], ALU.add).then_inc(i1.x2, 1)

                pool.memset(dtT[RK:RK + 1, :], 1.0).then_inc(r.dt_ones, 1)
                pool.wait_ge(r.dt_ones, 1)
                pool.memset(xw_one[:], 0.0).then_inc(r.dt_ones, 1)
                pool.wait_ge(r.dt_ones, 2)
                start(x2_tile, turn)
                for k in range(NB):
                    turns(pool, k, turn)

            @block.vector
            def _(dve):
                def head(k, m, par):
                    U = (k + 1) * MT + m
                    if from_on(U, 2):
                        dve.wait_ge(s.conv, CONV * (U - 1))
                    if (k + 1) % SPB == 0:
                        dve.memset(pad[:, par, 0:CONV - 1], 0.0).then_inc(s.head, 1)
                    else:
                        dve.tensor_copy(pad[:, par, 0:CONV - 1], tile(conv_carry, m)).then_inc(s.head, 1)

                def tap(k, m, par, i):
                    U = (k + 1) * MT + m
                    if i == 0:
                        dve.wait_ge(s.padded, U + 1)
                        dve.wait_ge(s.tap, U + 1)
                        dve.wait_ge(s.head, U + 1)
                    else:
                        dve.wait_ge(s.conv, CONV * U + i)
                    dve.scalar_tensor_tensor(acc[:, par, :], pad[:, par, i:i + BLK], col(cw, m, i), acc[:, par, :],
                                             ALU.mult, ALU.add).then_inc(s.conv, 1)
                    if i == CONV - 2:
                        dve.tensor_copy(tile(conv_carry, m), pad[:, par, BLK:BLK + CONV - 1]).then_inc(s.conv, 1)

                def steps(q, par):
                    dve.wait_ge(s.lg, q + 1)
                    if from_on(q, 2):
                        dve.wait_ge(s.da, (q - 1) * NS)
                        dve.wait_ge(s.u, q - 1)
                    dve.scalar_tensor_tensor(dts[:, par, :], ps[:, PDT, :], 0.0, soft[:], ALU.max, ALU.add).then_inc(s.dts, 1)

                def gate(T, m, par):
                    dve.wait_ge(s.ys, (T + 1) * NS)
                    dve.wait_ge(s.zs, T + 1)
                    if from_on(T, 2):
                        dve.wait_ge(y_store[par], 8 * (T - par))
                    dve.tensor_tensor(yo[:, par, :], ps[:, PY + par, :], tile(sz, m), ALU.mult).then_inc(s.gate, 1)

                def rms(k, lo, hi, out, used, count, done):
                    dve.wait_ge(s.rsx, k + 2)
                    if k >= 0:
                        dve.wait_ge(used, count)
                    dve.scalar_tensor_tensor(out[lo:hi, :], ps[lo:hi, PXP, :], nw[lo:hi, 0:1], soft[lo:hi, :],
                                             ALU.mult, ALU.mult).then_inc(done, 1)

                def drive(k, m, par, n):
                    T = k * MT + m
                    if kind(k, m)[3] and n % ROWS_AT_ONCE == 0:
                        dve.wait_ge(bc_load[2 * (n // ROWS_AT_ONCE)], 16 * (k + 1))
                    if n >= RING or from_on(T, 1):
                        dve.wait_ge(s.h, T * NS + n + 2 - RING)
                    dve.tensor_tensor(dbx[:, n % RING:n % RING + 2, :], u[:, par, :].unsqueeze(1).broadcast_to([P, 2, BLK]),
                                      bcb[:, n:n + 2, :], ALU.mult).then_inc(s.dbx, 2)

                def turn(k, m, par):
                    T = k * MT + m
                    scans, px, pz, first, last = kind(k, m)
                    zero_start = k % SPB == 0
                    for n in range(NS):
                        if scans:
                            if n == 0:
                                dve.wait_ge(s.u, T + 1)
                                drive(k, m, par, 0)
                            if n % 2 and n + 1 < NS:
                                drive(k, m, par, n + 1)
                            dve.wait_ge(s.da, T * NS + n + 1)
                            dve.wait_ge(s.dbx, T * NS + n + 1)
                            if n >= RING or from_on(T, 1):
                                dve.wait_ge(s.hc, T * NS + n + 1 - RING)
                            kept = carried(k, m, n)
                            if kept is not None:
                                dve.wait_ge(s.carry, kept)
                            dve.tensor_tensor_scan(hs[:, n % RING, :], da[:, n % RING, :], dbx[:, n % RING, :],
                                                   0.0 if zero_start else col(state, m, n), ALU.mult, ALU.add).then_inc(s.h, 1)
                        if px and n == 0:
                            head(k, m, par)
                        if scans and n == 2 and from_on(T, 1):
                            gate(T - 1, MT - 1 if first else m - 1, 1 - par)
                        at = 6 if last else 7
                        if px and at <= n < at + CONV - 1:
                            tap(k, m, par, n - at)
                        if scans and not last and n == 10:
                            steps(T + 1, 1 - par)
                        if last and px and n == 11:
                            rms(k, RK, NX, bcT, s.bc_out, 16 * (k + 1), s.bc_sb)
                        if last and px and n == 12:
                            rms(k, 0, RK, dtT, s.dtm, (k + 1) * MT, s.dt_in)
                        if last and px and n == 14:
                            steps(T + 1, 0)

                def x2_tile(i):
                    if i < T2:
                        dve.scalar_tensor_tensor(dn[:, i, :], dn[:, i, :], keep.query_hit[:, i:i + 1],
                                                 keep.rows[:], ALU.mult, ALU.mult).then_inc(i1.masked, 1)
                    t = i - 1
                    if 0 <= t < T2:
                        dve.wait_ge(i1.rs1, t + 1)
                        dve.wait_ge(i1.ag1, t + 1)
                        if t >= 2:
                            dve.wait_ge(i1.x2, t - 1)
                        dve.tensor_scalar(up[:, t % 2, :], dn[:, t, :], mv1[:, t, 0:1], rs1[:, t:t + 1],
                                          ALU.subtract, ALU.mult).then_inc(i1.up, 1)
                    if i < T2:
                        dve.wait_ge(i1.masked, i + 1)
                        layernorm_stats(dve, dn[:, i, :], st1, mv1, i, i1.st1, i1.ag1, i + 1)
                    t = i - 3
                    if 0 <= t < T2:
                        dve.wait_ge(i1.x2, t + 1)
                        layernorm_stats(dve, x2[:, t, :], st2, mv2, t, i1.st2, i1.ag2, t + 1)
                    t = i - X2_LAG + 1
                    if 0 <= t < T2:
                        dve.wait_ge(i1.rs2, t + 1)
                        dve.wait_ge(i1.ag2, t + 1)
                        if t >= 2:
                            dve.wait_ge(i1.tr, t - 1)
                        dve.tensor_scalar(xn[:, t % 2, :], x2[:, t, :], mv2[:, t, 0:1], rs2[:, t:t + 1],
                                          ALU.subtract, ALU.mult).then_inc(i1.xn, 1)

                dve.wait_ge(r.a, 1)
                dve.tensor_scalar(na[:], na[:], -1.0, None, ALU.mult).then_inc(r.neg, 1)
                start(x2_tile, turn)
                for k in range(NB):
                    turns(dve, k, turn)
                gate(NB * MT - 1, MT - 1, 1)
        clear(nc, (*r, *i1, *s, *bc_load))


def from_on(count, n):
    return not isinstance(count, int) or count >= n


def keeps(k):
    return k >= 0 and k % SPB < SPB - 1


def weights(k, m, par):
    return 8 * ((k + 1) * MT + m - par) + 16


def weights_z(k, m, par):
    return 8 * ((k + 1) * MT + m - 1 - (1 - par)) + 16


def carried(k, m, n):
    first = isinstance(m, int) and m == 0
    if not keeps((k - 1) if first and n < RING else k):
        return None
    return k // SPB * (SPB - 1) * MT * NS + (k % SPB * MT + m) * NS + n + 1 - RING


NE = 8
RE = 16
SCALING = 2.0
NL = NE * RE


def out_stage(nc, ctx, ps, keep, x2_in, y_in, w_out, w_gate_low, w_base, base_b, w_up, expert_ids, out):
    s = semaphores(nc, ctx, "t", "w w2 y0 y1 x0 x1 o st1 ag1 ln1 rs1 up x3 st2 ag2 ln2 rs2 xn tr ev gl top idx pick wt sum "
                   "mix scl ltr lev base bs st3 ag3 ln3 rs3 up3 fin out0 out1 out2 out3")
    y_load, x_load, out_store = (s.y0, s.y1), (s.x0, s.x1), (s.out0, s.out1, s.out2, s.out3)
    T = B * ST
    with ExitStack() as mem:
        def sb(name, shape, dt=F32):
            return mem.enter_context(nc.sbuf_tensor(name, shape, dt))

        wo = sb("t_wo", [P, MT, D])
        wgl = sb("wgl", [P, KC, NE + NL])
        wb = sb("wb", [P, KC, D])
        wu = sb("wu", [NL, D])
        bb = sb("bb", [P, D])
        eid = sb("eid", [P, NE])
        y = sb("t_y", [P, 2, MT, BLK])
        x3 = sb("x3", [P, 2 * TB, D])
        up = sb("t_up", [P, 2, D])
        xn = sb("t_xn", [P, 2, D])
        xnT = sb("t_xnT", [P, 4, KC, P])
        st1, mv1, ln1, rs1 = sb("t_st1", [P, T, 6]), sb("t_mv1", [P, T, 2]), sb("t_ln1", [P, T]), sb("t_rs1", [P, T])
        st2, mv2, ln2, rs2 = sb("t_st2", [P, T, 6]), sb("t_mv2", [P, T, 2]), sb("t_ln2", [P, T]), sb("t_rs2", [P, T])
        st3, mv3, ln3, rs3 = sb("t_st3", [P, T, 6]), sb("t_mv3", [P, T, 2]), sb("t_ln3", [P, T]), sb("t_rs3", [P, T])
        logit = sb("logit", [P, T, NE])
        top = sb("t_top", [P, T, 8])
        idx = sb("t_idx", [P, T, 8], mybir.dt.uint32)
        idf = sb("t_idf", [P, T, 2])
        gap = sb("gap", [P, T])
        total = sb("total", [P, T])
        second = sb("second", [P, T])
        wt = sb("t_wt", [P, T, 2])
        mix = sb("t_mix", [P, T, 2, NE])
        low = sb("t_low", [P, 2, NL])
        lowT = sb("t_lowT", [NL, 2, P])
        res = sb("t_res", [P, 2, D])
        up3 = sb("t_up3", [P, 2, D])
        fin = sb("t_fin", [P, 4, D])

        with nc.Block() as block:
            @block.sync
            def _(sp):
                def load_y(g):
                    if g >= 2:
                        sp.wait_ge(s.o, TB * (g - 1))
                    sp.dma_start(y[:, g % 2, :, :], y_in[g]).then_inc(y_load[g % 2], 16)

                def load_x(g):
                    if g >= 2:
                        sp.wait_ge(s.fin, TB * (g - 1))
                    sp.dma_start(x3[:, g % 2 * TB:g % 2 * TB + TB, :],
                                 x2_in[g].rearrange("(t p) d -> p t d", p=P)).then_inc(x_load[g % 2], 16)

                sp.dma_start(wo[:], w_out.rearrange("(m p) n -> p m n", p=P)).then_inc(s.w, 16)
                load_y(0)
                load_x(0)
                for dst, src in ((wgl[:], w_gate_low.rearrange("(c p) n -> p c n", p=P)),
                                 (wb[:], w_base.rearrange("(c p) n -> p c n", p=P)),
                                 (wu[:], w_up),
                                 (bb[:], base_b.rearrange("(a n) -> a n", a=1).broadcast_to([P, D])),
                                 (eid[:], expert_ids)):
                    sp.dma_start(dst, src).then_inc(s.w2, 16)
                load_y(1)
                load_x(1)
                for t in range(T):
                    sp.wait_ge(s.fin, t + 1)
                    sp.dma_start(out[t // TB, t % TB * P:t % TB * P + P, :], fin[:, t % 4, :]).then_inc(out_store[t % 4], 16)
                    g = t // TB + 2
                    if t % TB == 1 and g < NB:
                        load_y(g)
                    if t % TB == TB - 1 and g < NB:
                        load_x(g)
                for q in out_store:
                    sp.wait_ge(q, 16 * T // 4)

            @block.tensor
            def _(pe):
                pe.wait_ge(s.w, 16)
                for i in range(T + 2):
                    if i < T:
                        g = i // TB
                        pe.wait_ge(y_load[g % 2], 16 * (g // 2 + 1))
                        if i >= 2:
                            pe.wait_ge(s.up, i - 1)
                        for m in range(MT):
                            mm = pe.matmul(ps[:, i % 2, :], y[:, g % 2, m, i % TB * P:i % TB * P + P], wo[:, m, :],
                                           start=(m == 0), stop=(m == MT - 1))
                        mm.then_inc(s.o, 1)
                    t = i - 1
                    if 0 <= t < T:
                        pe.wait_ge(s.xn, t + 1)
                        if t >= 1:
                            pe.wait_ge(s.ev, t)
                        for k in range(KC):
                            mm = pe.transpose(ps[:, 2, k * P:k * P + P], xn[:, t % 2, k * P:k * P + P], keep.ident[:])
                        mm.then_inc(s.tr, 1)
                    t = i - 2
                    if 0 <= t < T:
                        pe.wait_ge(s.scl, t + 1)
                        if t >= 1:
                            pe.wait_ge(s.lev, t)
                        pe.transpose(ps[:, 6, 0:P], low[:, t % 2, :], keep.ident[:]).then_inc(s.ltr, 1)
                        if t >= 2:
                            pe.wait_ge(s.bs, t - 1)
                        for k in range(KC):
                            pe.matmul(ps[:, 4 + t % 2, :], xnT[:, t % 4, k, :], wb[:, k, :], start=(k == 0), stop=False)
                        pe.wait_ge(s.lev, t + 1)
                        pe.matmul(ps[:, 4 + t % 2, :], lowT[:, t % 2, :], wu[:], start=False, stop=True).then_inc(s.base, 1)
                    t = i - 1
                    if 0 <= t < T:
                        pe.wait_ge(s.ev, t + 1)
                        if t == 0:
                            pe.wait_ge(s.w2, 16 * 5)
                        if t >= 1:
                            pe.wait_ge(s.scl, t)
                        for k in range(KC):
                            mm = pe.matmul(ps[:, 3, 0:NE + NL], xnT[:, t % 4, k, :], wgl[:, k, :],
                                           start=(k == 0), stop=(k == KC - 1))
                        mm.then_inc(s.gl, 1)

            @block.scalar
            def _(act):
                act.preload_act_table_set("natural_log_exp_and_others")
                for i in range(T + 4):
                    t = i - 2
                    if 0 <= t < T:
                        act.wait_ge(s.pick, t + 1)
                        act.activation(second[:, t:t + 1], gap[:, t:t + 1], ACT.Exp).then_inc(s.wt, 1)
                    t = i - 3
                    if 0 <= t < T:
                        layernorm_tail(act, mv3, ln3, rs3, t, s.ag3, s.ln3, s.rs3, t + 1)
                    if i < T:
                        layernorm_tail(act, mv1, ln1, rs1, i, s.ag1, s.ln1, s.rs1, i + 1)
                    t = i - 1
                    if 0 <= t < T:
                        act.wait_ge(s.tr, t + 1)
                        act.activation(xnT[:, t % 4, :, :].rearrange("p c n -> p (c n)"), ps[:, 2, :], ACT.Copy).then_inc(s.ev, 1)
                    t = i - 2
                    if 0 <= t < T:
                        act.wait_ge(s.ltr, t + 1)
                        if t >= 2:
                            act.wait_ge(s.base, t - 1)
                        act.activation(lowT[:, t % 2, :], ps[:, 6, 0:P], ACT.Copy).then_inc(s.lev, 1)
                    if i < T:
                        layernorm_tail(act, mv2, ln2, rs2, i, s.ag2, s.ln2, s.rs2, i + 1)

            @block.gpsimd
            def _(pool):
                for i in range(T + 3):
                    t = i - 3
                    if 0 <= t < T:
                        pool.wait_ge(s.up3, t + 1)
                        pool.wait_ge(s.x3, t + 1)
                        if t >= 4:
                            pool.wait_ge(out_store[t % 4], 16 * (t // 4))
                        pool.tensor_tensor(fin[:, t % 4, :], x3[:, t % (2 * TB), :], up3[:, t % 2, :], ALU.add).then_inc(s.fin, 1)
                    if i < T:
                        g = i // TB
                        pool.wait_ge(x_load[g % 2], 16 * (g // 2 + 1))
                        pool.wait_ge(s.up, i + 1)
                        pool.tensor_tensor(x3[:, i % (2 * TB), :], x3[:, i % (2 * TB), :], up[:, i % 2, :], ALU.add).then_inc(s.x3, 1)

            @block.vector
            def _(dve):
                def pick(t):
                    dve.wait_ge(s.gl, t + 1)
                    dve.tensor_copy(logit[:, t, :], ps[:, 3, 0:NE]).then_inc(s.top, 1)
                    dve.wait_ge(s.top, 3 * t + 1)
                    dve.max(top[:, t, :], logit[:, t, :]).then_inc(s.top, 1)
                    dve.wait_ge(s.top, 3 * t + 2)
                    dve.tensor_tensor(gap[:, t:t + 1], top[:, t, 1:2], top[:, t, 0:1], ALU.subtract).then_inc(s.pick, 1)
                    dve.max_index(idx[:, t, :], top[:, t, :], logit[:, t, :]).then_inc(s.top, 1)

                def result(t):
                    dve.wait_ge(s.base, t + 1)
                    dve.tensor_tensor(res[:, t % 2, :], ps[:, 4 + t % 2, :], bb[:], ALU.add).then_inc(s.bs, 1)

                def mixture(t):
                    dve.wait_ge(s.top, 3 * t + 3)
                    dve.tensor_copy(idf[:, t, :], idx[:, t, 0:2]).then_inc(s.idx, 1)
                    dve.wait_ge(s.wt, t + 1)
                    dve.tensor_scalar(total[:, t:t + 1], second[:, t:t + 1], 1.0, None, ALU.add).then_inc(s.sum, 1)
                    dve.wait_ge(s.sum, 5 * t + 1)
                    dve.reciprocal(wt[:, t, 0:1], total[:, t:t + 1]).then_inc(s.sum, 1)
                    dve.wait_ge(s.sum, 5 * t + 2)
                    dve.tensor_tensor(wt[:, t, 1:2], second[:, t:t + 1], wt[:, t, 0:1], ALU.mult).then_inc(s.sum, 1)
                    dve.wait_ge(s.idx, t + 1)
                    dve.wait_ge(s.sum, 5 * t + 3)
                    for k in range(2):
                        dve.tensor_scalar(mix[:, t, k, :], eid[:], idf[:, t, k:k + 1], wt[:, t, k:k + 1],
                                          ALU.is_equal, ALU.mult).then_inc(s.sum, 1)
                    dve.wait_ge(s.sum, 5 * t + 5)
                    dve.tensor_tensor(mix[:, t, 0, :], mix[:, t, 0, :], mix[:, t, 1, :], ALU.add).then_inc(s.mix, 1)
                    dve.wait_ge(s.mix, t + 1)
                    if t >= 2:
                        dve.wait_ge(s.ltr, t - 1)
                    dve.scalar_tensor_tensor(low[:, t % 2, :].rearrange("p (e r) -> p e r", r=RE),
                                             ps[:, 3, NE:NE + NL].rearrange("p (e r) -> p e r", r=RE), SCALING,
                                             mix[:, t, 0, :].unsqueeze(2).broadcast_to([P, NE, RE]),
                                             ALU.mult, ALU.mult).then_inc(s.scl, 1)

                dve.wait_ge(s.w2, 16 * 5)
                for i in range(T + 4):
                    t = i - 2
                    if 0 <= t < T:
                        pick(t)
                    t = i - 3
                    if 0 <= t < T:
                        result(t)
                    t = i - 2
                    if 0 <= t < T:
                        mixture(t)
                    t = i - 3
                    if 0 <= t < T:
                        dve.wait_ge(s.bs, t + 1)
                        layernorm_stats(dve, res[:, t % 2, :], st3, mv3, t, s.st3, s.ag3, t + 1)
                    if i < T:
                        dve.wait_ge(s.o, i + 1)
                        layernorm_stats(dve, ps[:, i % 2, :], st1, mv1, i, s.st1, s.ag1, i + 1)
                    t = i - 3
                    if 0 <= t < T:
                        dve.wait_ge(s.ag3, t + 1)
                        dve.wait_ge(s.rs3, t + 1)
                        if t >= 2:
                            dve.wait_ge(s.fin, t - 1)
                        dve.tensor_scalar(up3[:, t % 2, :], res[:, t % 2, :], mv3[:, t, 0:1], rs3[:, t:t + 1],
                                          ALU.subtract, ALU.mult).then_inc(s.up3, 1)
                    if i < T:
                        dve.wait_ge(s.ag1, i + 1)
                        dve.wait_ge(s.rs1, i + 1)
                        if i >= 2:
                            dve.wait_ge(s.x3, i - 1)
                        dve.tensor_scalar(up[:, i % 2, :], ps[:, i % 2, :], mv1[:, i, 0:1], rs1[:, i:i + 1],
                                          ALU.subtract, ALU.mult).then_inc(s.up, 1)
                        dve.wait_ge(s.x3, i + 1)
                        layernorm_stats(dve, x3[:, i % (2 * TB), :], st2, mv2, i, s.st2, s.ag2, i + 1)
                        dve.wait_ge(s.ag2, i + 1)
                        dve.wait_ge(s.rs2, i + 1)
                        if i >= 2:
                            dve.wait_ge(s.tr, i - 1)
                        dve.tensor_scalar(xn[:, i % 2, :], x3[:, i % (2 * TB), :], mv2[:, i, 0:1], rs2[:, i:i + 1],
                                          ALU.subtract, ALU.mult).then_inc(s.xn, 1)


_W = ["L0_attn_x", "w_qkv", "L0_attn_wo", "w_dense", "w_cent", "L0_ffn_bias", "L0_ffn_assignments", "w_in",
      "L1_attn_conv_w", "conv_b", "w_x", "norm_w", "mean", "w_dt", "L1_attn_A_log",
      "d_skip", "w_out", "w_gate_low", "w_base", "L1_ffn_base_b", "w_up",
      "rope", "ident", "masks", "cluster_ids", "expert_ids"]


def run(stage, nc, *args):
    with ExitStack() as ctx:
        stage(nc, ctx, *args)


def two_layers(nc, t, out):
    def scratch(name, shape):
        return nc.dram_tensor(name, shape, F32, kind="Internal").ap()

    att_o, att_l, x2 = scratch("att_o", (H, HD, B * S)), scratch("att_l", (H, B * S)), scratch("x2_d", (NB, BLK, D))
    y = scratch("y_d", (NB, P, MT, BLK))
    bc = scratch("bc_d", (2 * NS, BLK))
    with ExitStack() as ctx:
        ps = ctx.enter_context(nc.psum_tensor("ps", [P, 8, 512], F32))
        ident = ctx.enter_context(nc.sbuf_tensor("identity", [P, P], F32))
        run(attention_stage, nc, ps, ident, t["L0_attn_x"], t["w_qkv"], t["rope"], t["ident"], t["masks"], att_o, att_l)
        with ExitStack() as mem:
            def sb(name, shape):
                return mem.enter_context(nc.sbuf_tensor(name, shape, F32))

            keep = namedtuple("keep", "ident hits query_hit rows")(
                ident, sb("keep_hits", [P, NC]), sb("keep_query_hit", [P, B * ST]),
                sb("keep_rows", [P, D]))
            small, transfers = scan_weights(nc, mem, t)
            xnT = sb("scan_in", [P, KC, B * S])
            work = sb("work", [P, 2 * B * ST, D])
            run(dense_stage, nc, ps, keep, work[:, 0:B * ST, :], work[:, B * ST:2 * B * ST, :], t["L0_attn_x"],
                att_o, att_l, t["L0_attn_wo"], t["w_dense"], t["w_cent"], t["L0_ffn_bias"], t["L0_ffn_assignments"], t["cluster_ids"],
                transfers)
            run(scan_stage, nc, ps, keep, work, xnT, small, t["w_in"], bc, x2, y)
        run(out_stage, nc, ps, namedtuple("keep", "ident")(ident), x2, y, t["w_out"], t["w_gate_low"], t["w_base"], t["L1_ffn_base_b"], t["w_up"],
                  t["expert_ids"], out)


def rope_tables(np):
    inv = 1.0 / 10000.0 ** (np.arange(0, HD, 2)[:HD // 2].astype(np.float32) / HD)
    f = np.outer(np.arange(S), inv).astype(np.float32)
    d = np.arange(P) % HD
    sign = np.where(d % 2 == 0, np.float32(-1), np.float32(1))[:, None]
    return np.stack([np.cos(f).T[d // 2], np.sin(f).T[d // 2] * sign], 1).astype(np.float32)


def kernel(**inputs):
    import numpy as np
    import concourse.bacc as _bacc
    from concourse import mybir as _mybir
    from concourse.bass_utils import run_bass_kernel_spmd as _run

    t = {k: np.asarray(v) for k, v in inputs.items()}
    wqkv = np.stack([t["L0_attn_wq"], t["L0_attn_wk"], t["L0_attn_wv"]])
    t["w_qkv"] = wqkv.reshape(3, KC, P, 2, HC).transpose(3, 2, 0, 1, 4)
    t["w_dense"] = t["L0_ffn_weight"].T
    t["w_cent"] = t["L0_ffn_centroids"].T
    t["w_in"] = t["L1_attn_in_proj_w"].reshape(KC, P, 2 * MT, P).transpose(2, 1, 0, 3)
    t["w_x"] = t["L1_attn_x_proj_w"].T
    t["norm_w"] = np.concatenate([t["L1_attn_dt_ln_w"], t["L1_attn_B_ln_w"], t["L1_attn_C_ln_w"]])[:, None]
    t["w_dt"] = np.concatenate([t["L1_attn_dt_proj_w"].T, t["L1_attn_dt_bias"][None]])
    for name, source in (("conv_b", "L1_attn_conv_b"), ("d_skip", "L1_attn_D_param")):
        t[name] = t[source].reshape(MT, P).T
    t["w_out"] = t["L1_attn_out_proj_w"].T
    t["w_gate_low"] = np.concatenate([t["L1_ffn_gate_w"].T, t["L1_ffn_lora_A"].reshape(NL, D).T], 1)
    t["w_base"] = t["L1_ffn_base_w"].T
    t["w_up"] = t["L1_ffn_lora_B"].transpose(0, 2, 1).reshape(NL, D)
    t["L0_attn_x"] = t["L0_attn_x"].reshape(NB, BLK, D)
    t["rope"] = rope_tables(np)
    group = np.array([0] * RK + [1] * NS + [2] * NS)
    t["mean"] = ((group[:, None] == group) / np.array([RK, NS, NS])[group]).astype(np.float32)
    t["ident"] = np.eye(P, dtype=np.float32)
    late = np.triu(np.full((P, P), -1e30, np.float32), 1)
    t["masks"] = np.stack([late, late.T], 1)
    t["cluster_ids"] = np.arange(NC, dtype=np.float32)[:, None]
    t["expert_ids"] = np.tile(np.arange(NE, dtype=np.float32), (P, 1))

    nc = _bacc.Bacc("TRN2", target_bir_lowering=False, num_devices=1)
    arrays, aps = {}, {}
    for name in _W:
        a = np.ascontiguousarray(t[name])
        arrays[f"in_{name}"] = a
        aps[name] = nc.dram_tensor(f"in_{name}", a.shape, _mybir.dt.from_np(a.dtype), kind="ExternalInput").ap()
    out = nc.dram_tensor("out_0", (NB, BLK, D), F32, kind="ExternalOutput").ap()
    two_layers(nc, aps, out)
    r = _run(nc, [arrays], core_ids=[0])
    return r.results[0]["out_0"].reshape(B, S, D)
```

```python
from collections import namedtuple
from contextlib import ExitStack

import concourse.bass as bass
from concourse import mybir

ALU = mybir.AluOpType
ACT = mybir.ActivationFunctionType
AX = mybir.AxisListType
F32 = mybir.dt.float32
BF16 = mybir.dt.bfloat16
I32 = mybir.dt.int32
ds = bass.ds

P = 128
D = 512
KC = D // P
B = 2
S = 1024
ST = S // P
BLK = 512
NB = B * S // BLK
TB = BLK // P
H = 32
HD = D // H
QH = 4
GH = P // HD
NG = B * H // GH
NSPLIT = 6
OUTS = QH + 1
QK = NSPLIT * HD
Q_PARTS = (0, 0, 0, 1, 1, 2)
K_PARTS = (0, 1, 2, 0, 1, 0)
VW = 32
LN_EPS = 1e-5


def semaphores(nc, ctx, stage, names):
    return namedtuple(stage, names)(*(ctx.enter_context(nc.semaphore(f"{stage}_{name}")) for name in names.split()))


def clear(nc, sems):
    with nc.Block() as block:
        @block.sync
        def _(sp):
            for s in sems:
                sp.sem_clear(s)




def score_width(j, half):
    return BLK * half + BLK - max(BLK * half, j * P)


SCORE_UNITS = [(j, half, h, max(1, BLK // score_width(j, half))) for j in range(ST) for half in range(j // TB, 2)
               for h in range(0, QH, max(1, BLK // score_width(j, half)))]
VALUE_UNITS = [(j, half) for j in range(ST) for half in range(j // TB, 2)]
MAX_UNITS = [(i, p, h, k) for i, ks in enumerate(((4,), (2,), (1,), (1,), (1, 4), (1, 2), (1, 1), (1, 1)))
             for p, k in enumerate(ks) for h in range(0, QH, k)]
FIRST = "SMMPMMPMPMSMSMPMaSSbSPMMSSdSePMMfPMPgMhWaSbSPMSMdPMePMSfPgMMhaSbWWMSPMdeSSSMPMfgPMMPhaSbSMWSSMSMdSeMfSWgWMShSSMMSWSMMMSMWTSWSSSSWSSWW"
SECOND = "SPPSSSPSPMSMvSSMSMWSMSMSSMSMSMWMMtMwSMWMSMSMSMPMMWMMSSMWMSMSSMSMPMMPMMWMMPMSMSSMSMSMWMSWTSSWvSSStSWSwWW"
PROJECT = "PPPPab" + "PPPPdaebfgh" * 3 + "PPPPdvefgh" + "twPPPPvtw"
ORDERS = (FIRST, SECOND)
NSC, NW = len(SCORE_UNITS), len(VALUE_UNITS)
NMAX = len(MAX_UNITS) + 1
RDQ = NSC + 2
COPY_AFTER = (VALUE_UNITS.index((TB - 1, 0)), NW - 1)
SLOTS = 3
FIRST_BANKS = (6, 7, 2, 3, 4)


def reads_behind(order):
    counts, n, w = [], 0, 0
    for what in order:
        if what == "S":
            n += 1
            counts.append(n)
        elif what == "W":
            n += w in COPY_AFTER
            w += 1
    return counts


READS = [reads_behind(order) for order in ORDERS]
LAST_SCORE = [max(u for u, unit in enumerate(SCORE_UNITS) if unit[0:2] == v) for v in VALUE_UNITS]


def walk(order, steps):
    done = dict.fromkeys(order, 0)
    for what in order:
        if what in steps:
            steps[what](done[what])
        done[what] += 1


def from_on(count, n):
    return not isinstance(count, int) or count >= n


def max_width(i, p):
    return min(BLK, (i + 1) * P - BLK * p)


def turn_groups(eng, quad):
    for r in range(2):
        for x in range(2):
            quad(r, r, x, True, 0)
    with eng.Fori(1, NG // 2 - 1) as i:
        for r in range(2):
            for x in range(2):
                quad(i * 2 + r, r, x, True, i)
    for r in range(2):
        for x in range(2):
            quad(NG - 2 + r, r, x, r == 0, NG // 2 - 1)


def attention_stage(nc, ctx, ps, ident_f, x, w_qkv, rope, ident, masks, att_o, att_l):
    with ExitStack() as mem:
        def sb(name, shape, dt=F32):
            return mem.enter_context(nc.sbuf_tensor(name, shape, dt))

        ident_b = sb("ident_b", [P, P], BF16)
        mask_f = sb("mask_f", [P, 2, P])
        mask_b = sb("mask_b", [P, 2, P], BF16)
        cos_sin = sb("cos_sin", [P, 2, S])
        xnT = sb("xnT", [P, KC, B * S])
        w3 = sb("w3", [P, 2, 3, KC, P])
        q6 = sb("q6", [QK + 3, 2 * GH, S], BF16)
        k6 = sb("k6", [QK + 3, 2 * GH, S], BF16)
        vh = sb("vh", [P, ST, 2 * GH, VW])
        va = sb("va", [P, ST, QH * VW])
        probs = sb("probs", [P, 2, QH, S])
        o_sb = sb("o_sb", [P, S])
        vT = sb("vT", [P, BLK])
        q_raw = sb("q_raw", [P, BLK])
        q_swap = sb("q_swap", [P, BLK])
        t_cos = sb("t_cos", [P, BLK])
        t_sin = sb("t_sin", [P, BLK])
        q_rot = sb("q_rot", [P, BLK])
        q_rest = sb("q_rest", [P, BLK])
        parts = sb("parts", [P, 2, 3, BLK], BF16)
        ones3 = parts[0:3, 0, 0:2, :].rearrange("p a n -> p (a n)")
        mx = sb("mx", [P, 2, QH, ST])
        nm = sb("nm", [P, QH, ST])
        m_rest = sb("m_rest", [QH * ST, P])
        m_parts = sb("m_parts", [QH * ST, 2, 3, P], BF16)
        st6 = sb("st6", [P, B * ST, 6])
        mv = sb("mv", [P, B * ST, 2])
        lnv = sb("lnv", [P, B * ST])
        rstd = sb("rstd", [P, B * ST])
        xt = probs[:].rearrange("p s a (t d) -> p (s a t) d", d=D)

        o_ps = ps[:, 0:2, :].rearrange("p a n -> p (a n)")
        st_ps = [ps[:, 2 + i, :] for i in range(SLOTS)]
        pr_ps = ps[:, 2 + SLOTS, :]
        mx_ps = [ps[:, 6 + i, :] for i in range(2)]

        scratch = nc.dram_tensor("split_parts", (2, 3, GH, HD, S), BF16, kind="Internal").ap()
        c = semaphores(nc, ctx, "ac", "ident const cast ones ones_in")
        n = semaphores(nc, ctx, "an", "x0 x1 x2 x3 stats aggr lnv rstd xn tr ev")
        a = semaphores(nc, ctx, "aa", "w0 w1 proj took swap sin rot hi rest mid lo kept0 kept1 rep0 rep1 vproj vt vtr vdone "
                       "act_rd scores max max_rd m_ready m_in m_chain m_split va pv out")
        with nc.Block() as block:
            @block.sync
            def _(sp):
                sp.dma_start(ident_f[:], ident).then_inc(c.ident, 16)
                for g, s in enumerate((n.x0, n.x1, n.x2, n.x3)):
                    sp.dma_start(xt[:, TB * g:TB * g + TB, :], x[g].rearrange("(t p) d -> p t d", p=P)).then_inc(s, 16)
                sp.dma_start(mask_f[:], masks).then_inc(c.const, 16)
                sp.dma_start(cos_sin[:], rope).then_inc(c.const, 16)
                sp.wait_ge(c.ones, 1)
                sp.dma_start(k6[QK:QK + 3, :, :], ones3.unsqueeze(1).broadcast_to([3, 2 * GH, S])).then_inc(c.ones_in, 16)
                sp.wait_ge(c.const, 32)
                sp.wait_ge(c.ones_in, 16)

            @block.gpsimd
            def _(pool):
                pool.memset(vh[:, :, :, HD:VW], 1.0)

            @block.vector
            def _(dve):
                def normalise(g):
                    dve.wait_ge(n.rstd, g + 1)
                    for t in range(TB * g, TB * g + TB):
                        dve.tensor_scalar(xt[:, t, :], xt[:, t, :], mv[:, t, 0:1], rstd[:, t:t + 1],
                                          ALU.subtract, ALU.mult).then_inc(n.xn, 1)

                dve.memset(ones3, 1.0).then_inc(c.ones, 1)
                for g, s in enumerate((n.x0, n.x1, n.x2, n.x3)):
                    dve.wait_ge(s, 16)
                    for t in range(TB * g, TB * g + TB):
                        dve.bn_stats(st6[:, t, :], xt[:, t, :]).then_inc(n.stats, 1)
                    for t in range(TB * g, TB * g + TB):
                        dve.wait_ge(n.stats, t + 1)
                        dve.bn_aggr(mv[:, t, :], st6[:, t, :]).then_inc(n.aggr, 1)
                    if g:
                        normalise(g - 1)
                normalise(NB - 1)
                dve.wait_ge(c.ident, 16)
                dve.wait_ge(c.const, 32)
                dve.tensor_copy(ident_b[:], ident_f[:])
                dve.tensor_copy(mask_b[:], mask_f[:])

            @block.scalar
            def _(act):
                act.preload_act_table_set("natural_log_exp_and_others")
                for g in range(NB + 1):
                    if g < NB:
                        four = slice(TB * g, TB * g + TB)
                        act.wait_ge(n.aggr, TB * (g + 1))
                        act.activation(lnv[:, four], mv[:, four, 1], ACT.Ln, bias=LN_EPS).then_inc(n.lnv, 1)
                        act.wait_ge(n.lnv, g + 1)
                        act.activation(rstd[:, four], lnv[:, four], ACT.Exp, scale=-0.5).then_inc(n.rstd, 1)
                    for t in range(TB * (g - 1), TB * g) if g else ():
                        act.wait_ge(n.tr, t + 1)
                        act.activation(xnT[:, :, t * P:t * P + P],
                                       ps[:, t % 4, :].rearrange("p (c n) -> p c n", c=KC), ACT.Copy).then_inc(n.ev, 1)

            @block.tensor
            def _(pe):
                pe.wait_ge(c.ident, 16)
                for t in range(B * ST):
                    pe.wait_ge(n.xn, t + 1)
                    if t >= 4:
                        pe.wait_ge(n.ev, t - 3)
                    for k in range(KC):
                        mm = pe.transpose(ps[:, t % 4, k * P:k * P + P], xt[:, t, k * P:k * P + P], ident_f[:])
                    mm.then_inc(n.tr, 1)

        units = ((1, 0), (1, 1), (0, 0), (0, 1))
        NU = len(units)
        kept, rep, w_in = (a.kept0, a.kept1), (a.rep0, a.rep1), (a.w0, a.w1)

        def copied(Gn, par):
            return (Gn - par) * (16 * NSPLIT) + 32 * NSPLIT

        def base_of(r, i):
            if isinstance(i, int):
                return (2 * i + r + 1) // (NG // B) * S
            return S if r else (i - 1) * S

        def tokens(base, tb, n=BLK):
            return slice(base + tb * BLK, base + tb * BLK + n) if isinstance(base, int) else ds(base + tb * BLK, n)

        with nc.Block() as block:
            @block.sync
            def _(sp):
                def split_out(Gn, par):
                    def send(u):
                        w, tb = units[u]
                        sp.wait_ge(a.lo, Gn * NU + u + 1)
                        if from_on(Gn, 1):
                            sp.wait_ge(rep[1 - par], copied(Gn - 1, 1 - par))
                        sp.dma_start(scratch[w, :, :, :, tb * BLK:tb * BLK + BLK].rearrange("s h r t -> (h r) s t"),
                                     parts[:, tb, :, :]).then_inc(kept[tb], 16)
                        if tb == 0:
                            return
                        for q in kept:
                            sp.wait_ge(q, Gn * 32 + 16 * (u // 2 + 1))
                        if from_on(Gn, 2):
                            sp.wait_ge(a.scores, Gn * (2 * NSC) - 2 * NSC)
                        for row, part in enumerate((Q_PARTS, K_PARTS)[w]):
                            sp.dma_start((q6, k6)[w][row * HD:row * HD + HD, par * GH:par * GH + GH, :],
                                         scratch[w, part].rearrange("h r t -> r h t")).then_inc(rep[par], 16)
                    return send

                def send_max(Q, r, x):
                    sp.wait_ge(a.m_split, Q + 1)
                    h = r * GH + x * QH
                    for row in range(3):
                        sp.dma_start(q6[QK + row:QK + row + 1, h:h + QH, :].rearrange("o h (i n) -> o (h i) n", n=P),
                                     m_parts[:, x, row, :]).then_inc(a.m_in, 16)

                def send_out(Q):
                    sp.wait_ge(a.act_rd, Q * RDQ + RDQ)
                    for h in range(QH):
                        sp.dma_start(att_o[ds(Q * QH + h, 1), :, :].rearrange("a r t -> (a r) t"),
                                     o_sb[VW * h:VW * h + HD, :]).then_inc(a.out, 16)
                    sp.dma_start(att_l[ds(Q * QH, QH), :], o_sb[HD:P:VW, :]).then_inc(a.out, 16)

                def quad(G, r, x, follows, i):
                    Q = G * 2 + x
                    if x == 0 and not (isinstance(i, int) and i == NG // 2 - 1):
                        sp.wait_ge(a.vproj, G * 2 + 2)
                        group = ds((i - 1) * 2 + r, 1) if not isinstance(i, int) else ds(2 + r, 1)
                        sp.dma_start(w3[:, r, :, :, :], w_qkv[group, :, :, :, :].rearrange("a p w c n -> (a p) w c n")).then_inc(w_in[r], 16)
                    if from_on(Q, 1):
                        send_out(Q - 1)
                    steps = {}
                    if follows and x == 0:
                        steps["h"] = split_out(G + 1, 1 - r)
                    if follows or x == 0:
                        steps["T"] = lambda n: send_max(Q + 1, r if x == 0 else 1 - r, 1 - x)
                    walk(ORDERS[x], steps)

                for r in range(2):
                    sp.dma_start(w3[:, r, :, :, :], w_qkv[r]).then_inc(w_in[r], 16)
                walk(PROJECT, {"h": split_out(0, 0)})
                send_max(0, 0, 0)
                turn_groups(sp, quad)
                send_out(2 * NG - 1)
                sp.wait_ge(a.out, 16 * OUTS * 2 * NG)

            @block.tensor
            def _(pe):
                def project(Gn, par, base, first):
                    def chunk(n):
                        u, k = n // KC, n % KC
                        w, tb = units[u] if first else (2, u)
                        if k == 0:
                            if first and u == 0:
                                pe.wait_ge(w_in[par], (Gn - par) * 8 + 16)
                                if from_on(Gn, 1):
                                    pe.wait_ge(a.vdone, Gn * 2)
                            elif first or u == 0:
                                pe.wait_ge(a.took, Gn * NU + (u if first else NU))
                            else:
                                pe.wait_ge(a.vdone, Gn * 2 + u)
                        mm = pe.matmul(pr_ps, w3[:, par, w, k, :], xnT[:, k, tokens(base, tb)], start=(k == 0), stop=(k == KC - 1))
                        if k == KC - 1:
                            mm.then_inc(a.proj if first else a.vproj, 1)
                    return chunk

                def turn_values(Gn):
                    def turn(u):
                        pe.wait_ge(a.vt, Gn * 2 + u + 1)
                        for c in range(TB):
                            mm = pe.transpose(pr_ps[:, c * P:c * P + P], vT[:, c * P:c * P + P], ident_f[:])
                        mm.then_inc(a.vtr, 1)
                    return turn

                def max_unit(Q, r, x, G):
                    def unit(n):
                        i, p, h, heads = MAX_UNITS[n]
                        w = max_width(i, p)
                        if n == 0 and x == 0:
                            pe.wait_ge(rep[r], copied(G, r))
                        bank = mx_ps[n % 2]
                        if isinstance(Q, int) and Q == 0:
                            bank = ps[:, FIRST_BANKS[n % len(FIRST_BANKS)], :]
                            if n >= len(FIRST_BANKS):
                                pe.wait_ge(a.max_rd, n + 1 - len(FIRST_BANKS))
                        elif n >= 2:
                            pe.wait_ge(a.max_rd, Q * NMAX + n - 1)
                        else:
                            pe.wait_ge(a.max_rd, Q * NMAX)
                        diag = BLK * p + w == (i + 1) * P
                        for y in range(heads):
                            head = r * GH + x * QH + h + y
                            mm = pe.matmul(bank[:, y * w:y * w + w], q6[0:QK, head, i * P:i * P + P],
                                           k6[0:QK, head, BLK * p:BLK * p + w], start=True, stop=not diag)
                            if diag:
                                mm = pe.matmul(bank[:, y * w + w - P:y * w + w], ident_b[:], mask_b[:, 0, :],
                                               start=False, stop=True)
                        mm.then_inc(a.max, 1)
                    return unit

                def max_turn(Q):
                    pe.wait_ge(a.m_ready, Q + 1)
                    pe.wait_ge(a.max_rd, Q * NMAX + NMAX - 1)
                    pe.transpose(mx_ps[0][0:QH * ST, 0:P], nm[:].rearrange("p h i -> p (h i)"), ident_f[:]).then_inc(a.max, 1)

                def quad(G, r, x, follows, i):
                    Q = G * 2 + x

                    def scores(u):
                        j, half, h, heads = SCORE_UNITS[u]
                        slot = st_ps[u % SLOTS]
                        if u == 0:
                            pe.wait_ge(a.m_in, Q * 48 + 48)
                        if u >= SLOTS:
                            pe.wait_ge(a.act_rd, Q * RDQ + READS[x][u - SLOTS])
                        elif from_on(Q, 1):
                            last = max(v for v in range(NSC) if v % SLOTS == u)
                            pe.wait_ge(a.act_rd, Q * RDQ - RDQ + READS[1 - x][last])
                        w = score_width(j, half)
                        hi = BLK * half + BLK
                        for y in range(heads):
                            head = r * GH + x * QH + h + y
                            diag = half == j // TB
                            mm = pe.matmul(slot[:, y * w:y * w + w], k6[:, head, j * P:j * P + P], q6[:, head, hi - w:hi],
                                           start=True, stop=not diag)
                            if diag:
                                mm = pe.matmul(slot[:, y * w:y * w + P], ident_b[:], mask_b[:, 1, :], start=False, stop=True)
                        mm.then_inc(a.scores, 1)

                    def weigh(n):
                        j, half = VALUE_UNITS[n]
                        pe.wait_ge(a.act_rd, Q * RDQ + READS[x][LAST_SCORE[n]])
                        if n == 0:
                            pe.wait_ge(a.va, Q + 1)
                        lo, hi = max(BLK * half, j * P), BLK * half + BLK
                        for h in range(QH):
                            mm = pe.matmul(o_ps[VW * h:VW * h + VW, lo:hi], va[:, j, VW * h:VW * h + VW],
                                           probs[:, j % 2, h, lo:hi], start=(j == 0), stop=(n in COPY_AFTER))
                        mm.then_inc(a.pv, 1)

                    steps = {"S": scores, "W": weigh}
                    if follows or x == 0:
                        steps["M"] = max_unit(Q + 1, r if x == 0 else 1 - r, 1 - x, G if x == 0 else G + 1)
                        steps["T"] = lambda n: max_turn(Q + 1)
                    if follows:
                        steps["P"] = project(G + 1, 1 - r, base_of(r, i), x == 0)
                        steps["t"] = turn_values(G + 1)
                    walk(ORDERS[x], steps)

                def first_chunk(n):
                    project(0, 0, 0, n < NU * KC)(n if n < NU * KC else n - NU * KC)

                walk(PROJECT, {"P": first_chunk, "t": turn_values(0)})
                for n in range(NMAX - 1):
                    max_unit(0, 0, 0, 0)(n)
                max_turn(0)
                turn_groups(pe, quad)

            @block.scalar
            def _(act):
                def take(Gn, par):
                    def out(u):
                        n = Gn * NU + u
                        act.wait_ge(a.proj, n + 1)
                        if from_on(n, 1):
                            act.wait_ge(a.swap, n)
                        act.activation(q_raw[:], pr_ps, ACT.Copy,
                                       scale=HD ** -0.5 if units[u][0] == 0 else 1.0).then_inc(a.took, 1)

                    def part1(u):
                        n = Gn * NU + u
                        act.wait_ge(a.rot, n + 1)
                        before = Gn * 2 + u // 2
                        if from_on(before, 1):
                            act.wait_ge(kept[units[u][1]], before * 16)
                        act.activation(parts[:, units[u][1], 0, :], q_rot[:], ACT.Copy).then_inc(a.hi, 1)

                    def part2(u):
                        act.wait_ge(a.rest, Gn * NU + u + 1)
                        act.activation(parts[:, units[u][1], 1, :], q_rest[:], ACT.Copy).then_inc(a.mid, 1)

                    def v_out(u):
                        act.wait_ge(a.vproj, Gn * 2 + u + 1)
                        if from_on(Gn * 2 + u, 1):
                            act.wait_ge(a.vtr, Gn * 2 + u)
                        act.activation(vT[:], pr_ps, ACT.Copy).then_inc(a.vt, 1)

                    def v_in(u):
                        act.wait_ge(a.vtr, Gn * 2 + u + 1)
                        if from_on(Gn, 2):
                            act.wait_ge(a.va, Gn * 2 - 2)
                        act.activation(vh[:, u * TB:u * TB + TB, par * GH:par * GH + GH, 0:HD],
                                       pr_ps.rearrange("p (c h d) -> p c h d", c=TB, d=HD), ACT.Copy).then_inc(a.vdone, 1)

                    return {"a": out, "e": part1, "g": part2, "v": v_out, "w": v_in}

                def values(G, r, x):
                    act.wait_ge(a.vdone, G * 2 + 2)
                    h = r * GH + x * QH
                    act.activation(va[:], vh[:, :, h:h + QH, :].rearrange("p j h v -> p j (h v)"), ACT.Copy).then_inc(a.va, 1)

                def quad(G, r, x, follows, i):
                    Q = G * 2 + x

                    def exps(u):
                        j, half, h, heads = SCORE_UNITS[u]
                        w, hi = score_width(j, half), BLK * half + BLK
                        if j >= 2:
                            act.wait_ge(a.pv, Q * NW + VALUE_UNITS.index((j - 2, half)) + 1)
                        elif from_on(Q, 1):
                            act.wait_ge(a.pv, Q * NW + j - 1)
                        act.wait_ge(a.scores, Q * NSC + u + 1)
                        act.activation(probs[:, j % 2, h:h + heads, hi - w:hi],
                                       st_ps[u % SLOTS][:, 0:heads * w].rearrange("p (x n) -> p x n", x=heads),
                                       ACT.Exp).then_inc(a.act_rd, 1)

                    def copy_out(w):
                        if w not in COPY_AFTER:
                            return
                        half = COPY_AFTER.index(w)
                        act.wait_ge(a.pv, Q * NW + w + 1)
                        if half == 0 and from_on(Q, 1):
                            act.wait_ge(a.out, Q * (16 * OUTS))
                        act.activation(o_sb[:, BLK * half:BLK * half + BLK], o_ps[:, BLK * half:BLK * half + BLK],
                                       ACT.Copy).then_inc(a.act_rd, 1)
                        if half and (follows or x == 0):
                            values(G + x, r ^ x, 1 - x)

                    steps = take(G + 1, 1 - r) if follows else {}
                    steps.update(S=exps, W=copy_out)
                    walk(ORDERS[x], steps)

                walk(PROJECT, take(0, 0))
                values(0, 0, 0)
                turn_groups(act, quad)

            @block.vector
            def _(dve):
                swap = [p ^ 1 for p in range(32)]

                def rope_and_split(Gn):
                    def turn(u):
                        n, tb = Gn * NU + u, units[u][1]
                        dve.wait_ge(a.took, n + 1)
                        if from_on(n, 1):
                            dve.wait_ge(a.sin, n)
                            dve.wait_ge(a.rot, n)
                        dve.tensor_tensor(t_cos[:], q_raw[:], cos_sin[:, 0, tb * BLK:tb * BLK + BLK], ALU.mult)
                        dve.stream_shuffle(q_swap[:], q_raw[:], swap).then_inc(a.swap, 1)

                    def add(u):
                        n = Gn * NU + u
                        dve.wait_ge(a.sin, n + 1)
                        dve.wait_ge(a.swap, n + 1)
                        if from_on(n, 1):
                            dve.wait_ge(a.hi, n)
                            dve.wait_ge(a.rest, n)
                        dve.tensor_tensor(q_rot[:], t_cos[:], t_sin[:], ALU.add).then_inc(a.rot, 1)

                    def rest(u):
                        n = Gn * NU + u
                        dve.wait_ge(a.hi, n + 1)
                        if from_on(n, 1):
                            dve.wait_ge(a.mid, n)
                            dve.wait_ge(a.lo, n)
                        dve.tensor_tensor(q_rest[:], q_rot[:], parts[:, units[u][1], 0, :], ALU.subtract).then_inc(a.rest, 1)

                    def last_part(u):
                        dve.wait_ge(a.mid, Gn * NU + u + 1)
                        dve.tensor_tensor(parts[:, units[u][1], 2, :], q_rest[:], parts[:, units[u][1], 1, :],
                                          ALU.subtract).then_inc(a.lo, 1)

                    return {"b": turn, "d": add, "f": rest, "h": last_part}

                def max_read(Q):
                    def read(n):
                        i, p, h, heads = MAX_UNITS[n]
                        w = max_width(i, p)
                        out = nm[:, h:h + heads, i:i + 1] if i < TB else mx[:, p, h:h + heads, i:i + 1]
                        dve.wait_ge(a.max, Q * NMAX + n + 1)
                        if n == 0 and from_on(Q, 1):
                            dve.wait_ge(a.m_ready, Q)
                        bank = mx_ps[n % 2]
                        if isinstance(Q, int) and Q == 0:
                            bank = ps[:, FIRST_BANKS[n % len(FIRST_BANKS)], :]
                        dve.tensor_reduce(out, bank[:, 0:heads * w].rearrange("p (x n) -> p x n", x=heads),
                                          AX.X, ALU.max, negate=True).then_inc(a.max_rd, 1)
                    return read

                def max_split(Q, x):
                    dve.wait_ge(a.max_rd, Q * NMAX + NMAX - 1)
                    dve.tensor_tensor(nm[:, :, 4:ST], mx[:, 0, :, 4:ST], mx[:, 1, :, 4:ST], ALU.min).then_inc(a.m_ready, 1)
                    turned = mx_ps[0][0:QH * ST, 0:P]
                    hi, mid, lo = (m_parts[:, x, row, :] for row in range(3))
                    dve.wait_ge(a.max, Q * NMAX + NMAX)
                    if from_on(Q, 2):
                        dve.wait_ge(a.m_in, Q * 48 - 48)
                    dve.tensor_copy(hi, turned).then_inc(a.m_chain, 1)
                    dve.wait_ge(a.m_chain, Q * 2 + 1)
                    dve.tensor_tensor(m_rest[:], turned, hi, ALU.subtract).then_inc(a.max_rd, 1)
                    dve.wait_ge(a.max_rd, Q * NMAX + NMAX)
                    dve.tensor_copy(mid, m_rest[:]).then_inc(a.m_chain, 1)
                    dve.wait_ge(a.m_chain, Q * 2 + 2)
                    dve.tensor_tensor(lo, m_rest[:], mid, ALU.subtract).then_inc(a.m_split, 1)

                def quad(G, r, x, follows, i):
                    Q = G * 2 + x
                    steps = rope_and_split(G + 1) if follows else {}
                    if follows or x == 0:
                        steps.update(M=max_read(Q + 1), T=lambda n: max_split(Q + 1, 1 - x))
                    walk(ORDERS[x], steps)

                walk(PROJECT, rope_and_split(0))
                for n in range(NMAX - 1):
                    max_read(0)(n)
                max_split(0, 0)
                turn_groups(dve, quad)

            @block.gpsimd
            def _(pool):
                def sines(Gn):
                    def sine(u):
                        n, tb = Gn * NU + u, units[u][1]
                        pool.wait_ge(a.swap, n + 1)
                        if from_on(n, 1):
                            pool.wait_ge(a.rot, n)
                        pool.tensor_tensor(t_sin[:], q_swap[:], cos_sin[:, 1, tb * BLK:tb * BLK + BLK], ALU.mult).then_inc(a.sin, 1)
                    return sine

                def quad(G, r, x, follows, i):
                    if follows:
                        walk(ORDERS[x], {"b": sines(G + 1)})

                walk(PROJECT, {"b": sines(0)})
                turn_groups(pool, quad)
        clear(nc, (*a, *c, *n))


def layernorm_tail(act, mv, lnv, rstd, t, aggr, lnv_done, rstd_done, n):
    act.wait_ge(aggr, n)
    act.activation(lnv[:, t:t + 1], mv[:, t, 1:2], ACT.Ln, bias=LN_EPS).then_inc(lnv_done, 1)
    act.wait_ge(lnv_done, n)
    act.activation(rstd[:, t:t + 1], lnv[:, t:t + 1], ACT.Exp, scale=-0.5).then_inc(rstd_done, 1)


def layernorm_stats(dve, src, st6, mv, t, stats, aggr, n):
    dve.bn_stats(st6[:, t, :], src).then_inc(stats, 1)
    dve.wait_ge(stats, n)
    dve.bn_aggr(mv[:, t, :], st6[:, t, :]).then_inc(aggr, 1)


NC = 64
HIT = 0.01
TEMPERATURE = 0.1


def dense_stage(nc, ctx, ps, keep, x1, dn, x, att_o, att_l, wo, w_dense, w_cent, bias,
                assignments, cluster_ids, later):
    s = semaphores(nc, ctx, "d", "wo w o0 o1 l0 l1 x0 x1 lnl inv div y st1 ag1 ln1 rs1 up add st2 ag2 ln2 rs2 xn tr ev "
                   "dn lg dn_rd top nb exp tot hit hits query later ids ones numbers one_hot count sel spread rows row_mask")
    o_load, l_load, x_load = (s.o0, s.o1), (s.l0, s.l1), (s.x0, s.x1)
    T = B * ST
    with ExitStack() as mem:
        def sb(name, shape, dt=F32):
            return mem.enter_context(nc.sbuf_tensor(name, shape, dt))

        wo_sb = sb("wo_sb", [P, KC, D])
        wd_sb = sb("wd_sb", [P, KC, D])
        wc_sb = sb("wc_sb", [P, KC, NC])
        bias_sb = sb("bias_sb", [P, D])
        oT = sb("oT", [P, 2, KC, BLK])
        lT = sb("lT", [P, 2, KC, BLK])
        x_sb = sb("x_sb", [P, 2 * TB, D])
        up = sb("up", [P, 2, D])
        xn = sb("xn", [P, 2, D])
        xnT = sb("d_xnT", [P, 4, KC, P])
        st1, mv1, ln1, rs1 = sb("st1", [P, T, 6]), sb("mv1", [P, T, 2]), sb("ln1", [P, T]), sb("rs1", [P, T])
        st2, mv2, ln2, rs2 = sb("st2", [P, T, 6]), sb("mv2", [P, T, 2]), sb("ln2", [P, T]), sb("rs2", [P, T])
        top, nb = sb("top", [P, T]), sb("nb", [P, T])
        ex, tot, inv = sb("ex", [P, 2, NC]), sb("tot", [P, T]), sb("d_inv", [P, T])
        hit = sb("hit", [P, 2, NC])
        ids = sb("ids", [NC, 1])
        assigned, numbers, one_hot = sb("assigned", [NC, D], I32), sb("numbers", [NC, D]), sb("one_hot", [NC, D])
        ones, chosen, chosen_b = sb("ones", [P, P]), sb("chosen", [NC, 1]), sb("chosen_b", [NC, P])

        with nc.Block() as block:
            @block.sync
            def _(sp):
                def load_block(g):
                    if g >= 2:
                        sp.wait_ge(s.y, TB * (g - 1))
                    at = g * BLK % S
                    for c in range(KC):
                        head = g * BLK // S * H + GH * c
                        sp.dma_start(oT[:, g % 2, c, :], att_o[head:head + GH, :, at:at + BLK]
                                     .rearrange("h r t -> (h r) t")).then_inc(o_load[g % 2], 16)
                        sp.dma_start(lT[:, g % 2, c, :], att_l[head:head + GH, at:at + BLK].unsqueeze(1)
                                     .broadcast_to([GH, HD, BLK])).then_inc(l_load[g % 2], 16)
                    if g >= 2:
                        sp.wait_ge(s.add, TB * (g - 1))
                    sp.dma_start(x_sb[:, g % 2 * TB:g % 2 * TB + TB, :],
                                 x[g].rearrange("(t p) d -> p t d", p=P)).then_inc(x_load[g % 2], 16)

                sp.dma_start(wo_sb[:], wo.rearrange("(c p) n -> p c n", p=P)).then_inc(s.wo, 16)
                load_block(0)
                for dst, src in ((wd_sb, w_dense), (wc_sb, w_cent)):
                    sp.dma_start(dst[:], src.rearrange("(c p) n -> p c n", p=P)).then_inc(s.w, 16)
                sp.dma_start(bias_sb[:], bias.rearrange("(a n) -> a n", a=1).broadcast_to([P, D])).then_inc(s.w, 16)
                for g in range(1, NB):
                    load_block(g)
                sp.dma_start(ids[:], cluster_ids).then_inc(s.ids, 16)
                sp.dma_start(assigned[:], assignments.rearrange("(a n) -> a n", a=1).broadcast_to([NC, D])).then_inc(s.ids, 16)
                for dst, src in later:
                    sp.dma_start(dst, src).then_inc(s.later, 16)
                sp.wait_ge(s.later, 16 * len(later))

            @block.tensor
            def _(pe):
                pe.wait_ge(s.wo, 16)
                for i in range(T + 3):
                    if i < T:
                        if i % TB == 0:
                            pe.wait_ge(s.div, KC * (i // TB + 1))
                        if i >= 2:
                            pe.wait_ge(s.up, i - 1)
                        for k in range(KC):
                            mm = pe.matmul(ps[:, i % 2, :], oT[:, i // TB % 2, k, i % TB * P:i % TB * P + P], wo_sb[:, k, :],
                                           start=(k == 0), stop=(k == KC - 1))
                        mm.then_inc(s.y, 1)
                    t = i - 2
                    if 0 <= t < T:
                        pe.wait_ge(s.xn, t + 1)
                        if t >= 2:
                            pe.wait_ge(s.ev, t - 1)
                        for k in range(KC):
                            mm = pe.transpose(ps[:, 2 + t % 2, k * P:k * P + P], xn[:, t % 2, k * P:k * P + P], keep.ident[:])
                        mm.then_inc(s.tr, 1)
                    t = i - 3
                    if 0 <= t < T:
                        if t == 0:
                            pe.wait_ge(s.w, 48)
                        pe.wait_ge(s.ev, t + 1)
                        if t >= 2:
                            pe.wait_ge(s.exp, t - 1)
                        for k in range(KC):
                            mm = pe.matmul(ps[:, 6 + t % 2, 0:NC], xnT[:, t % 4, k, :], wc_sb[:, k, :],
                                           start=(k == 0), stop=(k == KC - 1))
                        mm.then_inc(s.lg, 1)
                        if t >= 2:
                            pe.wait_ge(s.dn_rd, t - 1)
                        for k in range(KC):
                            mm = pe.matmul(ps[:, 4 + t % 2, :], xnT[:, t % 4, k, :], wd_sb[:, k, :],
                                           start=(k == 0), stop=(k == KC - 1))
                        mm.then_inc(s.dn, 1)
                pe.wait_ge(s.hits, T + 1)
                pe.matmul(ps[0:NC, 0, 0:1], keep.hits[:], ones[:, 0:1], start=True, stop=True).then_inc(s.count, 1)
                pe.wait_ge(s.one_hot, 1)
                pe.wait_ge(s.spread, 1)
                pe.matmul(ps[:, 1, :], chosen_b[:], one_hot[:], start=True, stop=True).then_inc(s.rows, 1)

            @block.scalar
            def _(act):
                def invert(g):
                    act.wait_ge(l_load[g % 2], 16 * KC * (g // 2 + 1))
                    for c in range(KC):
                        act.activation(lT[:, g % 2, c, :], lT[:, g % 2, c, :], ACT.Ln).then_inc(s.lnl, 1)
                    for c in range(KC):
                        act.wait_ge(s.lnl, KC * g + c + 1)
                        act.activation(lT[:, g % 2, c, :], lT[:, g % 2, c, :], ACT.Exp, scale=-1.0).then_inc(s.inv, 1)

                act.preload_act_table_set("natural_log_exp_and_others")
                invert(0)
                for i in range(T + 4):
                    if i % TB == 1 and i // TB + 1 < NB:
                        invert(i // TB + 1)
                    if i < T:
                        layernorm_tail(act, mv1, ln1, rs1, i, s.ag1, s.ln1, s.rs1, i + 1)
                    t = i - 4
                    if 0 <= t < T:
                        act.wait_ge(s.nb, t + 1)
                        if t >= 2:
                            act.wait_ge(s.hit, t - 1)
                        act.activation(ex[:, t % 2, :], ps[:, 6 + t % 2, 0:NC], ACT.Exp, bias=nb[:, t:t + 1],
                                       scale=1.0 / TEMPERATURE, accum_out=tot[:, t:t + 1]).then_inc(s.exp, 1)
                    if i < T:
                        layernorm_tail(act, mv2, ln2, rs2, i, s.ag2, s.ln2, s.rs2, i + 1)
                    t = i - 2
                    if 0 <= t < T:
                        act.wait_ge(s.tr, t + 1)
                        if t >= 4:
                            act.wait_ge(s.dn, t - 3)
                        act.activation(xnT[:, t % 4, :, :].rearrange("p c n -> p (c n)"), ps[:, 2 + t % 2, :],
                                       ACT.Copy).then_inc(s.ev, 1)

            @block.gpsimd
            def _(pool):
                for t in range(T):
                    if t % TB == 0:
                        pool.wait_ge(x_load[t // TB % 2], 16 * (t // TB // 2 + 1))
                    pool.wait_ge(s.up, t + 1)
                    pool.tensor_tensor(x1[:, t, :], x_sb[:, t % (2 * TB), :], up[:, t % 2, :], ALU.add).then_inc(s.add, 1)

            @block.vector
            def _(dve):
                def divide(g):
                    dve.wait_ge(o_load[g % 2], 16 * KC * (g // 2 + 1))
                    for c in range(KC):
                        dve.wait_ge(s.inv, KC * g + c + 1)
                        dve.tensor_tensor(oT[:, g % 2, c, :], oT[:, g % 2, c, :], lT[:, g % 2, c, :], ALU.mult).then_inc(s.div, 1)

                dve.memset(keep.hits[:], 0.0).then_inc(s.hits, 1)
                dve.memset(ones[:], 1.0).then_inc(s.ones, 1)
                divide(0)
                for i in range(T + 4):
                    t = i - 4
                    if i % TB == 2 and i // TB + 1 < NB:
                        divide(i // TB + 1)
                    if 0 <= t < T:
                        dve.wait_ge(s.lg, t + 1)
                        dve.tensor_reduce(top[:, t:t + 1], ps[:, 6 + t % 2, 0:NC], AX.X, ALU.max).then_inc(s.top, 1)
                    if i < T:
                        dve.wait_ge(s.y, i + 1)
                        layernorm_stats(dve, ps[:, i % 2, :], st1, mv1, i, s.st1, s.ag1, i + 1)
                    if 0 <= t < T:
                        dve.wait_ge(s.top, t + 1)
                        dve.tensor_scalar(nb[:, t:t + 1], top[:, t:t + 1], -1.0 / TEMPERATURE, None,
                                          ALU.mult).then_inc(s.nb, 1)
                        dve.wait_ge(s.dn, t + 1)
                        dve.tensor_tensor(dn[:, t, :], ps[:, 4 + t % 2, :], bias_sb[:], ALU.add).then_inc(s.dn_rd, 1)
                    if i < T:
                        dve.wait_ge(s.ag1, i + 1)
                        dve.wait_ge(s.rs1, i + 1)
                        if i >= 2:
                            dve.wait_ge(s.add, i - 1)
                        dve.tensor_scalar(up[:, i % 2, :], ps[:, i % 2, :], mv1[:, i, 0:1], rs1[:, i:i + 1],
                                          ALU.subtract, ALU.mult).then_inc(s.up, 1)
                    if 0 <= t < T:
                        dve.wait_ge(s.exp, t + 1)
                        dve.reciprocal(inv[:, t:t + 1], tot[:, t:t + 1]).then_inc(s.tot, 1)
                        dve.wait_ge(s.tot, t + 1)
                        if t >= 2:
                            dve.wait_ge(s.hits, t)
                            dve.wait_ge(s.query, t - 1)
                        dve.tensor_scalar(hit[:, t % 2, :], ex[:, t % 2, :], inv[:, t:t + 1], HIT,
                                          ALU.mult, ALU.is_gt).then_inc(s.hit, 1)
                        dve.wait_ge(s.hit, t + 1)
                        dve.tensor_reduce(keep.query_hit[:, t:t + 1], hit[:, t % 2, :], AX.X, ALU.max).then_inc(s.query, 1)
                        dve.wait_ge(s.hits, t + 1)
                        dve.tensor_tensor(keep.hits[:], keep.hits[:], hit[:, t % 2, :], ALU.max).then_inc(s.hits, 1)
                    if i < T:
                        dve.wait_ge(s.add, i + 1)
                        layernorm_stats(dve, x1[:, i, :], st2, mv2, i, s.st2, s.ag2, i + 1)
                        dve.wait_ge(s.ag2, i + 1)
                        dve.wait_ge(s.rs2, i + 1)
                        if i >= 2:
                            dve.wait_ge(s.tr, i - 1)
                        dve.tensor_scalar(xn[:, i % 2, :], x1[:, i, :], mv2[:, i, 0:1], rs2[:, i:i + 1],
                                          ALU.subtract, ALU.mult).then_inc(s.xn, 1)
                dve.wait_ge(s.ids, 32)
                dve.tensor_copy(numbers[:], assigned[:]).then_inc(s.numbers, 1)
                dve.wait_ge(s.numbers, 1)
                dve.tensor_scalar(one_hot[:], numbers[:], ids[:, 0:1], None, ALU.is_equal).then_inc(s.one_hot, 1)
                dve.wait_ge(s.count, 1)
                dve.tensor_scalar(chosen[:], ps[0:NC, 0, 0:1], 0.0, None, ALU.is_gt).then_inc(s.sel, 1)
                dve.wait_ge(s.sel, 1)
                dve.tensor_scalar(chosen_b[:], ones[0:NC, :], chosen[:, 0:1], None, ALU.mult).then_inc(s.spread, 1)
                dve.wait_ge(s.rows, 1)
                dve.tensor_copy(keep.rows[:], ps[:, 1, :]).then_inc(s.row_mask, 1)
        clear(nc, s)


DI = 1024
MT = DI // P
NS = 16
RK = 32
CONV = 4
NX = RK + 2 * NS
RMS_EPS = 1e-6
ROWS_AT_ONCE = 4
NBC = 2 * NS // ROWS_AT_ONCE
X2_LAG = 5
RING = 4
SPB = S // BLK


def tile(t, m):
    return t[:, m, :] if isinstance(m, int) else t[:, ds(m, 1), :].rearrange("p a n -> p (a n)")


def col(t, m, n=None):
    if n is not None:
        return tile(t, m)[:, n:n + 1]
    return t[:, m:m + 1] if isinstance(m, int) else t[:, ds(m, 1)]


def scan_weights(nc, ctx, t):
    def sb(name, shape, dt=F32):
        return ctx.enter_context(nc.sbuf_tensor(name, shape, dt))

    w = namedtuple("weights", "cw cb xw nw mean dtw na dp")(
        sb("cw", [P, MT, CONV]), sb("cb", [P, MT]), sb("xw", [P, MT, NX]), sb("nw", [NX, 1]), sb("mean", [NX, NX]),
        sb("dtw", [RK + 1, DI]), sb("na", [P, MT, NS]), sb("dp", [P, MT]))
    return w, ((w.cw[:], t["L1_attn_conv_w"].rearrange("(m p) k -> p m k", p=P)),
               (w.cb[:], t["conv_b"]),
               (w.xw[:], t["w_x"].rearrange("(m p) n -> p m n", p=P)),
               (w.nw[:], t["norm_w"]),
               (w.mean[:], t["mean"]),
               (w.dtw[:], t["w_dt"]),
               (w.na[:], t["L1_attn_A_log"].rearrange("(m p) n -> p m n", p=P)),
               (w.dp[:], t["d_skip"]))


def scan_stage(nc, ctx, ps, keep, work, xnT, weights_in, w_in, bc, x2_out, y_out):
    r = semaphores(nc, ctx, "r", "a neg dt_ones")
    i1 = semaphores(nc, ctx, "n", "masked st1 ag1 ln1 rs1 up x2 st2 ag2 ln2 rs2 xn tr ev store")
    s = semaphores(nc, ctx, "m", "wx0 wx1 wz0 wz1 px padded head tap conv xc pz zs xw_sel xp sq mean lnx rsx "
                   "dt_in bc_sb bc_out dtm dt_sel skip_sel ab ex lg dts u skip da dbx h carry hc ys gate y0 y1")
    bc_load = [ctx.enter_context(nc.semaphore(f"m_bc{i}")) for i in range(NBC)]
    wx, wz, y_store = (s.wx0, s.wx1), (s.wz0, s.wz1), (s.y0, s.y1)
    PY, PX, PZ, PDT, PXP, PMEAN = 0, (2, 7), 3, 4, 5, 6
    with ExitStack() as mem:
        def sb(name, shape, dt=F32):
            return mem.enter_context(nc.sbuf_tensor(name, shape, dt))

        cw, cb, xw, nw, mean, dtw, na, dp = weights_in
        skip = sb("skip", [P, 2, P])
        dtm_w = sb("dtm_w", [RK + 1, 2, P])
        conv_carry = sb("conv_carry", [P, MT, CONV - 1])
        state = sb("state", [P, MT, NS])
        x2 = work[:, 0:B * ST, :]
        dn = work[:, B * ST:2 * B * ST, :]
        bcb = work
        xc = sb("xc", [P, MT, BLK])
        sz = sb("sz", [P, MT, BLK])
        dts = sb("dts", [P, 2, BLK])
        u = sb("u", [P, 2, BLK])
        soft = keep.rows
        wxr = sb("wxr", [P, 2, KC, P])
        wzr = sb("wzr", [P, 2, KC, P])
        pad = sb("pad", [P, 2, BLK + CONV - 1])
        acc = sb("acc", [P, 2, BLK])
        xw_one = sb("xw_one", [P, 2, P])
        dtT = sb("dtT", [RK + 1, BLK])
        bcT = sb("bcT", [NX, BLK])
        da = sb("da", [P, RING, BLK])
        dbx = sb("dbx", [P, RING, BLK])
        hs = sb("hs", [P, RING, BLK])
        hc = sb("hc", [P, RING, BLK])
        yo = sb("yo", [P, 2, BLK])
        T2 = B * ST
        st1, mv1, ln1, rs1 = sb("n_st1", [P, T2, 6]), sb("n_mv1", [P, T2, 2]), sb("n_ln1", [P, T2]), sb("n_rs1", [P, T2])
        st2, mv2, ln2, rs2 = sb("n_st2", [P, T2, 6]), sb("n_mv2", [P, T2, 2]), sb("n_ln2", [P, T2]), sb("n_rs2", [P, T2])
        up, xn = da[:, 0:2, :], dbx[:, 0:2, :]

        def turns(eng, k, turn):
            apart = 3 if k == 0 else 1
            for m in range(apart):
                turn(k, m, m % 2)
            with eng.Fori(0, (MT - 1 - apart) // 2) as i:
                for step in range(2):
                    turn(k, i * 2 + (apart + step), (apart + step) % 2)
            turn(k, MT - 1, 1)

        def start(x2_tile, turn):
            m = 0
            for i in range(T2 + X2_LAG):
                x2_tile(i)
                if i >= TB + X2_LAG - 1 and (i - TB - X2_LAG + 1) % 2 == 0:
                    turn(-1, m, m % 2)
                    m += 1
            for m in range(m, MT):
                turn(-1, m, m % 2)

        def kind(k, m):
            first, last = isinstance(m, int) and m == 0, isinstance(m, int) and m == MT - 1
            return k >= 0, k < NB - 1, (k >= 0 if first else k < NB - 1), first, last

        with nc.Block() as block:
            @block.sync
            def _(sp):
                def load(k, m, par):
                    T = k * MT + m
                    _, px, pz, first, _ = kind(k, m)
                    if px:
                        if from_on(T + MT, 2):
                            sp.wait_ge(s.px, T + MT - 1)
                        sp.dma_start(wxr[:, par, :, :], weight_tile(m)).then_inc(wx[par], 16)
                    if pz:
                        if from_on(T + MT - 1, 2):
                            sp.wait_ge(s.pz, T + MT - 2)
                        sp.dma_start(wzr[:, 1 - par, :, :], weight_tile(2 * MT - 1 if first else m + (MT - 1))).then_inc(wz[1 - par], 16)

                def weight_tile(i):
                    return w_in[i] if isinstance(i, int) else w_in[ds(i, 1), :, :, :].rearrange("a p c n -> (a p) c n")

                def turn(k, m, par):
                    scans, px, _, first, last = kind(k, m)
                    if last and px:
                        load(k + 1, 0, 0)
                    elif not last:
                        load(k, m + 1, 1 - par)
                    if scans and from_on(k * MT + m, 1):
                        store(k, m, par)
                    if last and px:
                        broadcast(k + 1)

                def store(k, m, par):
                    first = isinstance(m, int) and m == 0
                    sp.wait_ge(s.gate, k * MT + m)
                    kb, mb = (k - 1, MT - 1) if first else (k, m - 1)
                    dst = y_out[kb, :, mb, :] if isinstance(mb, int) else y_out[kb, :, ds(mb, 1), :].rearrange("p a n -> p (a n)")
                    sp.dma_start(dst, yo[:, 1 - par, :]).then_inc(y_store[1 - par], 16)

                def broadcast(j):
                    sp.wait_ge(s.bc_sb, j + 1)
                    if j == 0:
                        sp.wait_ge(i1.store, 16 * NB)
                    if j:
                        for q in bc_load:
                            sp.wait_ge(q, 16 * j)
                    sp.dma_start(bc[:, :], bcT[RK:NX, :]).then_inc(s.bc_out, 16)
                    sp.wait_ge(s.bc_out, 16 * (j + 1))
                    for i in range(NBC):
                        n = (i // 2) * ROWS_AT_ONCE
                        row = (i % 2) * NS + n
                        if j:
                            sp.wait_ge((s.dbx, s.hc)[i % 2], ((j * MT) - 1) * NS + n + ROWS_AT_ONCE)
                        sp.dma_start(bcb[:, row:row + ROWS_AT_ONCE, :], bc[row:row + ROWS_AT_ONCE, :].unsqueeze(0)
                                     .broadcast_to([P, ROWS_AT_ONCE, BLK])).then_inc(bc_load[i], 16)

                def x2_tile(i):
                    t = i - X2_LAG
                    if 0 <= t and t % TB == TB - 1:
                        sp.wait_ge(i1.x2, t + 1)
                        sp.dma_start(x2_out[t // TB].rearrange("(t p) d -> p t d", p=P),
                                     x2[:, t + 1 - TB:t + 1, :]).then_inc(i1.store, 16)

                load(-1, 0, 0)
                start(x2_tile, turn)
                for k in range(NB):
                    turns(sp, k, turn)
                sp.wait_ge(i1.store, 16 * NB)
                store(NB, 0, 0)
                for q in y_store:
                    sp.wait_ge(q, 16 * NB * MT // 2)

            @block.tensor
            def _(pe):
                def project_x(k, m, par, c):
                    T = k * MT + m
                    if c == 0:
                        pe.wait_ge(wx[par], weights(k, m, par))
                        if k < 0:
                            pe.wait_ge(i1.ev, TB)
                        if from_on(T + MT, 2):
                            pe.wait_ge(s.tap, T + MT - 1)
                            pe.wait_ge(s.padded, T + MT - 1)
                    mm = pe.matmul(ps[:, PX[par], :], wxr[:, par, c, :], xnT[:, c, (k + 1) * BLK:(k + 2) * BLK],
                                   start=(c == 0), stop=(c == KC - 1))
                    if c == KC - 1:
                        mm.then_inc(s.px, 1)

                def project_z(k, m, par, c):
                    T = k * MT + m
                    first = kind(k, m)[3]
                    j = k if first else k + 1
                    if c == 0:
                        pe.wait_ge(wz[1 - par], weights_z(k, m, par))
                        if from_on(T + MT - 1, 1):
                            pe.wait_ge(s.zs, T + MT - 1)
                    mm = pe.matmul(ps[:, PZ, :], wzr[:, 1 - par, c, :], xnT[:, c, j * BLK:(j + 1) * BLK],
                                   start=(c == 0), stop=(c == KC - 1))
                    if c == KC - 1:
                        mm.then_inc(s.pz, 1)

                def step_sizes(q, par, first):
                    if from_on(q, 1):
                        pe.wait_ge(s.dts, q)
                    if first:
                        pe.wait_ge(s.dt_in, q // MT + 1)
                    pe.wait_ge(s.dt_sel, q + 1)
                    pe.matmul(ps[:, PDT, :], dtm_w[:, par, :], dtT[:], start=True, stop=True).then_inc(s.dtm, 1)

                def turn(k, m, par):
                    T = k * MT + m
                    scans, px, pz, first, last = kind(k, m)
                    if scans:
                        if from_on(T, 2):
                            pe.wait_ge(s.gate, T - 1)
                        pe.wait_ge(s.skip_sel, T + 1)
                        pe.matmul(ps[:, PY + par, :], skip[:, par, :], tile(xc, m), start=True, stop=False).then_inc(s.skip, 1)
                    for n in range(NS):
                        for c in ((n,) if not last else (2 * n, 2 * n + 1)):
                            if px and c < KC:
                                project_x(k, m, par, c)
                        c = n - (NS - KC if last else KC + 1)
                        if pz and 0 <= c < KC:
                            project_z(k, m, par, c)
                        if scans and not last and n == KC:
                            step_sizes(T + 1, 1 - par, False)
                        if px and n == (9 if last else NS - 1):
                            pe.wait_ge(s.xc, T + MT + 1)
                            pe.wait_ge(s.xw_sel, T + MT + 1)
                            if first and scans:
                                pe.wait_ge(s.dt_in, k + 1)
                                pe.wait_ge(s.bc_sb, k + 1)
                            pe.matmul(ps[:, PXP, :], xw_one[:, par, :], tile(xc, m), start=first, stop=last).then_inc(s.xp, 1)
                        if last and px and n == 10:
                            pe.wait_ge(s.sq, k + 2)
                            pe.matmul(ps[0:NX, PMEAN, :], mean[:], soft[0:NX, :], start=True, stop=True).then_inc(s.mean, 1)
                        if last and px and n == 12:
                            step_sizes(T + 1, 0, True)
                        if scans:
                            pe.wait_ge(s.hc, T * NS + n + 1)
                            pe.matmul(ps[:, PY + par, :], keep.ident[:], hc[:, n % RING, :],
                                      start=False, stop=(n == NS - 1)).then_inc(s.ys, 1)

                def x2_tile(i):
                    t = i - X2_LAG
                    if 0 <= t < T2:
                        pe.wait_ge(i1.xn, t + 1)
                        if t >= 2:
                            pe.wait_ge(i1.ev, t - 1)
                        for k in range(KC):
                            mm = pe.transpose(ps[:, PY + t % 2, k * P:k * P + P], xn[:, t % 2, k * P:k * P + P], keep.ident[:])
                        mm.then_inc(i1.tr, 1)

                start(x2_tile, turn)
                pe.wait_ge(i1.ev, T2)
                for k in range(NB):
                    turns(pe, k, turn)

            @block.scalar
            def _(act):
                def take_x(k, m, par):
                    U = (k + 1) * MT + m
                    act.wait_ge(s.px, U + 1)
                    if from_on(U, 2):
                        act.wait_ge(s.conv, CONV * (U - 1))
                        act.wait_ge(s.xc, U - 1)
                    act.activation(pad[:, par, CONV - 1:], ps[:, PX[par], :], ACT.Copy).then_inc(s.padded, 1)
                    act.activation(acc[:, par, :], ps[:, PX[par], :], ACT.Identity, bias=col(cb, m),
                                   scale=col(cw, m, CONV - 1)).then_inc(s.tap, 1)

                def silu_z(T, m):
                    act.wait_ge(s.pz, T + MT)
                    if from_on(T, 1):
                        act.wait_ge(s.gate, T)
                    act.activation(tile(sz, m), ps[:, PZ, :], ACT.Silu).then_inc(s.zs, 1)

                def silus(k, m, par):
                    T = k * MT + m
                    scans, px, pz, first, last = kind(k, m)
                    if px:
                        act.wait_ge(s.conv, CONV * (T + MT + 1))
                        if scans:
                            act.wait_ge(s.skip, T + 1)
                            act.wait_ge(s.u, T + 1)
                        act.activation(tile(xc, m), acc[:, par, :], ACT.Silu).then_inc(s.xc, 1)
                    if pz and not last:
                        silu_z(T, MT - 1 if first else m - 1)
                    if px or pz:
                        act.preload_act_table_set("natural_log_exp_and_others")

                def select(q, m, par):
                    if from_on(q, 2):
                        act.wait_ge(s.dtm, q - 1)
                        act.wait_ge(s.skip, q - 1)
                    act.activation(dtm_w[:, par, :], dtw[:, m * P:m * P + P] if isinstance(m, int)
                                   else dtw[:, ds(m * P, P)], ACT.Copy).then_inc(s.dt_sel, 1)
                    act.activation(skip[:, par, :], keep.ident[:], ACT.Copy, scale=col(dp, m)).then_inc(s.skip_sel, 1)

                def softplus(q):
                    act.wait_ge(s.dtm, q + 1)
                    if from_on(q, 1):
                        act.wait_ge(s.dts, q)
                    act.activation(soft[:], ps[:, PDT, :], ACT.Abs).then_inc(s.ab, 1)
                    act.wait_ge(s.ab, q + 1)
                    act.activation(soft[:], soft[:], ACT.Exp, scale=-1.0).then_inc(s.ex, 1)
                    act.wait_ge(s.ex, q + 1)
                    act.activation(soft[:], soft[:], ACT.Ln, bias=1.0).then_inc(s.lg, 1)

                def keep_state(T, m, n):
                    act.wait_ge(s.h, T * NS + n + 1)
                    act.activation(col(state, m, n), hs[:, n % RING, BLK - 1:BLK], ACT.Copy).then_inc(s.carry, 1)

                def turn(k, m, par):
                    T = k * MT + m
                    scans, px, pz, first, last = kind(k, m)
                    for n in range(NS):
                        if first and scans and n == 4:
                            silu_z(T - 1, MT - 2)
                            act.preload_act_table_set("natural_log_exp_and_others")
                        if px and n == (8 if last else 9):
                            take_x(k, m, par)
                        if n == 5 and (scans and not last or last and px):
                            select(T + 1, 0 if last else m + 1, 1 - par)
                        if n == (10 if last else 14):
                            silus(k, m, par)
                        if scans and not last and n == 10:
                            softplus(T + 1)
                        if px and n == 5:
                            if k < 0 and first:
                                act.wait_ge(r.dt_ones, 2)
                            if from_on(T + MT, 2):
                                act.wait_ge(s.xp, T + MT - 1)
                            act.activation(xw_one[:, par, 0:NX], tile(xw, m), ACT.Copy).then_inc(s.xw_sel, 1)
                        if last and px and n == 11:
                            act.wait_ge(s.xp, (k + 2) * MT)
                            act.activation(soft[0:NX, :], ps[0:NX, PXP, :], ACT.Square).then_inc(s.sq, 1)
                        if last and px and n == 13:
                            act.wait_ge(s.mean, k + 2)
                            act.activation(soft[0:NX, :], ps[0:NX, PMEAN, :], ACT.Ln, bias=RMS_EPS).then_inc(s.lnx, 1)
                            act.wait_ge(s.lnx, k + 2)
                            act.activation(soft[0:NX, :], soft[0:NX, :], ACT.Exp, scale=-0.5).then_inc(s.rsx, 1)
                        if last and px and n == 15:
                            act.wait_ge(s.dt_in, k + 2)
                            act.wait_ge(s.bc_sb, k + 2)
                            softplus(T + 1)
                        if scans:
                            if n == 0:
                                act.wait_ge(s.dts, T + 1)
                            if n >= RING or from_on(T, 1):
                                act.wait_ge(s.h, T * NS + n + 1 - RING)
                            act.activation(da[:, n % RING, :], dts[:, par, :], ACT.Exp,
                                           scale=col(na, m, n)).then_inc(s.da, 1)
                            if n < RING - 1:
                                if keeps((k - 1) if first else k) and from_on(T, 1):
                                    keep_state(T - 1, MT - 1 if first else m - 1, NS + n + 1 - RING)
                            elif keeps(k):
                                keep_state(T, m, n + 1 - RING)

                def x2_tile(i):
                    if i < T2:
                        layernorm_tail(act, mv1, ln1, rs1, i, i1.ag1, i1.ln1, i1.rs1, i + 1)
                    t = i - 3
                    if 0 <= t < T2:
                        layernorm_tail(act, mv2, ln2, rs2, t, i1.ag2, i1.ln2, i1.rs2, t + 1)
                    t = i - X2_LAG
                    if 0 <= t < T2:
                        act.wait_ge(i1.tr, t + 1)
                        act.activation(xnT[:, :, t * P:t * P + P], ps[:, PY + t % 2, :].rearrange("p (c n) -> p c n", c=KC),
                                       ACT.Copy).then_inc(i1.ev, 1)

                act.preload_act_table_set("natural_log_exp_and_others")
                act.activation(na[:], na[:], ACT.Exp).then_inc(r.a, 1)
                start(x2_tile, turn)
                act.wait_ge(r.neg, 1)
                for k in range(NB):
                    turns(act, k, turn)

            @block.gpsimd
            def _(pool):
                def drive(q, m, par):
                    pool.wait_ge(s.dts, q + 1)
                    if from_on(q, 2):
                        pool.wait_ge(s.dbx, (q - 1) * NS)
                    pool.tensor_tensor(u[:, par, :], dts[:, par, :], tile(xc, m), ALU.mult).then_inc(s.u, 1)

                def turn(k, m, par):
                    T = k * MT + m
                    scans, px, pz, first, last = kind(k, m)
                    if scans:
                        for n in range(NS):
                            pool.wait_ge(s.h, T * NS + n + 1)
                            if first and n % ROWS_AT_ONCE == 0:
                                pool.wait_ge(bc_load[2 * (n // ROWS_AT_ONCE) + 1], 16 * (k + 1))
                            if n >= RING or from_on(T, 1):
                                pool.wait_ge(s.ys, T * NS + n + 1 - RING)
                            pool.tensor_tensor(hc[:, n % RING, :], hs[:, n % RING, :], bcb[:, NS + n, :],
                                               ALU.mult).then_inc(s.hc, 1)
                            if not last and n == 11:
                                drive(T + 1, m + 1, 1 - par)
                            if last and px and n == 14:
                                next_block(k)
                    elif last and px:
                        next_block(k)

                def next_block(k):
                    pool.wait_ge(s.xc, (k + 2) * MT)
                    drive((k + 1) * MT, 0, 0)

                def x2_tile(i):
                    t = i - 1
                    if 0 <= t < T2:
                        pool.wait_ge(i1.up, t + 1)
                        pool.tensor_tensor(x2[:, t, :], x2[:, t, :], up[:, t % 2, :], ALU.add).then_inc(i1.x2, 1)

                pool.memset(dtT[RK:RK + 1, :], 1.0).then_inc(r.dt_ones, 1)
                pool.wait_ge(r.dt_ones, 1)
                pool.memset(xw_one[:], 0.0).then_inc(r.dt_ones, 1)
                pool.wait_ge(r.dt_ones, 2)
                start(x2_tile, turn)
                for k in range(NB):
                    turns(pool, k, turn)

            @block.vector
            def _(dve):
                def head(k, m, par):
                    U = (k + 1) * MT + m
                    if from_on(U, 2):
                        dve.wait_ge(s.conv, CONV * (U - 1))
                    if (k + 1) % SPB == 0:
                        dve.memset(pad[:, par, 0:CONV - 1], 0.0).then_inc(s.head, 1)
                    else:
                        dve.tensor_copy(pad[:, par, 0:CONV - 1], tile(conv_carry, m)).then_inc(s.head, 1)

                def tap(k, m, par, i):
                    U = (k + 1) * MT + m
                    if i == 0:
                        dve.wait_ge(s.padded, U + 1)
                        dve.wait_ge(s.tap, U + 1)
                        dve.wait_ge(s.head, U + 1)
                    else:
                        dve.wait_ge(s.conv, CONV * U + i)
                    dve.scalar_tensor_tensor(acc[:, par, :], pad[:, par, i:i + BLK], col(cw, m, i), acc[:, par, :],
                                             ALU.mult, ALU.add).then_inc(s.conv, 1)
                    if i == CONV - 2:
                        dve.tensor_copy(tile(conv_carry, m), pad[:, par, BLK:BLK + CONV - 1]).then_inc(s.conv, 1)

                def steps(q, par):
                    dve.wait_ge(s.lg, q + 1)
                    if from_on(q, 2):
                        dve.wait_ge(s.da, (q - 1) * NS)
                        dve.wait_ge(s.u, q - 1)
                    dve.scalar_tensor_tensor(dts[:, par, :], ps[:, PDT, :], 0.0, soft[:], ALU.max, ALU.add).then_inc(s.dts, 1)

                def gate(T, m, par):
                    dve.wait_ge(s.ys, (T + 1) * NS)
                    dve.wait_ge(s.zs, T + 1)
                    if from_on(T, 2):
                        dve.wait_ge(y_store[par], 8 * (T - par))
                    dve.tensor_tensor(yo[:, par, :], ps[:, PY + par, :], tile(sz, m), ALU.mult).then_inc(s.gate, 1)

                def rms(k, lo, hi, out, used, count, done):
                    dve.wait_ge(s.rsx, k + 2)
                    if k >= 0:
                        dve.wait_ge(used, count)
                    dve.scalar_tensor_tensor(out[lo:hi, :], ps[lo:hi, PXP, :], nw[lo:hi, 0:1], soft[lo:hi, :],
                                             ALU.mult, ALU.mult).then_inc(done, 1)

                def drive(k, m, par, n):
                    T = k * MT + m
                    if kind(k, m)[3] and n % ROWS_AT_ONCE == 0:
                        dve.wait_ge(bc_load[2 * (n // ROWS_AT_ONCE)], 16 * (k + 1))
                    if n >= RING or from_on(T, 1):
                        dve.wait_ge(s.h, T * NS + n + 2 - RING)
                    dve.tensor_tensor(dbx[:, n % RING:n % RING + 2, :], u[:, par, :].unsqueeze(1).broadcast_to([P, 2, BLK]),
                                      bcb[:, n:n + 2, :], ALU.mult).then_inc(s.dbx, 2)

                def turn(k, m, par):
                    T = k * MT + m
                    scans, px, pz, first, last = kind(k, m)
                    zero_start = k % SPB == 0
                    for n in range(NS):
                        if scans:
                            if n == 0:
                                dve.wait_ge(s.u, T + 1)
                                drive(k, m, par, 0)
                            if n % 2 and n + 1 < NS:
                                drive(k, m, par, n + 1)
                            dve.wait_ge(s.da, T * NS + n + 1)
                            dve.wait_ge(s.dbx, T * NS + n + 1)
                            if n >= RING or from_on(T, 1):
                                dve.wait_ge(s.hc, T * NS + n + 1 - RING)
                            kept = carried(k, m, n)
                            if kept is not None:
                                dve.wait_ge(s.carry, kept)
                            dve.tensor_tensor_scan(hs[:, n % RING, :], da[:, n % RING, :], dbx[:, n % RING, :],
                                                   0.0 if zero_start else col(state, m, n), ALU.mult, ALU.add).then_inc(s.h, 1)
                        if px and n == 0:
                            head(k, m, par)
                        if scans and n == 2 and from_on(T, 1):
                            gate(T - 1, MT - 1 if first else m - 1, 1 - par)
                        at = 6 if last else 7
                        if px and at <= n < at + CONV - 1:
                            tap(k, m, par, n - at)
                        if scans and not last and n == 10:
                            steps(T + 1, 1 - par)
                        if last and px and n == 11:
                            rms(k, RK, NX, bcT, s.bc_out, 16 * (k + 1), s.bc_sb)
                        if last and px and n == 12:
                            rms(k, 0, RK, dtT, s.dtm, (k + 1) * MT, s.dt_in)
                        if last and px and n == 14:
                            steps(T + 1, 0)

                def x2_tile(i):
                    if i < T2:
                        dve.scalar_tensor_tensor(dn[:, i, :], dn[:, i, :], keep.query_hit[:, i:i + 1],
                                                 keep.rows[:], ALU.mult, ALU.mult).then_inc(i1.masked, 1)
                    t = i - 1
                    if 0 <= t < T2:
                        dve.wait_ge(i1.rs1, t + 1)
                        dve.wait_ge(i1.ag1, t + 1)
                        if t >= 2:
                            dve.wait_ge(i1.x2, t - 1)
                        dve.tensor_scalar(up[:, t % 2, :], dn[:, t, :], mv1[:, t, 0:1], rs1[:, t:t + 1],
                                          ALU.subtract, ALU.mult).then_inc(i1.up, 1)
                    if i < T2:
                        dve.wait_ge(i1.masked, i + 1)
                        layernorm_stats(dve, dn[:, i, :], st1, mv1, i, i1.st1, i1.ag1, i + 1)
                    t = i - 3
                    if 0 <= t < T2:
                        dve.wait_ge(i1.x2, t + 1)
                        layernorm_stats(dve, x2[:, t, :], st2, mv2, t, i1.st2, i1.ag2, t + 1)
                    t = i - X2_LAG + 1
                    if 0 <= t < T2:
                        dve.wait_ge(i1.rs2, t + 1)
                        dve.wait_ge(i1.ag2, t + 1)
                        if t >= 2:
                            dve.wait_ge(i1.tr, t - 1)
                        dve.tensor_scalar(xn[:, t % 2, :], x2[:, t, :], mv2[:, t, 0:1], rs2[:, t:t + 1],
                                          ALU.subtract, ALU.mult).then_inc(i1.xn, 1)

                dve.wait_ge(r.a, 1)
                dve.tensor_scalar(na[:], na[:], -1.0, None, ALU.mult).then_inc(r.neg, 1)
                start(x2_tile, turn)
                for k in range(NB):
                    turns(dve, k, turn)
                gate(NB * MT - 1, MT - 1, 1)
        clear(nc, (*r, *i1, *s, *bc_load))


def keeps(k):
    return k >= 0 and k % SPB < SPB - 1


def weights(k, m, par):
    return 8 * ((k + 1) * MT + m - par) + 16


def weights_z(k, m, par):
    return 8 * ((k + 1) * MT + m - 1 - (1 - par)) + 16


def carried(k, m, n):
    first = isinstance(m, int) and m == 0
    if not keeps((k - 1) if first and n < RING else k):
        return None
    return k // SPB * (SPB - 1) * MT * NS + (k % SPB * MT + m) * NS + n + 1 - RING


NE = 8
RE = 16
SCALING = 2.0
NL = NE * RE


def out_stage(nc, ctx, ps, keep, x2_in, y_in, w_out, w_gate_low, w_base, base_b, w_up, expert_ids, out):
    s = semaphores(nc, ctx, "t", "w w2 y0 y1 x0 x1 o st1 ag1 ln1 rs1 up x3 st2 ag2 ln2 rs2 xn tr ev gl top idx pick wt sum "
                   "mix scl ltr lev base bs st3 ag3 ln3 rs3 up3 fin out0 out1 out2 out3")
    y_load, x_load, out_store = (s.y0, s.y1), (s.x0, s.x1), (s.out0, s.out1, s.out2, s.out3)
    T = B * ST
    with ExitStack() as mem:
        def sb(name, shape, dt=F32):
            return mem.enter_context(nc.sbuf_tensor(name, shape, dt))

        wo = sb("t_wo", [P, MT, D])
        wgl = sb("wgl", [P, KC, NE + NL])
        wb = sb("wb", [P, KC, D])
        wu = sb("wu", [NL, D])
        bb = sb("bb", [P, D])
        eid = sb("eid", [P, NE])
        y = sb("t_y", [P, 2, MT, BLK])
        x3 = sb("x3", [P, 2 * TB, D])
        up = sb("t_up", [P, 2, D])
        xn = sb("t_xn", [P, 2, D])
        xnT = sb("t_xnT", [P, 4, KC, P])
        st1, mv1, ln1, rs1 = sb("t_st1", [P, T, 6]), sb("t_mv1", [P, T, 2]), sb("t_ln1", [P, T]), sb("t_rs1", [P, T])
        st2, mv2, ln2, rs2 = sb("t_st2", [P, T, 6]), sb("t_mv2", [P, T, 2]), sb("t_ln2", [P, T]), sb("t_rs2", [P, T])
        st3, mv3, ln3, rs3 = sb("t_st3", [P, T, 6]), sb("t_mv3", [P, T, 2]), sb("t_ln3", [P, T]), sb("t_rs3", [P, T])
        logit = sb("logit", [P, T, NE])
        top = sb("t_top", [P, T, 8])
        idx = sb("t_idx", [P, T, 8], mybir.dt.uint32)
        idf = sb("t_idf", [P, T, 2])
        gap = sb("gap", [P, T])
        total = sb("total", [P, T])
        second = sb("second", [P, T])
        wt = sb("t_wt", [P, T, 2])
        mix = sb("t_mix", [P, T, 2, NE])
        low = sb("t_low", [P, 2, NL])
        lowT = sb("t_lowT", [NL, 2, P])
        res = sb("t_res", [P, 2, D])
        up3 = sb("t_up3", [P, 2, D])
        fin = sb("t_fin", [P, 4, D])

        with nc.Block() as block:
            @block.sync
            def _(sp):
                def load_y(g):
                    if g >= 2:
                        sp.wait_ge(s.o, TB * (g - 1))
                    sp.dma_start(y[:, g % 2, :, :], y_in[g]).then_inc(y_load[g % 2], 16)

                def load_x(g):
                    if g >= 2:
                        sp.wait_ge(s.fin, TB * (g - 1))
                    sp.dma_start(x3[:, g % 2 * TB:g % 2 * TB + TB, :],
                                 x2_in[g].rearrange("(t p) d -> p t d", p=P)).then_inc(x_load[g % 2], 16)

                sp.dma_start(wo[:], w_out.rearrange("(m p) n -> p m n", p=P)).then_inc(s.w, 16)
                load_y(0)
                load_x(0)
                for dst, src in ((wgl[:], w_gate_low.rearrange("(c p) n -> p c n", p=P)),
                                 (wb[:], w_base.rearrange("(c p) n -> p c n", p=P)),
                                 (wu[:], w_up),
                                 (bb[:], base_b.rearrange("(a n) -> a n", a=1).broadcast_to([P, D])),
                                 (eid[:], expert_ids)):
                    sp.dma_start(dst, src).then_inc(s.w2, 16)
                load_y(1)
                load_x(1)
                for t in range(T):
                    sp.wait_ge(s.fin, t + 1)
                    sp.dma_start(out[t // TB, t % TB * P:t % TB * P + P, :], fin[:, t % 4, :]).then_inc(out_store[t % 4], 16)
                    g = t // TB + 2
                    if t % TB == 1 and g < NB:
                        load_y(g)
                    if t % TB == TB - 1 and g < NB:
                        load_x(g)
                for q in out_store:
                    sp.wait_ge(q, 16 * T // 4)

            @block.tensor
            def _(pe):
                pe.wait_ge(s.w, 16)
                for i in range(T + 2):
                    if i < T:
                        g = i // TB
                        pe.wait_ge(y_load[g % 2], 16 * (g // 2 + 1))
                        if i >= 2:
                            pe.wait_ge(s.up, i - 1)
                        for m in range(MT):
                            mm = pe.matmul(ps[:, i % 2, :], y[:, g % 2, m, i % TB * P:i % TB * P + P], wo[:, m, :],
                                           start=(m == 0), stop=(m == MT - 1))
                        mm.then_inc(s.o, 1)
                    t = i - 1
                    if 0 <= t < T:
                        pe.wait_ge(s.xn, t + 1)
                        if t >= 1:
                            pe.wait_ge(s.ev, t)
                        for k in range(KC):
                            mm = pe.transpose(ps[:, 2, k * P:k * P + P], xn[:, t % 2, k * P:k * P + P], keep.ident[:])
                        mm.then_inc(s.tr, 1)
                    t = i - 2
                    if 0 <= t < T:
                        pe.wait_ge(s.scl, t + 1)
                        if t >= 1:
                            pe.wait_ge(s.lev, t)
                        pe.transpose(ps[:, 6, 0:P], low[:, t % 2, :], keep.ident[:]).then_inc(s.ltr, 1)
                        if t >= 2:
                            pe.wait_ge(s.bs, t - 1)
                        for k in range(KC):
                            pe.matmul(ps[:, 4 + t % 2, :], xnT[:, t % 4, k, :], wb[:, k, :], start=(k == 0), stop=False)
                        pe.wait_ge(s.lev, t + 1)
                        pe.matmul(ps[:, 4 + t % 2, :], lowT[:, t % 2, :], wu[:], start=False, stop=True).then_inc(s.base, 1)
                    t = i - 1
                    if 0 <= t < T:
                        pe.wait_ge(s.ev, t + 1)
                        if t == 0:
                            pe.wait_ge(s.w2, 16 * 5)
                        if t >= 1:
                            pe.wait_ge(s.scl, t)
                        for k in range(KC):
                            mm = pe.matmul(ps[:, 3, 0:NE + NL], xnT[:, t % 4, k, :], wgl[:, k, :],
                                           start=(k == 0), stop=(k == KC - 1))
                        mm.then_inc(s.gl, 1)

            @block.scalar
            def _(act):
                act.preload_act_table_set("natural_log_exp_and_others")
                for i in range(T + 4):
                    t = i - 2
                    if 0 <= t < T:
                        act.wait_ge(s.pick, t + 1)
                        act.activation(second[:, t:t + 1], gap[:, t:t + 1], ACT.Exp).then_inc(s.wt, 1)
                    t = i - 3
                    if 0 <= t < T:
                        layernorm_tail(act, mv3, ln3, rs3, t, s.ag3, s.ln3, s.rs3, t + 1)
                    if i < T:
                        layernorm_tail(act, mv1, ln1, rs1, i, s.ag1, s.ln1, s.rs1, i + 1)
                    t = i - 1
                    if 0 <= t < T:
                        act.wait_ge(s.tr, t + 1)
                        act.activation(xnT[:, t % 4, :, :].rearrange("p c n -> p (c n)"), ps[:, 2, :], ACT.Copy).then_inc(s.ev, 1)
                    t = i - 2
                    if 0 <= t < T:
                        act.wait_ge(s.ltr, t + 1)
                        if t >= 2:
                            act.wait_ge(s.base, t - 1)
                        act.activation(lowT[:, t % 2, :], ps[:, 6, 0:P], ACT.Copy).then_inc(s.lev, 1)
                    if i < T:
                        layernorm_tail(act, mv2, ln2, rs2, i, s.ag2, s.ln2, s.rs2, i + 1)

            @block.gpsimd
            def _(pool):
                for i in range(T + 3):
                    t = i - 3
                    if 0 <= t < T:
                        pool.wait_ge(s.up3, t + 1)
                        pool.wait_ge(s.x3, t + 1)
                        if t >= 4:
                            pool.wait_ge(out_store[t % 4], 16 * (t // 4))
                        pool.tensor_tensor(fin[:, t % 4, :], x3[:, t % (2 * TB), :], up3[:, t % 2, :], ALU.add).then_inc(s.fin, 1)
                    if i < T:
                        g = i // TB
                        pool.wait_ge(x_load[g % 2], 16 * (g // 2 + 1))
                        pool.wait_ge(s.up, i + 1)
                        pool.tensor_tensor(x3[:, i % (2 * TB), :], x3[:, i % (2 * TB), :], up[:, i % 2, :], ALU.add).then_inc(s.x3, 1)

            @block.vector
            def _(dve):
                def pick(t):
                    dve.wait_ge(s.gl, t + 1)
                    dve.tensor_copy(logit[:, t, :], ps[:, 3, 0:NE]).then_inc(s.top, 1)
                    dve.wait_ge(s.top, 3 * t + 1)
                    dve.max(top[:, t, :], logit[:, t, :]).then_inc(s.top, 1)
                    dve.wait_ge(s.top, 3 * t + 2)
                    dve.tensor_tensor(gap[:, t:t + 1], top[:, t, 1:2], top[:, t, 0:1], ALU.subtract).then_inc(s.pick, 1)
                    dve.max_index(idx[:, t, :], top[:, t, :], logit[:, t, :]).then_inc(s.top, 1)

                def result(t):
                    dve.wait_ge(s.base, t + 1)
                    dve.tensor_tensor(res[:, t % 2, :], ps[:, 4 + t % 2, :], bb[:], ALU.add).then_inc(s.bs, 1)

                def mixture(t):
                    dve.wait_ge(s.top, 3 * t + 3)
                    dve.tensor_copy(idf[:, t, :], idx[:, t, 0:2]).then_inc(s.idx, 1)
                    dve.wait_ge(s.wt, t + 1)
                    dve.tensor_scalar(total[:, t:t + 1], second[:, t:t + 1], 1.0, None, ALU.add).then_inc(s.sum, 1)
                    dve.wait_ge(s.sum, 5 * t + 1)
                    dve.reciprocal(wt[:, t, 0:1], total[:, t:t + 1]).then_inc(s.sum, 1)
                    dve.wait_ge(s.sum, 5 * t + 2)
                    dve.tensor_tensor(wt[:, t, 1:2], second[:, t:t + 1], wt[:, t, 0:1], ALU.mult).then_inc(s.sum, 1)
                    dve.wait_ge(s.idx, t + 1)
                    dve.wait_ge(s.sum, 5 * t + 3)
                    for k in range(2):
                        dve.tensor_scalar(mix[:, t, k, :], eid[:], idf[:, t, k:k + 1], wt[:, t, k:k + 1],
                                          ALU.is_equal, ALU.mult).then_inc(s.sum, 1)
                    dve.wait_ge(s.sum, 5 * t + 5)
                    dve.tensor_tensor(mix[:, t, 0, :], mix[:, t, 0, :], mix[:, t, 1, :], ALU.add).then_inc(s.mix, 1)
                    dve.wait_ge(s.mix, t + 1)
                    if t >= 2:
                        dve.wait_ge(s.ltr, t - 1)
                    dve.scalar_tensor_tensor(low[:, t % 2, :].rearrange("p (e r) -> p e r", r=RE),
                                             ps[:, 3, NE:NE + NL].rearrange("p (e r) -> p e r", r=RE), SCALING,
                                             mix[:, t, 0, :].unsqueeze(2).broadcast_to([P, NE, RE]),
                                             ALU.mult, ALU.mult).then_inc(s.scl, 1)

                dve.wait_ge(s.w2, 16 * 5)
                for i in range(T + 4):
                    t = i - 2
                    if 0 <= t < T:
                        pick(t)
                    t = i - 3
                    if 0 <= t < T:
                        result(t)
                    t = i - 2
                    if 0 <= t < T:
                        mixture(t)
                    t = i - 3
                    if 0 <= t < T:
                        dve.wait_ge(s.bs, t + 1)
                        layernorm_stats(dve, res[:, t % 2, :], st3, mv3, t, s.st3, s.ag3, t + 1)
                    if i < T:
                        dve.wait_ge(s.o, i + 1)
                        layernorm_stats(dve, ps[:, i % 2, :], st1, mv1, i, s.st1, s.ag1, i + 1)
                    t = i - 3
                    if 0 <= t < T:
                        dve.wait_ge(s.ag3, t + 1)
                        dve.wait_ge(s.rs3, t + 1)
                        if t >= 2:
                            dve.wait_ge(s.fin, t - 1)
                        dve.tensor_scalar(up3[:, t % 2, :], res[:, t % 2, :], mv3[:, t, 0:1], rs3[:, t:t + 1],
                                          ALU.subtract, ALU.mult).then_inc(s.up3, 1)
                    if i < T:
                        dve.wait_ge(s.ag1, i + 1)
                        dve.wait_ge(s.rs1, i + 1)
                        if i >= 2:
                            dve.wait_ge(s.x3, i - 1)
                        dve.tensor_scalar(up[:, i % 2, :], ps[:, i % 2, :], mv1[:, i, 0:1], rs1[:, i:i + 1],
                                          ALU.subtract, ALU.mult).then_inc(s.up, 1)
                        dve.wait_ge(s.x3, i + 1)
                        layernorm_stats(dve, x3[:, i % (2 * TB), :], st2, mv2, i, s.st2, s.ag2, i + 1)
                        dve.wait_ge(s.ag2, i + 1)
                        dve.wait_ge(s.rs2, i + 1)
                        if i >= 2:
                            dve.wait_ge(s.tr, i - 1)
                        dve.tensor_scalar(xn[:, i % 2, :], x3[:, i % (2 * TB), :], mv2[:, i, 0:1], rs2[:, i:i + 1],
                                          ALU.subtract, ALU.mult).then_inc(s.xn, 1)


_W = ["L0_attn_x", "w_qkv", "L0_attn_wo", "w_dense", "w_cent", "L0_ffn_bias", "L0_ffn_assignments", "w_in",
      "L1_attn_conv_w", "conv_b", "w_x", "norm_w", "mean", "w_dt", "L1_attn_A_log",
      "d_skip", "w_out", "w_gate_low", "w_base", "L1_ffn_base_b", "w_up",
      "rope", "ident", "masks", "cluster_ids", "expert_ids"]


def run(stage, nc, *args):
    with ExitStack() as ctx:
        stage(nc, ctx, *args)


def two_layers(nc, t, out):
    def scratch(name, shape):
        return nc.dram_tensor(name, shape, F32, kind="Internal").ap()

    att_o, att_l, x2 = scratch("att_o", (B * H, HD, S)), scratch("att_l", (B * H, S)), scratch("x2_d", (NB, BLK, D))
    y = scratch("y_d", (NB, P, MT, BLK))
    bc = scratch("bc_d", (2 * NS, BLK))
    with ExitStack() as ctx:
        ps = ctx.enter_context(nc.psum_tensor("ps", [P, 8, 512], F32))
        ident = ctx.enter_context(nc.sbuf_tensor("identity", [P, P], F32))
        run(attention_stage, nc, ps, ident, t["L0_attn_x"], t["w_qkv"], t["rope"], t["ident"], t["masks"], att_o, att_l)
        with ExitStack() as mem:
            def sb(name, shape):
                return mem.enter_context(nc.sbuf_tensor(name, shape, F32))

            keep = namedtuple("keep", "ident hits query_hit rows")(
                ident, sb("keep_hits", [P, NC]), sb("keep_query_hit", [P, B * ST]),
                sb("keep_rows", [P, D]))
            small, transfers = scan_weights(nc, mem, t)
            xnT = sb("scan_in", [P, KC, B * S])
            work = sb("work", [P, 2 * B * ST, D])
            run(dense_stage, nc, ps, keep, work[:, 0:B * ST, :], work[:, B * ST:2 * B * ST, :], t["L0_attn_x"],
                att_o, att_l, t["L0_attn_wo"], t["w_dense"], t["w_cent"], t["L0_ffn_bias"], t["L0_ffn_assignments"], t["cluster_ids"],
                transfers)
            run(scan_stage, nc, ps, keep, work, xnT, small, t["w_in"], bc, x2, y)
        run(out_stage, nc, ps, namedtuple("keep", "ident")(ident), x2, y, t["w_out"], t["w_gate_low"], t["w_base"], t["L1_ffn_base_b"], t["w_up"],
                  t["expert_ids"], out)


def rope_tables(np):
    inv = 1.0 / 10000.0 ** (np.arange(0, HD, 2)[:HD // 2].astype(np.float32) / HD)
    f = np.outer(np.arange(S), inv).astype(np.float32)
    d = np.arange(P) % HD
    sign = np.where(d % 2 == 0, np.float32(-1), np.float32(1))[:, None]
    return np.stack([np.cos(f).T[d // 2], np.sin(f).T[d // 2] * sign], 1).astype(np.float32)


def kernel(**inputs):
    import numpy as np
    import concourse.bacc as _bacc
    from concourse import mybir as _mybir
    from concourse.bass_utils import run_bass_kernel_spmd as _run

    t = {k: np.asarray(v) for k, v in inputs.items()}
    wqkv = np.stack([t["L0_attn_wq"], t["L0_attn_wk"], t["L0_attn_wv"]])
    t["w_qkv"] = wqkv.reshape(3, KC, P, KC, P).transpose(3, 2, 0, 1, 4)
    t["w_dense"] = t["L0_ffn_weight"].T
    t["w_cent"] = t["L0_ffn_centroids"].T
    t["w_in"] = t["L1_attn_in_proj_w"].reshape(KC, P, 2 * MT, P).transpose(2, 1, 0, 3)
    t["w_x"] = t["L1_attn_x_proj_w"].T
    t["norm_w"] = np.concatenate([t["L1_attn_dt_ln_w"], t["L1_attn_B_ln_w"], t["L1_attn_C_ln_w"]])[:, None]
    t["w_dt"] = np.concatenate([t["L1_attn_dt_proj_w"].T, t["L1_attn_dt_bias"][None]])
    for name, source in (("conv_b", "L1_attn_conv_b"), ("d_skip", "L1_attn_D_param")):
        t[name] = t[source].reshape(MT, P).T
    t["w_out"] = t["L1_attn_out_proj_w"].T
    t["w_gate_low"] = np.concatenate([t["L1_ffn_gate_w"].T, t["L1_ffn_lora_A"].reshape(NL, D).T], 1)
    t["w_base"] = t["L1_ffn_base_w"].T
    t["w_up"] = t["L1_ffn_lora_B"].transpose(0, 2, 1).reshape(NL, D)
    t["L0_attn_x"] = t["L0_attn_x"].reshape(NB, BLK, D)
    t["rope"] = rope_tables(np)
    group = np.array([0] * RK + [1] * NS + [2] * NS)
    t["mean"] = ((group[:, None] == group) / np.array([RK, NS, NS])[group]).astype(np.float32)
    t["ident"] = np.eye(P, dtype=np.float32)
    late = np.triu(np.full((P, P), -1e30, np.float32), 1)
    t["masks"] = np.stack([late, late.T], 1)
    t["cluster_ids"] = np.arange(NC, dtype=np.float32)[:, None]
    t["expert_ids"] = np.tile(np.arange(NE, dtype=np.float32), (P, 1))

    nc = _bacc.Bacc("TRN2", target_bir_lowering=False, num_devices=1)
    arrays, aps = {}, {}
    for name in _W:
        a = np.ascontiguousarray(t[name])
        arrays[f"in_{name}"] = a
        aps[name] = nc.dram_tensor(f"in_{name}", a.shape, _mybir.dt.from_np(a.dtype), kind="ExternalInput").ap()
    out = nc.dram_tensor("out_0", (NB, BLK, D), F32, kind="ExternalOutput").ap()
    two_layers(nc, aps, out)
    r = _run(nc, [arrays], core_ids=[0])
    return r.results[0]["out_0"].reshape(B, S, D)
```
